# Optimizing a Trainium2 kernel written in Bass

```python
import numpy as np
import jax
import jax.numpy as jnp

def _softmax(x, axis=-1):
    return jax.nn.softmax(x, axis=axis)

def _gelu(x):
    return jax.nn.gelu(x, approximate=True)

def _silu(x):
    return jax.nn.silu(x)

def _sigmoid(x):
    return jax.nn.sigmoid(x)

def _layernorm(x, axis=-1, eps=1e-05):
    m = jnp.mean(x, axis=axis, keepdims=True)
    v = jnp.var(x, axis=axis, keepdims=True)
    return (x - m) / jnp.sqrt(v + eps)

def _scatter_add(tgt, idx, src, axis=0):
    return tgt.at[idx].add(src)

def _segment_sum(src, seg, n):
    return jax.ops.segment_sum(src, seg, n)
kernel_name = 'mk_conv_preact_d2_conv_nchw128_r2_3a5c0e'

def setup_inputs(seed: int=0):
    np.random.seed(seed)
    _w = jnp.asarray

    def _rec_inputs():
        import jax
        import jax.numpy as jnp
        _gk = jax.random.key(seed)
        x = -0.0002422 + 1 * jax.random.normal(jax.random.fold_in(_gk, 1), (8, 64, 80, 80), jnp.float32)
        return x
    x = _rec_inputs()

    def _L0_conv_setup():
        import jax, jax.numpy as jnp
        import numpy as np
        K = 3
        STRIDE = 1
        IN_CH, OUT_CH = (64, 64)
        N, H, W = (8, 80, 80)

        def conv2d(x, w, b, stride=1, pad=1):
            out = jax.lax.conv_general_dilated(x, w, (stride, stride), [(pad, pad), (pad, pad)], dimension_numbers=('NCHW', 'OIHW', 'NCHW'))
            return out + b[None, :, None, None]

        def grid_sample_bilinear(x, gx, gy):
            n, c, h, w = x.shape
            ho, wo = (gx.shape[1], gx.shape[2])
            ix = (gx + 1.0) * 0.5 * (w - 1)
            iy = (gy + 1.0) * 0.5 * (h - 1)
            x0 = jnp.floor(ix)
            y0 = jnp.floor(iy)
            x1 = x0 + 1.0
            y1 = y0 + 1.0
            wx1 = ix - x0
            wx0 = 1.0 - wx1
            wy1 = iy - y0
            wy0 = 1.0 - wy1
            x_flat = x.reshape(n, c, h * w)

            def corner(yi, xi, wgt):
                valid = (xi >= 0) & (xi <= w - 1) & (yi >= 0) & (yi <= h - 1)
                xi_c = jnp.clip(xi, 0, w - 1).astype(jnp.int32)
                yi_c = jnp.clip(yi, 0, h - 1).astype(jnp.int32)
                idx = (yi_c * w + xi_c).reshape(n, 1, ho * wo)
                v = jnp.take_along_axis(x_flat, idx, axis=2).reshape(n, c, ho, wo)
                return v * (wgt * valid).reshape(n, 1, ho, wo)
            return corner(y0, x0, wy0 * wx0) + corner(y0, x1, wy0 * wx1) + corner(y1, x0, wy1 * wx0) + corner(y1, x1, wy1 * wx1)
        key = jax.random.key(seed)
        k1, k2, k3, k4, k5 = jax.random.split(key, 5)
        x = jax.random.normal(k1, (N, IN_CH, H, W), dtype=jnp.float32)
        s_off = 1.0 / np.sqrt(IN_CH * 3 * 3)
        s_cv = 1.0 / np.sqrt(IN_CH * K * K)
        w_off = jax.random.normal(k2, (2 * K * K, IN_CH, 3, 3), dtype=jnp.float32) * (0.1 * s_off)
        b_off = jax.random.normal(k3, (2 * K * K,), dtype=jnp.float32) * 0.01
        w_conv = jax.random.normal(k4, (OUT_CH, IN_CH, K, K), dtype=jnp.float32) * s_cv
        b_conv = jax.random.normal(k5, (OUT_CH,), dtype=jnp.float32) * s_cv
        return {'x': x, 'w_off': w_off, 'b_off': b_off, 'w_conv': w_conv, 'b_conv': b_conv}
    _L0_conv_all = _L0_conv_setup()
    _L0_conv_in = {k: v for k, v in _L0_conv_all.items() if k in ('w_off', 'b_off', 'w_conv', 'b_conv')}
    del _L0_conv_all

    def _L1_conv_setup():
        import jax, jax.numpy as jnp
        import numpy as np
        WS = 3
        MIN_C, MAX_C = (1, 16)
        NUM_GROUPS = 32
        GN_EPS = 1e-05

        def _downsample_half(x):
            B, C, H, W = x.shape
            return x.reshape(B, C, H // 2, 2, W // 2, 2).mean(axis=(3, 5))

        def _linear_interp_1d(x, out_size, axis):
            in_size = x.shape[axis]
            coords = jnp.maximum((jnp.arange(out_size) + 0.5) * (in_size / out_size) - 0.5, 0.0)
            i0 = jnp.clip(jnp.floor(coords).astype(jnp.int32), 0, in_size - 1)
            i1 = jnp.clip(i0 + 1, 0, in_size - 1)
            w = (coords - i0).astype(x.dtype)
            shape = [1] * x.ndim
            shape[axis] = out_size
            w = w.reshape(shape)
            x0 = jnp.take(x, i0, axis=axis)
            x1 = jnp.take(x, i1, axis=axis)
            return x0 * (1.0 - w) + x1 * w

        def _connection_counts(x):
            B, C, H, W = x.shape
            xd = _downsample_half(x)
            xu = _linear_interp_1d(_linear_interp_1d(xd, H, 2), W, 3)
            df = jnp.abs(x - xu).sum(axis=1, keepdims=True)
            df_flat = df.reshape(B, -1)
            df_min = df_flat.min(axis=1).reshape(B, 1, 1, 1)
            df_max = df_flat.max(axis=1).reshape(B, 1, 1, 1)
            dfn = (df - df_min) / (df_max - df_min + 1e-08)
            dfp = dfn ** 4
            thr = 0.9
            mask = (dfp > thr).astype(x.dtype)
            above = jnp.round((dfp - thr) / (1.0 - thr + 1e-08) * (MAX_C - MIN_C))
            above = jnp.maximum(above, 0.0) * mask
            return MIN_C + above
        key = jax.random.key(seed)
        ks = jax.random.split(key, 7)
        B, C, H, W = (2, 64, 80, 80)
        x = jax.random.normal(ks[0], (B, C, H, W), dtype=jnp.float32)
        gamma = jax.random.uniform(ks[1], (C,), dtype=jnp.float32, minval=0.5, maxval=1.5)
        beta = jax.random.normal(ks[2], (C,), dtype=jnp.float32) * 0.1
        w1 = jax.random.normal(ks[3], (2 * C, C), dtype=jnp.float32) * (1.0 / np.sqrt(C))
        b1 = jax.random.normal(ks[4], (2 * C,), dtype=jnp.float32) * 0.01
        w2 = jax.random.normal(ks[5], (C, 2 * C), dtype=jnp.float32) * (1.0 / np.sqrt(2 * C))
        b2 = jax.random.normal(ks[6], (C,), dtype=jnp.float32) * 0.01
        return {'x': x, 'gamma': gamma, 'beta': beta, 'w1': w1, 'b1': b1, 'w2': w2, 'b2': b2}
    _L1_conv_all = _L1_conv_setup()
    _L1_conv_in = {k: v for k, v in _L1_conv_all.items() if k in ('gamma', 'beta', 'w1', 'b1', 'w2', 'b2')}
    del _L1_conv_all
    return {'x': x, 'L0_conv_w_off': _L0_conv_in['w_off'], 'L0_conv_b_off': _L0_conv_in['b_off'], 'L0_conv_w_conv': _L0_conv_in['w_conv'], 'L0_conv_b_conv': _L0_conv_in['b_conv'], 'L1_conv_gamma': _L1_conv_in['gamma'], 'L1_conv_beta': _L1_conv_in['beta'], 'L1_conv_w1': _L1_conv_in['w1'], 'L1_conv_b1': _L1_conv_in['b1'], 'L1_conv_w2': _L1_conv_in['w2'], 'L1_conv_b2': _L1_conv_in['b2']}

def reference(x, L0_conv_w_off, L0_conv_b_off, L0_conv_w_conv, L0_conv_b_conv, L1_conv_gamma, L1_conv_beta, L1_conv_w1, L1_conv_b1, L1_conv_w2, L1_conv_b2):
    import jax
    import jax.numpy as jnp

    def _L0_conv_ref(x, w_off, b_off, w_conv, b_conv):
        import jax, jax.numpy as jnp
        import numpy as np
        K = 3
        STRIDE = 1
        IN_CH, OUT_CH = (64, 64)
        N, H, W = (8, 80, 80)

        def conv2d(x, w, b, stride=1, pad=1):
            out = jax.lax.conv_general_dilated(x, w, (stride, stride), [(pad, pad), (pad, pad)], dimension_numbers=('NCHW', 'OIHW', 'NCHW'))
            return out + b[None, :, None, None]

        def grid_sample_bilinear(x, gx, gy):
            n, c, h, w = x.shape
            ho, wo = (gx.shape[1], gx.shape[2])
            ix = (gx + 1.0) * 0.5 * (w - 1)
            iy = (gy + 1.0) * 0.5 * (h - 1)
            x0 = jnp.floor(ix)
            y0 = jnp.floor(iy)
            x1 = x0 + 1.0
            y1 = y0 + 1.0
            wx1 = ix - x0
            wx0 = 1.0 - wx1
            wy1 = iy - y0
            wy0 = 1.0 - wy1
            x_flat = x.reshape(n, c, h * w)

            def corner(yi, xi, wgt):
                valid = (xi >= 0) & (xi <= w - 1) & (yi >= 0) & (yi <= h - 1)
                xi_c = jnp.clip(xi, 0, w - 1).astype(jnp.int32)
                yi_c = jnp.clip(yi, 0, h - 1).astype(jnp.int32)
                idx = (yi_c * w + xi_c).reshape(n, 1, ho * wo)
                v = jnp.take_along_axis(x_flat, idx, axis=2).reshape(n, c, ho, wo)
                return v * (wgt * valid).reshape(n, 1, ho, wo)
            return corner(y0, x0, wy0 * wx0) + corner(y0, x1, wy0 * wx1) + corner(y1, x0, wy1 * wx0) + corner(y1, x1, wy1 * wx1)
        n, _, h, w = x.shape
        off = conv2d(x, w_off, b_off, stride=1, pad=1)
        off = off.reshape(n, 2, K * K, h, w).mean(axis=2)
        gy_base = jnp.linspace(-1.0, 1.0, h, dtype=x.dtype)[:, None]
        gx_base = jnp.linspace(-1.0, 1.0, w, dtype=x.dtype)[None, :]
        gx = jnp.broadcast_to(gy_base, (h, w))[None] + off[:, 0]
        gy = jnp.broadcast_to(gx_base, (h, w))[None] + off[:, 1]
        warped = grid_sample_bilinear(x, gx, gy)
        return conv2d(warped, w_conv, b_conv, stride=STRIDE, pad=K // 2)

    def _L1_conv_ref(x, gamma, beta, w1, b1, w2, b2):
        import jax, jax.numpy as jnp
        import numpy as np
        WS = 3
        MIN_C, MAX_C = (1, 16)
        NUM_GROUPS = 32
        GN_EPS = 1e-05

        def _downsample_half(x):
            B, C, H, W = x.shape
            return x.reshape(B, C, H // 2, 2, W // 2, 2).mean(axis=(3, 5))

        def _linear_interp_1d(x, out_size, axis):
            in_size = x.shape[axis]
            coords = jnp.maximum((jnp.arange(out_size) + 0.5) * (in_size / out_size) - 0.5, 0.0)
            i0 = jnp.clip(jnp.floor(coords).astype(jnp.int32), 0, in_size - 1)
            i1 = jnp.clip(i0 + 1, 0, in_size - 1)
            w = (coords - i0).astype(x.dtype)
            shape = [1] * x.ndim
            shape[axis] = out_size
            w = w.reshape(shape)
            x0 = jnp.take(x, i0, axis=axis)
            x1 = jnp.take(x, i1, axis=axis)
            return x0 * (1.0 - w) + x1 * w

        def _connection_counts(x):
            B, C, H, W = x.shape
            xd = _downsample_half(x)
            xu = _linear_interp_1d(_linear_interp_1d(xd, H, 2), W, 3)
            df = jnp.abs(x - xu).sum(axis=1, keepdims=True)
            df_flat = df.reshape(B, -1)
            df_min = df_flat.min(axis=1).reshape(B, 1, 1, 1)
            df_max = df_flat.max(axis=1).reshape(B, 1, 1, 1)
            dfn = (df - df_min) / (df_max - df_min + 1e-08)
            dfp = dfn ** 4
            thr = 0.9
            mask = (dfp > thr).astype(x.dtype)
            above = jnp.round((dfp - thr) / (1.0 - thr + 1e-08) * (MAX_C - MIN_C))
            above = jnp.maximum(above, 0.0) * mask
            return MIN_C + above
        B, C, H, W = x.shape
        K2 = WS * WS
        counts = _connection_counts(x)
        k = jnp.clip(counts.astype(jnp.int32), None, K2)
        p = WS // 2
        xp = jnp.pad(x, ((0, 0), (0, 0), (p, p), (p, p)))
        patches = jnp.stack([xp[:, :, dy:dy + H, dx:dx + W] for dy in range(WS) for dx in range(WS)], axis=2)
        xn = x / jnp.maximum(jnp.linalg.norm(x, axis=1, keepdims=True), 1e-12)
        pn = patches / jnp.maximum(jnp.linalg.norm(patches, axis=1, keepdims=True), 1e-12)
        sim = jnp.einsum('bchw,bcjhw->bjhw', xn, pn)
        order = jnp.argsort(-sim, axis=1)
        sim_sorted = jnp.take_along_axis(sim, order, axis=1)
        patches_sorted = jnp.take_along_axis(patches, order[:, None], axis=2)
        rank = jnp.arange(K2).reshape(1, K2, 1, 1)
        sel = (rank < k).astype(x.dtype)
        w = jnp.exp(sim_sorted) * sel
        w = w / (w.sum(axis=1, keepdims=True) + 1e-08)
        output = jnp.einsum('bcjhw,bjhw->bchw', patches_sorted, w)
        gx = x.reshape(B, NUM_GROUPS, C // NUM_GROUPS, H, W)
        mu = gx.mean(axis=(2, 3, 4), keepdims=True)
        var = gx.var(axis=(2, 3, 4), keepdims=True)
        nx = ((gx - mu) / jnp.sqrt(var + GN_EPS)).reshape(B, C, H, W)
        nx = nx * gamma[None, :, None, None] + beta[None, :, None, None]
        enhanced = output + nx
        h = jnp.einsum('bchw,oc->bohw', enhanced, w1) + b1[None, :, None, None]
        h = jax.nn.relu(h)
        ffn = jnp.einsum('bchw,oc->bohw', h, w2) + b2[None, :, None, None]
        return enhanced + ffn

    def _gn(v, G=32, eps=1e-05):
        B_, C_, H_, W_ = v.shape
        g = v.reshape(B_, G, C_ // G, H_, W_)
        m = jnp.mean(g, axis=(2, 3, 4), keepdims=True)
        s = jnp.var(g, axis=(2, 3, 4), keepdims=True)
        return ((g - m) / jnp.sqrt(s + eps)).reshape(v.shape)

    def _ln_c(v, eps=1e-06):
        m = jnp.mean(v, axis=1, keepdims=True)
        s = jnp.var(v, axis=1, keepdims=True)
        return (v - m) / jnp.sqrt(s + eps)

    def _ln_t(v, eps=1e-05):
        m = jnp.mean(v, axis=-1, keepdims=True)
        s = jnp.var(v, axis=-1, keepdims=True)
        return (v - m) / jnp.sqrt(s + eps)

    def _to_tokens(v):
        B_, C_, H_, W_ = v.shape
        return v.reshape(B_, C_, H_ * W_).transpose(0, 2, 1)

    def _from_tokens(t, like):
        B_, C_, H_, W_ = like.shape
        return t.transpose(0, 2, 1).reshape(B_, C_, H_, W_)
    x = x + _L0_conv_ref(_gn(x), L0_conv_w_off, L0_conv_b_off, L0_conv_w_conv, L0_conv_b_conv)
    x = x + _L1_conv_ref(_gn(x), L1_conv_gamma, L1_conv_beta, L1_conv_w1, L1_conv_b1, L1_conv_w2, L1_conv_b2)
    return x

_drawn_inputs = setup_inputs


def setup_inputs(seed=0):
    import zlib

    import numpy as np

    out = dict(_drawn_inputs(seed))
    spreads = {}
    factors = {'L1_conv_b1': 27.433, 'L1_conv_b2': 8.0}
    for name, (base, spread) in spreads.items():
        noise = np.random.default_rng([zlib.crc32(name.encode()), seed]).standard_normal(out[name].shape)
        drawn = base * np.exp(spread * noise) if base else spread * noise
        out[name] = jnp.asarray(drawn.astype(out[name].dtype))
    for name, factor in factors.items():
        out[name] = (out[name] * factor).astype(out[name].dtype)
    return out
```

```python
from contextlib import ExitStack

import numpy as np

import concourse.bass as bass
from concourse import mybir

F32 = mybir.dt.float32
BF16 = mybir.dt.bfloat16
I32 = mybir.dt.int32
ALU = mybir.AluOpType
ACT = mybir.ActivationFunctionType
AX = mybir.AxisListType

N_IMG, C, H, W = 8, 64, 80, 80
PAIRS = N_IMG // 2
PX = H * W
P = 2 * C
TAPS = 9
GEN = 9
HID = 2 * C
HP, WP = H + 2, W + 2
BAND = 8
BANDS = H // BAND
BPX = BAND * W
TILES = BPX // 128
NT = BANDS * TILES
ROWS = 4
CPX = ROWS * W
CHUNKS = H // ROWS
EPS = 1e-5
ENTRY = 2 * C
IMG_ENTRIES = W + PX
AHEAD = 64
MAGIC = 12582912.0
OFFC = 2 * TAPS
LN_SHIFT = 2.0 ** 30

_COLS = {}
_n = 0
for _name, _w in [("ident", P), ("group", P), ("selz", 4), ("grid", NT * 2), ("blk", 32), ("hash_hi", 32),
                  ("hash_lo", 32), ("tri", H), ("pair", H), ("iota", H), ("hval", 1), ("one", 1),
                  ("lower", GEN * GEN), ("rowmask", HP)]:
    _COLS[_name] = (_n, _n + _w)
    _n += _w
N_CONST = _n


def constants():
    c = np.zeros((P, N_CONST), np.float32)

    def put(name, a):
        c[:a.shape[0], _COLS[name][0]:_COLS[name][1]] = a

    put("ident", np.eye(P))
    k = np.arange(P)
    put("group", 0.5 * (k[:, None] // 2 == k[None, :] // 2))
    row = np.arange(2 * OFFC)
    sel = np.zeros((P, 4))
    sel[64 + row, row // TAPS] = 1.0 / TAPS
    put("selz", sel)
    line = np.linspace(-1.0, 1.0, H, dtype=np.float32)
    pixel = np.arange(NT)[None, :] * P + k[:, None]
    put("grid", np.stack([line[pixel // W], line[pixel % W]], -1).reshape(P, NT * 2))
    blk = np.zeros((P, 32))
    blk[k, k // C] = 1.0
    put("blk", blk)
    code = np.random.RandomState(7).randint(1, 1 << 16, C)
    for name, part in (("hash_hi", code // 256 * 256), ("hash_lo", code % 256)):
        m = np.zeros((P, 32))
        m[k, k // C] = np.tile(part, 2)
        put(name, m)
    h = np.arange(H)
    put("tri", (h[:, None] < h[None, :]) * 1.0)
    put("pair", (h[:, None] == h[None, :]) * 1.0 + (h[:, None] + 1 == h[None, :]))
    put("iota", np.tile(h, (P, 1)))
    put("hval", h[:, None])
    put("one", np.ones((P, 1)))
    j = np.arange(GEN)
    put("lower", np.tile((j[None, :] < j[:, None]).reshape(1, -1) * 1.0, (P, 1)))
    m = np.ones((P, HP))
    m[:, [0, -1]] = 0.0
    put("rowmask", m)
    return c


class Chain:

    def __init__(self, eng, sem):
        self.eng, self.sem, self.base, self.n = eng, sem, 0, 0

    def link(self, ins):
        ins.then_inc(self.sem, 1)
        self.n += 1
        self.eng.wait_ge(self.sem, self.base + self.n)

    def loop(self, i, per):
        self.saved = (self.base, self.n)
        self.base, self.n = self.base + self.n + i * per, 0
        self.per = per

    def end(self, iterations):
        assert self.n == self.per, (self.n, self.per)
        self.base, self.n = self.saved
        self.n += iterations * self.per


def program(nc, x_d, w_off_d, b_off_d, w_conv_d, b_conv_d, gamma_d, beta_d, w1_d, b1_d, w2_d, b2_d, const_d, tables, sums, out_d):
    with ExitStack() as ctx:
        def sb(name, shape, dt=F32):
            return ctx.enter_context(nc.sbuf_tensor(name, shape, dt))

        def sem(name):
            return ctx.enter_context(nc.semaphore(name))

        cst = sb("cst", [P, N_CONST])

        def const(name, rows=P):
            a, b = _COLS[name]
            return cst[0:rows, a:b]

        off_lhs = sb("off_lhs", [P, 2 * OFFC])
        b_off_raw = sb("b_off_raw", [P, 2 * TAPS])
        conv_lhs = sb("conv_lhs", [P, TAPS, P])
        w1_lhs = sb("w1_lhs", [P, 2, P])
        w2_lhs = sb("w2_lhs", [P, 2, P])
        vec = sb("vec", [P, 8])
        b_conv, gamma, beta, b1, b2 = (vec[:, k:k + 1] for k in range(5))
        grid_b = sb("grid_b", [P, NT, 2])
        hash_lhs = sb("hash_lhs", [P, 2, 32], BF16)
        blk_bf = sb("blk_bf", [P, 32], BF16)
        xb = [sb(f"xb{k}", [P, HP * W]) for k in range(2)]
        g_band = sb("g_band", [P, 2, BPX])
        zbuf = sb("zbuf", [P, HP * WP])
        tok = sb("tok", [P, 2, TILES, 2, C])
        gat = sb("gat", [P, 2, TILES, 2, 2 * ENTRY])
        idx_i = sb("idx_i", [P, NT, 2], I32)
        idx_s = sb("idx_s", [P, 2, TILES * 2], I32)
        wgt = sb("wgt", [P, NT * 2, 4])
        wtok = sb("wtok", [P, 2, TILES, 2, C])
        wpad = sb("wpad", [P, HP * WP])
        hsum = sb("hsum", [P, 2, BAND * (W // 2)])
        xd = sb("xd", [P, 42, 42])
        up = sb("up", [P, 2, BAND, 42])
        d_band = g_band
        m_band = tok[0:96].rearrange("p u t i c -> p u (t i c)")
        s_band = sb("s_band", [P, 2, BPX], BF16)
        q_band = sb("q_band", [P, 2, BPX], BF16)
        enh = sb("enh", [P, PX])
        at = 0
        w_off_raw = enh[:, at:at + 2 * TAPS * TAPS]
        at += 2 * TAPS * TAPS
        conv_raw = enh[:, at:at + C * TAPS]
        at += C * TAPS
        conv_blk = enh[:, at:at + P]
        at += P
        w1_raw = enh[:, at:at + 2 * C].rearrange("p (a c) -> p a c", a=2)
        at += 2 * C
        w2_raw = enh[0:C, at:at + HID]
        hid = gat[:, 0].rearrange("p t i n -> p (t i n)")[:, 0:4 * CPX].rearrange("p (u i n) -> p u i n", u=2, i=2)
        stats = sb("stats", [P, 16 * 6])
        sv = sb("sv", [P, 24])
        pos = sb("pos", [P, NT * 2, 2])
        cell = sb("cell", [P, NT * 2, 2])
        tent = sb("tent", [P, 2, NT * 2, 2])
        ent = sb("ent", [P, NT * 2])
        maps = sb("maps", [H, 4, 2, W])
        fl = sb("fl", [H, 2, 2, W])
        kmap = sb("kmap", [H, 2, W])
        kcol = sb("kcol", [H, 2, H])
        mm = sb("mm", [H, 12])
        diag = sb("diag", [4, 8])
        ones4 = sb("ones4", [4, H])
        hot = sb("hot", [H, H + 1])
        lst = sb("lst", [1, H + 2], I32)
        cum = sb("cum", [1, 2])
        blk_r = sb("blk_r", [P, 32])
        grow = sb("grow", [P, 3, WP])
        gsq = gat[:, 1].rearrange("p t i n -> p (t i n)")[:, GEN * (W + P):GEN * (W + P) + 3 * WP].rearrange("p (a w) -> p a w", a=3)
        prod = gat[:, 1].rearrange("p t i n -> p (t i n)")[:, 0:GEN * W].rearrange("p (j w) -> p j w", w=W)
        rn = sb("rn", [H, 6, GEN, 2])
        sim = sb("sim", [H, 2, GEN])
        cmp = sb("cmp", [H, 2, 2, GEN, GEN])
        sel = sb("sel", [H, 6, 2, GEN])
        dent = sb("dent", [H, 2, 2])
        wrep = gat[0:H, 1].rearrange("p t i n -> p (t i n)")[:, GEN * W:GEN * (W + P)].rearrange("p (j i c) -> p j i c", j=GEN, i=2)
        agg = sb("agg", [P, 2, W])

        def windows(dy):
            return bass.AP(grow[:].tensor, grow[:, dy, 0:1].offset, [list(grow[:].ap[0]), [1, 3], [1, W]])

        ps = ctx.enter_context(nc.psum_tensor("ps", [P, 8, 512], F32))
        flat = ps[:, :, :].rearrange("p b n -> p (b n)")

        c_in = sem("c_in"); w_in = sem("w_in")
        setup_dve = sem("setup_dve"); setup_pe = sem("setup_pe"); ready = sem("ready"); pool_zero = sem("pool_zero"); table_zero = sem("table_zero")
        x_in = [sem(f"x_in{k}") for k in range(2)]
        dve = sem("dve"); act_own = sem("act_own")
        grp_in = sem("grp_in"); grp_out = sem("grp_out"); ln_in = sem("ln_in"); ln_out = sem("ln_out")
        norm_ok = sem("norm_ok")
        g_ok = sem("g_ok"); z_ps = sem("z_ps"); z_sb = sem("z_sb"); t_ps = sem("t_ps"); tok_ok = sem("tok_ok")
        tok_out = [sem(f"tok_out{k}") for k in range(2)]
        z_shift = sem("z_shift"); off_ps = sem("off_ps"); idx_ok = sem("idx_ok"); staged = sem("staged")
        gat_in = [sem(f"gat_in{k}") for k in range(2)]
        wtok_ok = sem("wtok_ok"); w_ps = sem("w_ps"); w_sb = sem("w_sb")
        conv_ps = sem("conv_ps"); x1_ok = sem("x1_ok")
        d_ok = sem("d_ok"); feat_ok = sem("feat_ok"); m_ps = sem("m_ps"); m_sb = sem("m_sb"); enh_ok = sem("enh_ok")
        maps_in = sem("maps_in")
        sm_pe = sem("sm_pe"); sm_dve = sem("sm_dve"); lst_ok = sem("lst_ok")
        r_act = sem("r_act"); r_dve = sem("r_dve"); r_pe = sem("r_pe"); r_own = sem("r_own"); r_done = sem("r_done")
        ln_r = sem("ln_r")
        h_ps = sem("h_ps"); h_sb = sem("h_sb"); f_ps = sem("f_ps"); y_ok = sem("y_ok")
        y_out = sem("y_out"); r_done2 = sem("r_done2")
        m_out = [sem(f"m_out{k}") for k in range(2)]

        N_W = 12
        block = ctx.enter_context(nc.Block())

        def rows(buf, first, n=BAND, width=W, col=0, wide=W):
            return buf[:, bass.ds(first * wide, n * wide)].rearrange("p (r w) -> p r w", w=wide)[:, :, col:col + width]

        @block.sync
        def _(sp):
            sp.dma_start(cst[:, :], const_d).then_inc(c_in, 16)
            sp.dma_start(xb[0][:, W:W + PX], x_d[0]).then_inc(x_in[0], 16)
            for half in range(2):
                sp.dma_start(w_off_raw[half * C:(half + 1) * C, :].rearrange("c (o t) -> c o t", t=TAPS),
                             w_off_d.rearrange("o c a b -> c o (a b)")).then_inc(w_in, 16)
                sp.dma_start(conv_raw[half * C:(half + 1) * C, :],
                             w_conv_d.rearrange("o c a b -> o (c a b)")).then_inc(w_in, 16)
                sp.dma_start(w1_raw[:, half, :], w1_d).then_inc(w_in, 16)
                for k, v in enumerate((b_conv_d, gamma_d, beta_d, None, b2_d)):
                    if v is not None:
                        sp.dma_start(vec[half * C:(half + 1) * C, k:k + 1],
                                     v.rearrange("(c a) -> c a", a=1)).then_inc(w_in, 16)
            sp.dma_start(vec[:, 3:4], b1_d.rearrange("(c a) -> c a", a=1)).then_inc(w_in, 16)
            sp.dma_start(w2_raw[:, :], w2_d).then_inc(w_in, 16)
            sp.dma_start(b_off_raw[:, :], b_off_d.rearrange("(a n) -> a n", a=1).broadcast_to([P, 2 * TAPS])).then_inc(w_in, 16)
            sp.wait_ge(pool_zero, 7)
            for q in range(PAIRS):
                for im in range(2):
                    a = im * IMG_ENTRIES
                    sp.dma_start(tables[q][a:a + W, 0:C], zbuf[0:W, 0:C]).then_inc(table_zero, 16)
                    sp.dma_start(tables[q][a + PX:a + PX + W, C:2 * C], zbuf[0:W, 0:C]).then_inc(table_zero, 16)
            for q in range(PAIRS):
                if q + 1 < PAIRS:
                    if q >= 1:
                        sp.wait_ge(y_ok, AHEAD + CHUNKS * q)
                    sp.dma_start(xb[(q + 1) % 2][:, W:W + PX], x_d[q + 1]).then_inc(x_in[(q + 1) % 2], 16)
                with sp.Fori(0, BANDS // 2) as i:
                    for u in range(2):
                        sp.wait_ge(tok_ok, AHEAD + BANDS * q + i * 2 + u + 1)
                        for im in range(2):
                            for dy in range(2):
                                first = im * IMG_ENTRIES + W - dy * W
                                sp.dma_start(tables[q][bass.ds((i * 2 + u) * BPX + first, BPX), dy * C:(dy + 1) * C].rearrange(
                                    "(t p) c -> p t c", p=P), tok[:, u, :, im, :]).then_inc(tok_out[u], 16)
                sp.wait_ge(z_sb, AHEAD + CHUNKS * (q + 1))
                for t in range(TAPS):
                    dy, dx = t // 3, t % 3
                    src = zbuf[t:2 * OFFC:TAPS, :].rearrange("p (h w) -> p h w", w=WP)[:, dy:dy + H, dx:dx + W]
                    sp.dma_start(zbuf[64 + t:64 + 2 * OFFC:TAPS, 0:PX].rearrange("p (h w) -> p h w", w=W), src)\
                      .then_inc(z_shift, 16)
                with sp.Fori(0, BANDS // 2) as i:
                    for u in range(2):
                        sp.wait_ge(m_sb, AHEAD + CHUNKS * q + (i * 2 + u) * 2 + 2)
                        for k in range(3):
                            sp.dma_start(sums[k][:, bass.ds((i * 2 + u) * BPX, BPX)], m_band[32 * k:32 * k + 2, u, :])\
                              .then_inc(m_out[u], 16)
                for u in range(2):
                    sp.wait_ge(m_out[u], AHEAD + 16 * 3 * (BANDS // 2) * (q + 1))
                for k, (kind, shift) in enumerate(((0, 0), (1, 0), (2, 0), (1, 1))):
                    sp.dma_start(maps[0:H - shift, k], sums[kind][:, shift * W:PX].rearrange("i (h w) -> h i w", w=W))\
                      .then_inc(maps_in, 16)
                with sp.Fori(0, BANDS // 2) as i:
                    for u in range(2):
                        sp.wait_ge(y_ok, AHEAD + CHUNKS * q + (i * 2 + u) * 2 + 2)
                        sp.dma_start(out_d[q][:, bass.ds((i * 2 + u) * BPX, BPX)], enh[:, bass.ds((i * 2 + u) * BPX, BPX)])\
                          .then_inc(y_out, 16)
            sp.wait_ge(y_out, 16 * BANDS * PAIRS)

        @block.gpsimd
        def _(pool):
            for counter in (z_ps, t_ps, wtok_ok, z_sb, tok_ok, w_sb, w_ps, x1_ok, m_ps, m_sb, feat_ok, h_sb, f_ps, y_ok, r_done, conv_ps, *tok_out, *m_out):
                pool.sem_inc(counter, AHEAD)
            nc.gpsimd.memset(zbuf[:, :], 0.0).then_inc(pool_zero, 1)
            nc.gpsimd.memset(wpad[:, :], 0.0).then_inc(pool_zero, 1)
            nc.gpsimd.memset(grow[:, :, :], 0.0).then_inc(pool_zero, 1)
            for k in range(2):
                nc.gpsimd.memset(xb[k][:, 0:W], 0.0).then_inc(pool_zero, 1)
                nc.gpsimd.memset(xb[k][:, W + PX:], 0.0).then_inc(pool_zero, 1)
            for q in range(PAIRS):
                pool.wait_ge(idx_ok, q + 1)
                for k in range(2):
                    pool.wait_ge(tok_out[k], AHEAD + 16 * 4 * (BANDS // 2) * (q + 1))
                before = (BANDS // 2) * q
                with pool.Fori(before + 1, before + 1 + BANDS // 2) as copies:
                    i = copies - (before + 1)
                    for u in range(2):
                        band = BANDS * q + i * 2 + u
                        if u == 0:
                            if q:
                                pool.wait_ge(wtok_ok, AHEAD + band)
                            else:
                                pool.wait_ge(wtok_ok, AHEAD + i * 2)
                            nc.gpsimd.tensor_copy(idx_s[:, :, :], idx_i[:, bass.ds(i * 2 * TILES, 2 * TILES), :].rearrange(
                                "p (u t) m -> p u (t m)", u=2)).then_inc(staged, 1)
                            pool.wait_ge(table_zero, 16 * 4 * PAIRS)
                            pool.wait_ge(staged, copies)
                        for t in range(TILES):
                            for im in range(2):
                                pool.indirect_dma_start(gat[:, u, t, im, :], None, tables[q][:, :],
                                                        bass.IndirectOffsetOnAxis(ap=idx_s[:, u, 2 * t + im:2 * t + im + 1], axis=0))\
                                    .then_inc(gat_in[u], 16)

        @block.scalar
        def _(act):
            own = Chain(act, act_own)
            act.preload_act_table_set("natural_log_exp_and_others")

            def rsqrt_seed(n, src, mid, dst):
                act.wait_ge(ln_in, n)
                own.link(nc.scalar.activation(mid, src, ACT.Ln))
                nc.scalar.activation(dst, mid, ACT.Exp, scale=-0.5).then_inc(ln_out, 1)

            act.wait_ge(c_in, 16)
            for q in range(PAIRS):
                x = xb[q % 2]
                rsqrt_seed(3 * q + 1, sv[:, 4:5], sv[:, 5:6], sv[:, 6:7])
                act.wait_ge(norm_ok, 2 * q + 1)
                if q == 0:
                    act.wait_ge(pool_zero, 7)
                with act.Fori(0, BANDS // 2) as i:
                    for u in range(2):
                        band = BANDS * q + i * 2 + u
                        if q:
                            act.wait_ge(z_ps, AHEAD + 2 * (band - 1))
                            act.wait_ge(t_ps, AHEAD + band - 1)
                        elif u == 0:
                            act.wait_ge(z_ps, AHEAD + i * 4)
                            act.wait_ge(t_ps, AHEAD + i * 2)
                        act.wait_ge(c_in, 16)
                        nc.scalar.activation(g_band[:, u, :], x[:, bass.ds((i * 2 + u) * BPX + W, BPX)], ACT.Identity,
                                             bias=sv[:, 8:9], scale=sv[:, 7:8]).then_inc(g_ok, 1)
                        for k in range(2):
                            chunk = 2 * band + k
                            act.wait_ge(z_ps, AHEAD + chunk + 1)
                            act.wait_ge(c_in, 16)
                            nc.scalar.activation(rows(zbuf[0:2 * OFFC], (i * 2 + u) * BAND + k * ROWS + 1, ROWS, W, 1, WP),
                                                 ps[0:2 * OFFC, 4 + k, 0:CPX].rearrange("p (r w) -> p r w", w=W),
                                                 ACT.Copy).then_inc(z_sb, 1)
                with act.Fori(0, BANDS // 2) as i:
                    for u in range(2):
                        band = BANDS * q + i * 2 + u
                        act.wait_ge(w_ps, AHEAD + band + 1)
                        if q:
                            act.wait_ge(conv_ps, AHEAD + CHUNKS * q)
                        act.wait_ge(c_in, 16)
                        nc.scalar.activation(rows(wpad, (i * 2 + u) * BAND + 1, BAND, W, 1, WP),
                                             flat[:, 2 * u * 512:2 * u * 512 + BPX].rearrange("p (h w) -> p h w", w=W),
                                             ACT.Copy).then_inc(w_sb, 1)
                rsqrt_seed(3 * q + 2, sv[:, 4:5], sv[:, 5:6], sv[:, 6:7])
                rsqrt_seed(3 * q + 3, sv[:, 11:12], sv[:, 5:6], sv[:, 12:13])
                act.wait_ge(norm_ok, 2 * q + 2)
                if q:
                    act.wait_ge(y_out, 16 * BANDS * q)
                with act.Fori(0, BANDS // 2) as i:
                    for u in range(2):
                        band = BANDS * q + i * 2 + u
                        src = x[:, bass.ds((i * 2 + u) * BPX + W, BPX)]
                        if q:
                            act.wait_ge(m_ps, AHEAD + 2 * (band - 1))
                        elif u == 0:
                            act.wait_ge(m_ps, AHEAD + i * 4)
                        act.wait_ge(d_ok, band + 1)
                        act.wait_ge(c_in, 16)
                        nc.scalar.activation(d_band[:, u, :], d_band[:, u, :], ACT.Abs)
                        nc.scalar.activation(s_band[:, u, :], src, ACT.Sign, bias=sv[:, 8:9], scale=sv[:, 7:8])
                        nc.scalar.activation(q_band[:, u, :], src, ACT.Square, bias=sv[:, 8:9], scale=sv[:, 7:8]).then_inc(feat_ok, 1)
                        nc.scalar.activation(enh[:, bass.ds((i * 2 + u) * BPX, BPX)], src, ACT.Identity,
                                             bias=sv[:, 16:17], scale=sv[:, 15:16]).then_inc(enh_ok, 1)
                        if q:
                            act.wait_ge(m_out[u], AHEAD + 16 * 3 * ((BANDS // 2) * q + i))
                        else:
                            act.wait_ge(m_out[u], AHEAD + i * 16 * 3)
                        for k in range(2):
                            act.wait_ge(m_ps, AHEAD + 2 * band + k + 1)
                            act.wait_ge(c_in, 16)
                            nc.scalar.activation(m_band[:, u, k * CPX:(k + 1) * CPX], ps[0:96, 4 + k, 0:CPX],
                                                 ACT.Copy).then_inc(m_sb, 1)
                act.wait_ge(lst_ok, q + 1)
                count = act.value_load(lst[0:1, H:H + 1], min_val=1, max_val=H)
                before = act.value_load(lst[0:1, H + 1:H + 2], min_val=0, max_val=H * PAIRS)
                with act.Fori(0, count) as i:
                    h = act.value_load(lst[0:1, bass.ds(i, 1)], min_val=0, max_val=H - 1)
                    act.wait_ge(r_done, AHEAD + before + i)
                    act.wait_ge(lst_ok, q + 1)
                    nc.scalar.activation(grow[:, :, 1:1 + W], rows(x, h, 3), ACT.Identity,
                                         bias=sv[:, 8:9], scale=sv[:, 7:8]).then_inc(r_act, 1)
                    act.wait_ge(r_dve, (before + i) * 5 + 1)
                    nc.scalar.activation(gsq[:, :, :], grow[:, :, :], ACT.Square).then_inc(r_act, 1)
                    act.wait_ge(r_dve, (before + i) * 5 + 3)
                    nc.scalar.activation(rn[:, 1], rn[:, 0], ACT.Ln, scale=LN_SHIFT).then_inc(ln_r, 1)
                    act.wait_ge(ln_r, before + i + 1)
                    nc.scalar.activation(rn[:, 2], rn[:, 1], ACT.Exp, scale=-0.5).then_inc(r_act, 1)
                    act.wait_ge(r_dve, (before + i) * 5 + 4)
                    nc.scalar.activation(sel[:, 0], sim[:, :, :], ACT.Exp).then_inc(r_act, 1)
                with act.Fori(0, CHUNKS // 2) as i:
                    for u in range(2):
                        chunk = CHUNKS * q + i * 2 + u
                        act.wait_ge(h_ps, chunk + 1)
                        if q:
                            act.wait_ge(f_ps, AHEAD + chunk - 1)
                        elif u == 0:
                            act.wait_ge(f_ps, AHEAD + i * 2)
                        act.wait_ge(c_in, 16)
                        for im in range(2):
                            ins = nc.scalar.activation(hid[:, u, im, :], ps[:, 2 * u + im, 0:CPX], ACT.Relu, bias=b1)
                        ins.then_inc(h_sb, 1)

        @block.vector
        def _(v):
            own = Chain(v, dve)

            def link(ins):
                own.link(ins)

            for t in (off_lhs, conv_blk, w1_lhs, w2_lhs):
                nc.vector.memset(t[:], 0.0).then_inc(setup_dve, 1)
            nc.vector.memset(ones4[:], 1.0).then_inc(setup_dve, 1)
            nc.vector.memset(cum[:], 0.0).then_inc(setup_dve, 1)
            nc.vector.memset(maps[:], -1.0e9).then_inc(setup_dve, 1)
            v.wait_ge(setup_dve, 7)
            v.wait_ge(c_in, 16)
            v.wait_ge(w_in, 16 * 17)
            raw = w_off_raw[:, :].rearrange("p (o k t) -> p o t k", o=2, t=TAPS)
            for im in range(2):
                a = slice(im * C, (im + 1) * C)
                nc.vector.tensor_reduce(off_lhs[a, im * OFFC:(im + 1) * OFFC].rearrange("p (o t) -> p o t", o=2),
                                        raw[a], AX.X, ALU.add)
            link(nc.vector.tensor_reduce(sv[:, 20:22], b_off_raw[:, :].rearrange("p (o k) -> p o k", o=2), AX.X, ALU.add))
            for o in range(2):
                link(nc.vector.tensor_scalar(sv[:, 22 + o:23 + o], sv[:, 20 + o:21 + o], 1.0 / TAPS, None, ALU.mult))
                link(nc.vector.tensor_scalar(grid_b[:, :, o], const("grid").rearrange("p (t o) -> p t o", o=2)[:, :, o],
                                             sv[:, 22 + o:23 + o], None, ALU.add))
            link(nc.vector.tensor_copy(hash_lhs[:, 0, :], const("hash_hi")))
            link(nc.vector.tensor_copy(hash_lhs[:, 1, :], const("hash_lo")))
            link(nc.vector.tensor_copy(blk_bf[:, :], const("blk")))
            for t in range(TAPS):
                for im in range(2):
                    a = slice(im * C, (im + 1) * C)
                    ins = nc.vector.tensor_copy(conv_blk[a, im * C:(im + 1) * C],
                                                conv_raw[a, :].rearrange("p (c t) -> p c t", t=TAPS)[:, :, t])
                ins.then_inc(ready, 1)
                v.wait_ge(setup_pe, t + 1)
                link(nc.vector.tensor_copy(conv_lhs[:, t, :], ps[:, 0, 0:P]))
            v.wait_ge(setup_pe, TAPS + 2)
            for im in range(2):
                a = slice(im * C, (im + 1) * C)
                link(nc.vector.tensor_copy(w1_lhs[a, im, :], ps[a, 1, 0:P]))
                link(nc.vector.tensor_copy(w2_lhs[:, im, a], ps[:, 2, 0:C]))
            nc.vector.tensor_copy(sv[:, 23:24], sv[:, 22:23]).then_inc(ready, 1)

            def group_stats(n):
                x = xb[n // 2 % 2]
                with v.Fori(0, 4) as i:
                    for k in range(4):
                        ins = nc.vector.bn_stats(stats[:, bass.ds((i * 4 + k) * 6, 6)], x[:, bass.ds((i * 4 + k) * 400 + W, 400)])
                    own.loop(i, 1)
                    link(ins)
                    own.end(4)
                link(nc.vector.bn_aggr(sv[:, 0:2], stats[:, :]))
                nc.vector.tensor_copy(sv[:, 18:20], sv[:, 0:2]).then_inc(grp_in, 1)
                v.wait_ge(grp_out, n + 1)
                link(nc.vector.tensor_copy(sv[:, 2:4], ps[:, 7, 0:2]))
                link(nc.vector.tensor_tensor(sv[:, 9:10], sv[:, 0:1], sv[:, 2:3], ALU.subtract))
                link(nc.vector.tensor_tensor(sv[:, 9:10], sv[:, 9:10], sv[:, 9:10], ALU.mult))
                link(nc.vector.tensor_tensor(sv[:, 10:11], sv[:, 9:10], sv[:, 3:4], ALU.add))
                nc.vector.tensor_scalar(sv[:, 4:5], sv[:, 10:11], EPS, None, ALU.add).then_inc(ln_in, 1)

            def refine(n, val, seed, dst):
                v.wait_ge(ln_out, n)
                link(nc.vector.tensor_tensor(sv[:, 9:10], seed, seed, ALU.mult))
                link(nc.vector.tensor_tensor(sv[:, 9:10], sv[:, 9:10], val, ALU.mult))
                link(nc.vector.tensor_scalar(sv[:, 9:10], sv[:, 9:10], -0.5, 1.5, ALU.mult, ALU.add))
                link(nc.vector.tensor_tensor(dst, sv[:, 9:10], seed, ALU.mult))

            def minus_mean():
                return nc.vector.scalar_tensor_tensor(out=sv[:, 8:9], in0=sv[:, 2:3], scalar=-1.0, in1=sv[:, 7:8],
                                                      op0=ALU.mult, op1=ALU.mult)

            for q in range(PAIRS):
                x = xb[q % 2]
                v.wait_ge(x_in[q % 2], 16 * (q // 2 + 1))
                group_stats(2 * q)
                refine(3 * q + 1, sv[:, 4:5], sv[:, 6:7], sv[:, 7:8])
                minus_mean().then_inc(norm_ok, 1)
                with v.Fori(0, BANDS // 2) as i:
                    for u in range(2):
                        band = BANDS * q + i * 2 + u
                        v.wait_ge(t_ps, AHEAD + band + 1)
                        if q:
                            v.wait_ge(tok_out[u], AHEAD + 16 * 4 * ((BANDS // 2) * q + i))
                        else:
                            v.wait_ge(tok_out[u], AHEAD + i * 16 * 4)
                        nc.vector.tensor_copy(tok[:, u].rearrange("p t i c -> p (t i c)"),
                                              flat[:, 2 * u * 512:2 * u * 512 + BPX]).then_inc(tok_ok, 1)
                v.wait_ge(off_ps, q + 1)
                link(nc.vector.tensor_tensor(pos[:, :, :].rearrange("p (t i) o -> p t i o", i=2),
                                             ps[:, 6, 0:4 * NT].rearrange("p (t i o) -> p t i o", i=2, o=2),
                                             grid_b[:, :, :].unsqueeze(2).broadcast_to([P, NT, 2, 2]), ALU.add))
                link(nc.vector.tensor_scalar(pos[:], pos[:], 1.0, 0.5 * (W - 1), ALU.add, ALU.mult))
                link(nc.vector.tensor_scalar(cell[:], pos[:], -0.5, 0.0, ALU.add, ALU.max))
                link(nc.vector.tensor_scalar(cell[:], cell[:], float(W - 2), MAGIC, ALU.min, ALU.add))
                link(nc.vector.tensor_scalar(cell[:], cell[:], MAGIC, None, ALU.subtract))
                link(nc.vector.tensor_tensor(tent[:, 0], pos[:], cell[:], ALU.subtract))
                link(nc.vector.tensor_scalar(tent[:, 1], tent[:, 0], 1.0, None, ALU.subtract))
                tf = tent[:].rearrange("p a t o -> p (a t o)")
                link(nc.vector.scalar_tensor_tensor(out=tf, in0=tf, scalar=-1.0, in1=tf, op0=ALU.mult, op1=ALU.min))
                link(nc.vector.tensor_scalar(tent[:], tent[:], 1.0, 0.0, ALU.add, ALU.max))
                link(nc.vector.tensor_scalar(ent[:], cell[:, :, 1], float(W), None, ALU.mult))
                link(nc.vector.tensor_tensor(ent[:], ent[:], cell[:, :, 0], ALU.add))
                for im in range(2):
                    link(nc.vector.tensor_scalar(idx_i[:, :, im], ent[:].rearrange("p (t i) -> p t i", i=2)[:, :, im],
                                                 float(im * IMG_ENTRIES + W), None, ALU.add))
                for dx in range(2):
                    for dy in range(2):
                        ins = nc.vector.tensor_tensor(wgt[:, :, 2 * dx + dy], tent[:, dx, :, 0], tent[:, dy, :, 1], ALU.mult)
                        if dx + dy < 2:
                            link(ins)
                ins.then_inc(idx_ok, 1)
                v.wait_ge(idx_ok, q + 1)
                with v.Fori(0, BANDS // 2) as i:
                    own.loop(i, 4)
                    for u in range(2):
                        band = BANDS * q + i * 2 + u
                        v.wait_ge(gat_in[u], 16 * 2 * TILES * ((BANDS // 2) * q + i + 1))
                        g = gat[:, u].rearrange("p t i (k c) -> p (t i k) c", c=C)
                        wb = wgt[:, bass.ds((i * 2 + u) * 2 * TILES, 2 * TILES), :].rearrange("p t k -> p (t k)")\
                            .unsqueeze(2).broadcast_to([P, 8 * TILES, C])
                        link(nc.vector.tensor_tensor(g, g, wb, ALU.mult))
                        g2 = gat[:, u].rearrange("p t i (k c) -> p (t i) k c", k=2)
                        link(nc.vector.tensor_tensor(g2[:, :, 0, :], g2[:, :, 0, :], g2[:, :, 1, :], ALU.add))
                        if q:
                            v.wait_ge(w_ps, AHEAD + band - 1)
                        elif u == 0:
                            v.wait_ge(w_ps, AHEAD + i * 2)
                        nc.vector.tensor_tensor(wtok[:, u].rearrange("p t i c -> p (t i) c"), g2[:, :, 0, 0:C],
                                                g2[:, :, 0, C:2 * C], ALU.add).then_inc(wtok_ok, 1)
                    own.end(BANDS // 2)
                with v.Fori(0, CHUNKS // 2) as i:
                    for u in range(2):
                        v.wait_ge(conv_ps, AHEAD + CHUNKS * q + i * 2 + u + 1)
                        xs = x[:, bass.ds((i * 2 + u) * CPX + W, CPX)]
                        nc.vector.scalar_tensor_tensor(out=xs, in0=ps[:, 4 + u, 0:CPX], scalar=b_conv, in1=xs,
                                                       op0=ALU.add, op1=ALU.add).then_inc(x1_ok, 1)
                v.wait_ge(x1_ok, AHEAD + CHUNKS * (q + 1))
                group_stats(2 * q + 1)
                refine(3 * q + 2, sv[:, 4:5], sv[:, 6:7], sv[:, 7:8])
                link(minus_mean())
                link(nc.vector.tensor_tensor(sv[:, 11:12], sv[:, 7:8], sv[:, 7:8], ALU.mult))
                link(nc.vector.tensor_tensor(sv[:, 11:12], sv[:, 11:12], sv[:, 10:11], ALU.mult))
                link(nc.vector.tensor_scalar(sv[:, 11:12], sv[:, 11:12], EPS, None, ALU.add))
                nc.vector.tensor_copy(sv[:, 9:10], sv[:, 8:9]).then_inc(ln_in, 1)
                refine(3 * q + 3, sv[:, 11:12], sv[:, 12:13], sv[:, 13:14])
                link(nc.vector.tensor_tensor(sv[:, 14:15], sv[:, 13:14], gamma, ALU.mult))
                link(nc.vector.scalar_tensor_tensor(out=sv[:, 15:16], in0=sv[:, 14:15], scalar=1.0, in1=sv[:, 7:8],
                                                    op0=ALU.add, op1=ALU.mult))
                link(nc.vector.tensor_tensor(sv[:, 16:17], sv[:, 2:3], sv[:, 15:16], ALU.mult))
                link(nc.vector.tensor_tensor(sv[:, 16:17], beta, sv[:, 16:17], ALU.subtract))
                link(nc.vector.tensor_scalar(blk_r[:, :], const("blk"), sv[:, 7:8], None, ALU.mult))
                nc.vector.tensor_copy(sv[:, 9:10], sv[:, 8:9]).then_inc(norm_ok, 1)
                with v.Fori(0, BANDS // 2) as i:
                    own.loop(i, 4)
                    for u in range(2):
                        img = x[:, bass.ds((i * 2 + u) * BPX + W, BPX)].rearrange("p (n b) -> p n b", b=2)
                        link(nc.vector.tensor_tensor(hsum[:, u, :], img[:, :, 0], img[:, :, 1], ALU.add))
                        hs = hsum[:, u, :].rearrange("p (h a w) -> p h a w", a=2, w=W // 2)
                        link(nc.vector.tensor_tensor(xd[:, bass.ds((i * 2 + u) * (BAND // 2) + 1, BAND // 2), 1:41],
                                                     hs[:, :, 0, :], hs[:, :, 1, :], ALU.add))
                    own.end(BANDS // 2)
                link(nc.vector.tensor_copy(xd[:, 1:41, 0:42:41], xd[:, 1:41, 1:41:39]))
                link(nc.vector.tensor_copy(xd[:, 0:42:41, :], xd[:, 1:41:39, :]))
                with v.Fori(0, BANDS // 2) as i:
                    own.loop(i, 8)
                    for u in range(2):
                        band = BANDS * q + i * 2 + u
                        upr = up[:, u].rearrange("p (h a) w -> p h a w", a=2)
                        half = (i * 2 + u) * (BAND // 2)
                        for a in range(2):
                            link(nc.vector.scalar_tensor_tensor(
                                out=upr[:, :, a, :], in0=xd[:, bass.ds(half + 1, BAND // 2), :], scalar=3.0,
                                in1=xd[:, bass.ds(half + 2 * a, BAND // 2), :], op0=ALU.mult, op1=ALU.add))
                        if q:
                            v.wait_ge(m_ps, AHEAD + 2 * (band - 1))
                        elif u == 0:
                            v.wait_ge(m_ps, AHEAD + i * 4)
                        db = d_band[:, u, :].rearrange("p (h w a) -> p h w a", w=W // 2, a=2)
                        for a in range(2):
                            link(nc.vector.scalar_tensor_tensor(out=db[:, :, :, a], in0=up[:, u, :, 1:41], scalar=3.0,
                                                                in1=up[:, u, :, 2 * a:2 * a + 40], op0=ALU.mult, op1=ALU.add))
                        nc.vector.scalar_tensor_tensor(out=d_band[:, u, :], in0=d_band[:, u, :], scalar=-1.0 / 64,
                                                       in1=x[:, bass.ds((i * 2 + u) * BPX + W, BPX)], op0=ALU.mult,
                                                       op1=ALU.add).then_inc(d_ok, 1)
                    own.end(BANDS // 2)
                v.wait_ge(maps_in, 16 * 4 * (q + 1))
                df = maps[:, 0]
                link(nc.vector.tensor_reduce(mm[:, 0:2], df, AX.X, ALU.max))
                link(nc.vector.tensor_reduce(mm[:, 4:6], df, AX.X, ALU.min))
                nc.vector.tensor_scalar(mm[:, 2:4], mm[:, 4:6], -1.0, None, ALU.mult).then_inc(sm_dve, 1)
                v.wait_ge(sm_pe, 5 * q + 1)
                link(nc.vector.tensor_reduce(diag[:, 4:5], ps[0:4, 7, 0:H], AX.X, ALU.max))
                nc.vector.tensor_scalar(diag[:, 0:4], const("ident", 4)[:, 0:4], diag[:, 4:5], None, ALU.mult).then_inc(sm_dve, 1)
                v.wait_ge(sm_pe, 5 * q + 2)
                link(nc.vector.tensor_copy(mm[:, 6:10], ps[0:H, 7, 0:4]))
                link(nc.vector.tensor_tensor(mm[:, 10:12], mm[:, 6:8], mm[:, 8:10], ALU.add))
                link(nc.vector.tensor_scalar(mm[:, 10:12], mm[:, 10:12], 1e-8, None, ALU.add))
                link(nc.vector.reciprocal(mm[:, 10:12], mm[:, 10:12]))
                for im in range(2):
                    link(nc.vector.tensor_scalar(fl[:, 0, im], df[:, im], mm[:, 8 + im:9 + im], mm[:, 10 + im:11 + im],
                                                 ALU.add, ALU.mult))
                link(nc.vector.tensor_tensor(fl[:, 0], fl[:, 0], fl[:, 0], ALU.mult))
                link(nc.vector.tensor_tensor(fl[:, 0], fl[:, 0], fl[:, 0], ALU.mult))
                link(nc.vector.tensor_scalar(kmap[:], fl[:, 0], -0.9, 15.0 / (1.0 - 0.9 + 1e-8), ALU.add, ALU.mult))
                link(nc.vector.tensor_scalar(kmap[:], kmap[:], MAGIC, MAGIC, ALU.add, ALU.subtract))
                link(nc.vector.tensor_scalar(kmap[:], kmap[:], 0.0, None, ALU.max))
                link(nc.vector.tensor_scalar(fl[:, 0], fl[:, 0], 0.9, None, ALU.is_gt))
                link(nc.vector.tensor_tensor(kmap[:], kmap[:], fl[:, 0], ALU.mult))
                link(nc.vector.tensor_scalar(kmap[:], kmap[:], 1.0, float(GEN), ALU.add, ALU.min))
                link(nc.vector.tensor_scalar(fl[:, 0], kmap[:], 1.0, None, ALU.is_gt))
                link(nc.vector.tensor_scalar(fl[:, 1], maps[:, 2], 1e-20, None, ALU.is_lt))
                link(nc.vector.tensor_tensor(fl[:, 0], fl[:, 0], fl[:, 1], ALU.max))
                code, below = maps[:, 1], maps[:, 3]
                link(nc.vector.tensor_tensor(fl[:, 1, :, 0:W - 1], code[:, :, 0:W - 1], code[:, :, 1:W], ALU.is_equal))
                link(nc.vector.tensor_tensor(fl[:, 0, :, 0:W - 1], fl[:, 0, :, 0:W - 1], fl[:, 1, :, 0:W - 1], ALU.max))
                link(nc.vector.tensor_reduce(mm[:, 0:1], fl[:, 0].rearrange("p i w -> p (i w)"), AX.X, ALU.max))
                link(nc.vector.tensor_tensor(fl[:, 0], code, below, ALU.is_equal))
                for a, b in ((0, 1), (1, 0)):
                    link(nc.vector.tensor_tensor(fl[:, 1, :, 0:W - 1], code[:, :, a:W - 1 + a], below[:, :, b:W - 1 + b], ALU.is_equal))
                    link(nc.vector.tensor_tensor(fl[:, 0, :, 0:W - 1], fl[:, 0, :, 0:W - 1], fl[:, 1, :, 0:W - 1], ALU.max))
                nc.vector.tensor_reduce(mm[:, 1:2], fl[:, 0].rearrange("p i w -> p (i w)"), AX.X, ALU.max).then_inc(sm_dve, 1)
                v.wait_ge(sm_pe, 5 * q + 3)
                link(nc.vector.tensor_copy(kcol[:].rearrange("p i h -> p (i h)"), ps[0:H, 7, 0:2 * H]))
                nc.vector.tensor_scalar(hot[:, H:H + 1], ps[0:H, 7, 2 * H:2 * H + 1], 1.0, None, ALU.min).then_inc(sm_dve, 1)
                v.wait_ge(sm_dve, 5 * q + 4)
                v.wait_ge(sm_pe, 5 * q + 4)
                link(nc.vector.tensor_copy(mm[:, 2:3], ps[0:H, 7, 0:1]))
                nc.vector.tensor_scalar(hot[:, 0:H], const("iota", H), mm[:, 2:3], hot[:, H:H + 1], ALU.is_equal, ALU.mult)\
                    .then_inc(sm_dve, 1)
                v.wait_ge(sm_pe, 5 * q + 5)
                link(nc.vector.tensor_copy(lst[:, 0:H], ps[0:1, 7, 0:H]))
                link(nc.vector.tensor_scalar(lst[:, H:H + 1], ps[0:1, 7, H:H + 1], 1.0, None, ALU.max))
                link(nc.vector.tensor_copy(lst[:, H + 1:H + 2], cum[:, 0:1]))
                link(nc.vector.tensor_copy(cum[:, 1:2], lst[:, H:H + 1]))
                nc.vector.tensor_tensor(cum[:, 0:1], cum[:, 0:1], cum[:, 1:2], ALU.add).then_inc(lst_ok, 1)
                v.wait_ge(lst_ok, q + 1)
                count = v.value_load(lst[0:1, H:H + 1], min_val=1, max_val=H)
                before = v.value_load(lst[0:1, H + 1:H + 2], min_val=0, max_val=H * PAIRS)
                v.wait_ge(enh_ok, BANDS * (q + 1))
                with v.Fori(0, count) as i:
                    h = v.value_load(lst[0:1, bass.ds(i, 1)], min_val=0, max_val=H - 1)
                    row = before + i
                    LINKS = 25
                    k_own = [0]

                    def rlink(ins):
                        k_own[0] += 1
                        ins.then_inc(r_own, 1)
                        v.wait_ge(r_own, row * LINKS + k_own[0])

                    v.wait_ge(r_act, row * 4 + 1)
                    v.wait_ge(lst_ok, q + 1)
                    nc.vector.tensor_tensor(grow[:, :, 1:1 + W], grow[:, :, 1:1 + W],
                                            const("rowmask")[:, bass.ds(h, 3)].unsqueeze(2).broadcast_to([P, 3, W]),
                                            ALU.mult).then_inc(r_dve, 1)
                    v.wait_ge(r_dve, row * 5 + 1)
                    center = grow[:, 1, 1:1 + W]
                    for dy in range(3):
                        win = windows(dy)
                        ins = nc.vector.tensor_tensor(prod[:, 3 * dy:3 * dy + 3, :], win,
                                                      center.unsqueeze(1).broadcast_to([P, 3, W]), ALU.mult)
                    ins.then_inc(r_dve, 1)
                    v.wait_ge(r_pe, row * 2 + 1)
                    dots = ps[0:H, 6, 0:2 * GEN]
                    rlink(nc.vector.tensor_copy(rn[:, 5].rearrange("p j i -> p (j i)"), dots))
                    nc.vector.tensor_scalar(rn[:, 0].rearrange("p j i -> p (j i)"), ps[0:H, 6, 2 * GEN:4 * GEN], 1e-24, None,
                                            ALU.max).then_inc(r_dve, 1)
                    v.wait_ge(r_act, row * 4 + 3)
                    rlink(nc.vector.tensor_scalar(rn[:, 2], rn[:, 2], LN_SHIFT ** 0.5, None, ALU.mult))
                    for _ in range(2):
                        rlink(nc.vector.tensor_tensor(rn[:, 3], rn[:, 2], rn[:, 2], ALU.mult))
                        rlink(nc.vector.tensor_tensor(rn[:, 3], rn[:, 3], rn[:, 0], ALU.mult))
                        rlink(nc.vector.tensor_scalar(rn[:, 3], rn[:, 3], -0.5, 1.5, ALU.mult, ALU.add))
                        rlink(nc.vector.tensor_tensor(rn[:, 2], rn[:, 2], rn[:, 3], ALU.mult))
                    rlink(nc.vector.tensor_tensor(rn[:, 4], rn[:, 5], rn[:, 2], ALU.mult))
                    nc.vector.tensor_tensor(sim[:].rearrange("p i j -> p j i"), rn[:, 4],
                                            rn[:, 2, GEN // 2, :].unsqueeze(1).broadcast_to([H, GEN, 2]), ALU.mult).then_inc(r_dve, 1)
                    v.wait_ge(r_dve, row * 5 + 4)
                    s_i = sim[:].unsqueeze(2).broadcast_to([H, 2, GEN, GEN])
                    s_j = sim[:].unsqueeze(3).broadcast_to([H, 2, GEN, GEN])
                    rlink(nc.vector.tensor_tensor(cmp[:, 0], s_i, s_j, ALU.is_gt))
                    rlink(nc.vector.tensor_tensor(cmp[:, 1], s_i, s_j, ALU.is_equal))
                    low = const("lower", H)
                    for im in range(2):
                        rlink(nc.vector.tensor_tensor(cmp[:, 1, im].rearrange("p a b -> p (a b)"),
                                                      cmp[:, 1, im].rearrange("p a b -> p (a b)"), low, ALU.mult))
                    rlink(nc.vector.tensor_tensor(cmp[:, 0], cmp[:, 0], cmp[:, 1], ALU.add))
                    rlink(nc.vector.tensor_reduce(sel[:, 1], cmp[:, 0], AX.X, ALU.add))
                    rlink(nc.vector.tensor_tensor(sel[:, 2], sel[:, 1],
                                                  kcol[:, :, bass.ds(h, 1)].broadcast_to([H, 2, GEN]), ALU.is_lt))
                    v.wait_ge(r_act, row * 4 + 4)
                    rlink(nc.vector.tensor_tensor(sel[:, 3], sel[:, 2], sel[:, 0], ALU.mult))
                    rlink(nc.vector.tensor_reduce(dent[:, 0], sel[:, 3], AX.X, ALU.add))
                    rlink(nc.vector.tensor_scalar(dent[:, 1], dent[:, 0], 1e-8, None, ALU.add))
                    rlink(nc.vector.reciprocal(dent[:, 0], dent[:, 1]))
                    rlink(nc.vector.tensor_tensor(sel[:, 4], sel[:, 3], dent[:, 0].unsqueeze(2).broadcast_to([H, 2, GEN]), ALU.mult))
                    nc.vector.tensor_copy(wrep[:].rearrange("p j i c -> p i j c"),
                                          sel[:, 4].unsqueeze(3).broadcast_to([H, 2, GEN, C])).then_inc(r_dve, 1)
                    v.wait_ge(r_pe, row * 2 + 2)
                    for dy in range(3):
                        win = windows(dy)
                        ins = nc.vector.tensor_tensor(prod[:, 3 * dy:3 * dy + 3, :],
                                                      ps[:, dy, 0:3 * W].rearrange("p (j w) -> p j w", w=W), win, ALU.mult)
                        if dy == 2:
                            rlink(ins)
                    rlink(nc.vector.tensor_reduce(agg[:, 0], prod[:].rearrange("p j w -> p w j"), AX.X, ALU.add))
                    assert k_own[0] == LINKS, k_own
                    v.wait_ge(lst_ok, q + 1)
                    nc.vector.tensor_scalar(agg[:, 1], center, sv[:, 14:15], beta, ALU.mult, ALU.add).then_inc(r_done2, 1)
                    v.wait_ge(r_done2, row + 1)
                    v.wait_ge(lst_ok, q + 1)
                    nc.vector.tensor_tensor(enh[:, bass.ds(h * W, W)], agg[:, 0], agg[:, 1], ALU.add).then_inc(r_done, 1)
                with v.Fori(0, BANDS // 2) as i:
                    own.loop(i, 4)
                    for u in range(2):
                        for k in range(2):
                            chunk = CHUNKS * q + (i * 2 + u) * 2 + k
                            at = (i * 2 + u) * BPX + k * CPX
                            v.wait_ge(f_ps, AHEAD + chunk + 1)
                            y = enh[:, bass.ds(at, CPX)]
                            link(nc.vector.scalar_tensor_tensor(out=y, in0=ps[:, 4 + k, 0:CPX], scalar=b2, in1=y,
                                                                op0=ALU.add, op1=ALU.add))
                            nc.vector.tensor_tensor(y, y, x[:, bass.ds(at + W, CPX)], ALU.add).then_inc(y_ok, 1)
                    own.end(BANDS // 2)

        @block.tensor
        def _(pe):
            def group_mean(n):
                pe.wait_ge(grp_in, n + 1)
                nc.tensor.matmul(ps[:, 7, 0:2], const("group"), sv[:, 18:20], start=True, stop=True).then_inc(grp_out, 1)

            pe.wait_ge(c_in, 16)
            ident = const("ident")
            for t in range(TAPS):
                pe.wait_ge(ready, t + 1)
                nc.tensor.transpose(ps[:, 0, 0:P], conv_blk[:, :], ident).then_inc(setup_pe, 1)
            pe.wait_ge(w_in, 16 * 17)
            nc.tensor.transpose(ps[:, 1, 0:P], w1_raw[:, :, :].rearrange("p a c -> p (a c)"), ident).then_inc(setup_pe, 1)
            nc.tensor.transpose(ps[:, 2, 0:C], w2_raw[:, :], const("ident", C)[:, 0:C]).then_inc(setup_pe, 1)
            pe.wait_ge(ready, TAPS + 1)
            for q in range(PAIRS):
                group_mean(2 * q)
                if q:
                    pe.wait_ge(y_ok, AHEAD + CHUNKS * q)
                with pe.Fori(0, BANDS // 2) as i:
                    for u in range(2):
                        band = BANDS * q + i * 2 + u
                        pe.wait_ge(g_ok, band + 1)
                        for k in range(2):
                            if q:
                                pe.wait_ge(z_sb, AHEAD + 2 * band + k - 1)
                            elif u:
                                pe.wait_ge(z_sb, AHEAD + i * 4 + 2 + k - 1)
                            elif k == 0:
                                pe.wait_ge(z_sb, AHEAD + i * 4)
                            nc.tensor.matmul(ps[0:2 * OFFC, 4 + k, 0:CPX], off_lhs[:, :], g_band[:, u, k * CPX:(k + 1) * CPX],
                                             start=True, stop=True).then_inc(z_ps, 1)
                        if q:
                            pe.wait_ge(tok_ok, AHEAD + band - 1)
                        elif u == 0:
                            pe.wait_ge(tok_ok, AHEAD + i * 2)
                        for t in range(TILES):
                            ins = nc.tensor.transpose(ps[:, 2 * u + t // 4, (t % 4) * P:(t % 4 + 1) * P],
                                                      g_band[:, u, t * P:(t + 1) * P], ident)
                        ins.then_inc(t_ps, 1)
                pe.wait_ge(z_shift, 16 * TAPS * (q + 1))
                for n in range(NT):
                    ins = nc.tensor.matmul(ps[:, 6, 4 * n:4 * n + 4], zbuf[64:64 + 2 * OFFC, n * P:(n + 1) * P],
                                           cst[64:64 + 2 * OFFC, _COLS["selz"][0]:_COLS["selz"][1]], start=True, stop=True)
                ins.then_inc(off_ps, 1)
                with pe.Fori(0, BANDS // 2) as i:
                    for u in range(2):
                        band = BANDS * q + i * 2 + u
                        pe.wait_ge(wtok_ok, AHEAD + band + 1)
                        if u:
                            pe.wait_ge(w_sb, AHEAD + band - 1) if q else (pe.wait_ge(w_sb, AHEAD + i * 2))
                        elif q:
                            pe.wait_ge(w_sb, AHEAD + band - 1)
                        else:
                            pe.wait_ge(w_sb, AHEAD + i * 2)
                        for t in range(TILES):
                            ins = nc.tensor.transpose(ps[:, 2 * u + t // 4, (t % 4) * P:(t % 4 + 1) * P],
                                                      wtok[:, u, t].rearrange("p i c -> p (i c)"), ident)
                        ins.then_inc(w_ps, 1)
                pe.wait_ge(w_sb, AHEAD + BANDS * (q + 1))
                with pe.Fori(0, CHUNKS // 2) as i:
                    for u in range(2):
                        if q:
                            pe.wait_ge(x1_ok, AHEAD + CHUNKS * q + i * 2 + u - 1)
                        elif u == 0:
                            pe.wait_ge(x1_ok, AHEAD + i * 2)
                        for t in range(TAPS):
                            ins = nc.tensor.matmul(ps[:, 4 + u, 0:CPX], conv_lhs[:, t, :],
                                                   rows(wpad, (i * 2 + u) * ROWS + t // 3, ROWS, W, t % 3, WP),
                                                   start=(t == 0), stop=(t == TAPS - 1))
                        ins.then_inc(conv_ps, 1)
                group_mean(2 * q + 1)
                pe.wait_ge(norm_ok, 2 * q + 2)
                with pe.Fori(0, BANDS // 2) as i:
                    for u in range(2):
                        band = BANDS * q + i * 2 + u
                        pe.wait_ge(feat_ok, AHEAD + band + 1)
                        for k in range(2):
                            part = slice(k * CPX, (k + 1) * CPX)
                            if q:
                                pe.wait_ge(m_sb, AHEAD + 2 * band + k - 1)
                            elif u:
                                pe.wait_ge(m_sb, AHEAD + i * 4 + 2 + k - 1)
                            elif k == 0:
                                pe.wait_ge(m_sb, AHEAD + i * 4)
                            nc.tensor.matmul(ps[0:32, 4 + k, 0:CPX], blk_r[:, :], d_band[:, u, part], start=True, stop=True)
                            for n in range(2):
                                nc.tensor.matmul(ps[32:64, 4 + k, 0:CPX], hash_lhs[:, n, :], s_band[:, u, part],
                                                 start=(n == 0), stop=(n == 1))
                            nc.tensor.matmul(ps[64:96, 4 + k, 0:CPX], blk_bf[:, :], q_band[:, u, part], start=True, stop=True)\
                                .then_inc(m_ps, 1)
                pe.wait_ge(sm_dve, 5 * q + 1)
                nc.tensor.transpose(ps[0:4, 7, 0:H], mm[:, 0:4], const("ident", H)[:, 0:H]).then_inc(sm_pe, 1)
                pe.wait_ge(sm_dve, 5 * q + 2)
                nc.tensor.matmul(ps[0:H, 7, 0:4], ones4[:, :], diag[:, 0:4], start=True, stop=True).then_inc(sm_pe, 1)
                pe.wait_ge(sm_dve, 5 * q + 3)
                for im in range(2):
                    nc.tensor.transpose(ps[0:H, 7, im * H:(im + 1) * H], kmap[:, im, :], const("ident", H)[:, 0:H])
                nc.tensor.matmul(ps[0:H, 7, 2 * H:2 * H + 1], const("ident", H)[:, 0:H], mm[:, 0:1], start=True, stop=False, skip_group_check=True)
                nc.tensor.matmul(ps[0:H, 7, 2 * H:2 * H + 1], const("pair", H), mm[:, 1:2], start=False, stop=True, skip_group_check=True)\
                    .then_inc(sm_pe, 1)
                pe.wait_ge(sm_dve, 5 * q + 4)
                nc.tensor.matmul(ps[0:H, 7, 0:1], const("tri", H), hot[:, H:H + 1], start=True, stop=True).then_inc(sm_pe, 1)
                pe.wait_ge(sm_dve, 5 * q + 5)
                nc.tensor.matmul(ps[0:1, 7, 0:H], const("hval", H), hot[:, 0:H], start=True, stop=True)
                nc.tensor.matmul(ps[0:1, 7, H:H + 1], const("one", H), hot[:, H:H + 1], start=True, stop=True).then_inc(sm_pe, 1)
                pe.wait_ge(lst_ok, q + 1)
                count = pe.value_load(lst[0:1, H:H + 1], min_val=1, max_val=H)
                before = pe.value_load(lst[0:1, H + 1:H + 2], min_val=0, max_val=H * PAIRS)
                with pe.Fori(0, count) as i:
                    row = before + i
                    pe.wait_ge(r_act, row * 4 + 2)
                    pe.wait_ge(r_dve, row * 5 + 2)
                    pe.wait_ge(lst_ok, q + 1)
                    for j in range(GEN):
                        nc.tensor.matmul(ps[0:H, 6, 2 * j:2 * j + 2], prod[:, j, :], const("blk")[:, 0:2], start=True, stop=True)
                    for j in range(GEN):
                        ins = nc.tensor.matmul(ps[0:H, 6, 2 * GEN + 2 * j:2 * GEN + 2 * j + 2], gsq[:, j // 3, j % 3:j % 3 + W],
                                               const("blk")[:, 0:2], start=True, stop=True)
                    ins.then_inc(r_pe, 1)
                    pe.wait_ge(r_dve, row * 5 + 5)
                    pe.wait_ge(lst_ok, q + 1)
                    for j in range(GEN):
                        ins = nc.tensor.matmul(ps[:, j // 3, (j % 3) * W:(j % 3 + 1) * W], wrep[:, j].rearrange("p i c -> p (i c)"),
                                               const("ident", H)[:, 0:H], start=True, stop=True)
                    ins.then_inc(r_pe, 1)
                    pe.wait_ge(r_done, AHEAD + row + 1)
                with pe.Fori(0, CHUNKS // 2) as i:
                    for u in range(2):
                        chunk = CHUNKS * q + i * 2 + u
                        if q:
                            pe.wait_ge(h_sb, AHEAD + chunk - 1)
                        elif u == 0:
                            pe.wait_ge(h_sb, AHEAD + i * 2)
                        for im in range(2):
                            ins = nc.tensor.matmul(ps[:, 2 * u + im, 0:CPX], w1_lhs[:, im, :],
                                                   enh[:, bass.ds((i * 2 + u) * CPX, CPX)], start=True, stop=True)
                        ins.then_inc(h_ps, 1)
                        pe.wait_ge(h_sb, AHEAD + chunk + 1)
                        if q:
                            pe.wait_ge(y_ok, AHEAD + chunk - 1)
                        elif u == 0:
                            pe.wait_ge(y_ok, AHEAD + i * 2)
                        for im in range(2):
                            ins = nc.tensor.matmul(ps[:, 4 + u, 0:CPX], w2_lhs[:, im, :], hid[:, u, im, :],
                                                   start=(im == 0), stop=(im == 1))
                        ins.then_inc(f_ps, 1)


_INS = ["x", "L0_conv_w_off", "L0_conv_b_off", "L0_conv_w_conv", "L0_conv_b_conv", "L1_conv_gamma", "L1_conv_beta",
        "L1_conv_w1", "L1_conv_b1", "L1_conv_w2", "L1_conv_b2"]


def kernel(**inputs):
    import concourse.bacc as bacc
    from concourse.bass_utils import run_bass_kernel_spmd as run

    nc = bacc.Bacc("TRN2", target_bir_lowering=False, num_devices=1)
    arrays, args = {}, []
    for name in _INS:
        a = np.ascontiguousarray(inputs[name])
        if name == "x":
            a = a.reshape(PAIRS, P, PX)
        arrays[name] = a
        args.append(nc.dram_tensor(name, a.shape, F32, kind="ExternalInput").ap())
    arrays["consts"] = constants()
    args.append(nc.dram_tensor("consts", (P, N_CONST), F32, kind="ExternalInput").ap())
    args.append([nc.dram_tensor(f"table{q}", (2 * IMG_ENTRIES, ENTRY), F32).ap() for q in range(PAIRS)])
    args.append(nc.dram_tensor("sums", (3, 2, PX), F32).ap())
    out = nc.dram_tensor("y", (PAIRS, P, PX), F32, kind="ExternalOutput").ap()
    program(nc, *args, out)
    r = run(nc, [arrays], core_ids=[0])
    return r.results[0]["y"].reshape(N_IMG, C, H, W)
```

```python
import itertools
from contextlib import ExitStack

import numpy as np

import concourse.bass as bass
from concourse import mybir

F32 = mybir.dt.float32
BF16 = mybir.dt.bfloat16
I32 = mybir.dt.int32
ALU = mybir.AluOpType
ACT = mybir.ActivationFunctionType
AX = mybir.AxisListType

N_IMG, C, H, W = 8, 64, 80, 80
PAIRS = N_IMG // 2
PX = H * W
P = 2 * C
TAPS = 9
GEN = 9
HID = 2 * C
HP, WP = H + 2, W + 2
BAND = 8
BANDS = H // BAND
BPX = BAND * W
TILES = BPX // 128
NT = BANDS * TILES
ROWS = 4
CPX = ROWS * W
CHUNKS = H // ROWS
EPS = 1e-5
ENTRY = 2 * C
IMG_ENTRIES = W + PX
AHEAD = 64
MAGIC = 12582912.0
OFFC = 2 * TAPS
LN_SHIFT = 2.0 ** 30

_COLS = {}
_n = 0
for _name, _w in [("ident", P), ("group", P), ("selz", 4), ("grid", NT * 2), ("blk", 32), ("hash_hi", 32),
                  ("hash_lo", 32), ("tri", H), ("pair", H), ("iota", H), ("hval", 1), ("one", 1),
                  ("lower", GEN * GEN), ("rowmask", HP)]:
    _COLS[_name] = (_n, _n + _w)
    _n += _w
N_CONST = _n


def constants():
    c = np.zeros((P, N_CONST), np.float32)

    def put(name, a):
        c[:a.shape[0], _COLS[name][0]:_COLS[name][1]] = a

    put("ident", np.eye(P))
    k = np.arange(P)
    put("group", 0.5 * (k[:, None] // 2 == k[None, :] // 2))
    row = np.arange(2 * OFFC)
    sel = np.zeros((P, 4))
    sel[64 + row, row // TAPS] = 1.0 / TAPS
    put("selz", sel)
    line = np.linspace(-1.0, 1.0, H, dtype=np.float32)
    pixel = np.arange(NT)[None, :] * P + k[:, None]
    put("grid", np.stack([line[pixel // W], line[pixel % W]], -1).reshape(P, NT * 2))
    blk = np.zeros((P, 32))
    blk[k, k // C] = 1.0
    put("blk", blk)
    code = np.random.RandomState(7).randint(1, 1 << 16, C)
    for name, part in (("hash_hi", code // 256 * 256), ("hash_lo", code % 256)):
        m = np.zeros((P, 32))
        m[k, k // C] = np.tile(part, 2)
        put(name, m)
    h = np.arange(H)
    put("tri", (h[:, None] < h[None, :]) * 1.0)
    put("pair", (h[:, None] == h[None, :]) * 1.0 + (h[:, None] + 1 == h[None, :]))
    put("iota", np.tile(h, (P, 1)))
    put("hval", h[:, None])
    put("one", np.ones((P, 1)))
    j = np.arange(GEN)
    put("lower", np.tile((j[None, :] < j[:, None]).reshape(1, -1) * 1.0, (P, 1)))
    m = np.ones((P, HP))
    m[:, [0, -1]] = 0.0
    put("rowmask", m)
    return c


class Chain:

    def __init__(self, eng, sem):
        self.eng, self.sem, self.base, self.n = eng, sem, 0, 0

    def link(self, ins):
        ins.then_inc(self.sem, 1)
        self.n += 1
        self.eng.wait_ge(self.sem, self.base + self.n)

    def loop(self, i, per):
        self.saved = (self.base, self.n)
        self.base, self.n = self.base + self.n + i * per, 0
        self.per = per

    def end(self, iterations):
        assert self.n == self.per, (self.n, self.per)
        self.base, self.n = self.saved
        self.n += iterations * self.per


def program(nc, x_d, w_off_d, b_off_d, w_conv_d, b_conv_d, gamma_d, beta_d, w1_d, b1_d, w2_d, b2_d, const_d, tables, sums, out_d):
    with ExitStack() as ctx:
        def sb(name, shape, dt=F32):
            return ctx.enter_context(nc.sbuf_tensor(name, shape, dt))

        def sem(name):
            return ctx.enter_context(nc.semaphore(name))

        cst = sb("cst", [P, N_CONST])

        def const(name, rows=P):
            a, b = _COLS[name]
            return cst[0:rows, a:b]

        off_lhs = sb("off_lhs", [P, 2 * OFFC])
        b_off_raw = sb("b_off_raw", [P, 2 * TAPS])
        conv_lhs = sb("conv_lhs", [P, TAPS, P])
        w1_lhs = sb("w1_lhs", [P, 2, P])
        w2_lhs = sb("w2_lhs", [P, 2, P])
        vec = sb("vec", [P, 8])
        b_conv, gamma, beta, b1, b2 = (vec[:, k:k + 1] for k in range(5))
        grid_b = sb("grid_b", [P, NT, 2])
        hash_lhs = sb("hash_lhs", [P, 2, 32], BF16)
        blk_bf = sb("blk_bf", [P, 32], BF16)
        xb = [sb(f"xb{k}", [P, HP * W]) for k in range(2)]
        g_band = sb("g_band", [P, 2, BPX])
        d_band = sb("d_band", [P, 2, BPX])
        m_band = sb("m_band", [96, 2, BPX])
        zbuf = sb("zbuf", [P, HP * WP])
        gat = sb("gat", [P, 2, TILES, 2, 2 * ENTRY])
        idx_i = sb("idx_i", [P, NT, 2], I32)
        idx_s = sb("idx_s", [P, 2, TILES * 2], I32)
        wgt = sb("wgt", [P, NT * 2, 4])
        tok = gat[:, 0].rearrange("p t i n -> p (t i n)")[:, 0:2 * BPX].rearrange("p (u t i c) -> p u t i c", u=2, t=TILES, i=2)
        wtok = g_band[:].rearrange("p u (t i c) -> p u t i c", t=TILES, i=2)
        wpad = sb("wpad", [P, HP * WP])
        hsum = sb("hsum", [P, 2, BAND * (W // 2)])
        xd = sb("xd", [P, 42, 42])
        up = sb("up", [P, 2, BAND, 42])
        s_band = sb("s_band", [P, 2, BPX], BF16)
        q_band = sb("q_band", [P, 2, BPX], BF16)
        enh = sb("enh", [P, PX])
        at = 0
        w_off_raw = enh[:, at:at + 2 * TAPS * TAPS]
        at += 2 * TAPS * TAPS
        conv_raw = enh[:, at:at + C * TAPS]
        at += C * TAPS
        conv_blk = enh[:, at:at + P]
        at += P
        w1_raw = enh[:, at:at + 2 * C].rearrange("p (a c) -> p a c", a=2)
        at += 2 * C
        w2_raw = enh[0:C, at:at + HID]
        hid = d_band[:, 0].rearrange("p (i n) -> p i n", i=2)
        stats = sb("stats", [P, CHUNKS * 6])
        stats_a = sb("stats_a", [P, 16 * 6])
        sv = sb("sv", [P, 24])
        sa = sb("sa", [P, 24])
        pos = sb("pos", [P, NT * 2, 2])
        cell = sb("cell", [P, NT * 2, 2])
        tent = sb("tent", [P, 2, NT * 2, 2])
        ent = sb("ent", [P, NT * 2])
        maps = sb("maps", [H, 4, 2, W])
        fl = sb("fl", [H, 2, 2, W])
        kmap = sb("kmap", [H, 2, W])
        kcol = sb("kcol", [H, 2, H])
        mm = sb("mm", [H, 12])
        diag = sb("diag", [4, 8])
        ones4 = sb("ones4", [4, H])
        hot = sb("hot", [H, H + 1])
        lst = sb("lst", [1, H + 2], I32)
        cum = sb("cum", [1, 2])
        blk_r = sb("blk_r", [P, 32])
        grow = sb("grow", [P, 3, WP])
        gsq = d_band[:].rearrange("p u n -> p (u n)")[:, GEN * W:GEN * W + 3 * WP].rearrange("p (a w) -> p a w", a=3)
        prod = d_band[:].rearrange("p u n -> p (u n)")[:, 0:GEN * W].rearrange("p (j w) -> p j w", w=W)
        rn = sb("rn", [H, 6, GEN, 2])
        sim = sb("sim", [H, 2, GEN])
        cmp = sb("cmp", [H, 2, 2, GEN, GEN])
        sel = sb("sel", [H, 6, 2, GEN])
        dent = sb("dent", [H, 2, 2])
        wrep = m_band[0:H].rearrange("p u n -> p (u n)")[:, 0:GEN * P].rearrange("p (j i c) -> p j i c", j=GEN, i=2)
        agg = hsum[:, 1, 0:2 * W].rearrange("p (a w) -> p a w", a=2)

        def windows(dy):
            return bass.AP(grow[:].tensor, grow[:, dy, 0:1].offset, [list(grow[:].ap[0]), [1, 3], [1, W]])

        ps = ctx.enter_context(nc.psum_tensor("ps", [P, 8, 512], F32))
        flat = ps[:, :, :].rearrange("p b n -> p (b n)")

        c_in = sem("c_in"); w_in = sem("w_in")
        setup_dve = sem("setup_dve"); setup_pe = sem("setup_pe"); ready = sem("ready"); pool_zero = sem("pool_zero"); table_zero = sem("table_zero")
        x_in = [sem(f"x_in{k}") for k in range(2)]
        dve = sem("dve"); act_own = sem("act_own")
        grp_in = sem("grp_in"); grp_out = sem("grp_out"); ln_in = sem("ln_in"); ln_out = sem("ln_out")
        norm_a = sem("norm_a"); norm_b = sem("norm_b")
        g_ok = sem("g_ok"); z_ps = sem("z_ps"); z_sb = sem("z_sb"); t_ps = sem("t_ps"); tok_ok = sem("tok_ok")
        tok_out = [sem(f"tok_out{k}") for k in range(2)]
        z_shift = sem("z_shift"); off_ps = sem("off_ps"); idx_ok = sem("idx_ok")
        staged = [sem(f"staged{k}") for k in range(2)]
        gat_in = [sem(f"gat_in{k}") for k in range(2)]
        wtok_ok = sem("wtok_ok"); w_ps = sem("w_ps"); w_sb = sem("w_sb")
        conv_ps = sem("conv_ps"); x1_ok = sem("x1_ok")
        d_ok = sem("d_ok"); feat_ok = sem("feat_ok"); m_ps = sem("m_ps"); m_sb = sem("m_sb"); enh_ok = sem("enh_ok")
        maps_in = sem("maps_in")
        sm_pe = sem("sm_pe"); sm_dve = sem("sm_dve"); lst_ok = sem("lst_ok")
        r_act = sem("r_act"); r_dve = sem("r_dve"); r_pe = sem("r_pe"); r_own = sem("r_own"); r_done = sem("r_done")
        ln_r = sem("ln_r")
        h_ps = sem("h_ps"); h_sb = sem("h_sb"); f_ps = sem("f_ps"); y_ok = sem("y_ok")
        y_out = sem("y_out"); r_done2 = sem("r_done2")
        m_out = [sem(f"m_out{k}") for k in range(2)]

        block = ctx.enter_context(nc.Block())

        ROUNDS = range(-1, PAIRS + 1)

        def sweep(eng, step, own=None, links=0):
            step(0, 0, 0, True)
            with eng.Fori(0, BANDS // 2 - 1) as i:
                if own:
                    own.loop(i, 2 * links)
                step(i * 2 + 1, i, 1, False)
                step(i * 2 + 2, i + 1, 0, False)
                if own:
                    own.end(BANDS // 2 - 1)
            step(BANDS - 1, BANDS // 2 - 1, 1, False)

        def rows(buf, first, n=BAND, width=W, col=0, wide=W):
            return buf[:, bass.ds(first * wide, n * wide)].rearrange("p (r w) -> p r w", w=wide)[:, :, col:col + width]

        @block.sync
        def _(sp):
            sp.dma_start(cst[:, :], const_d).then_inc(c_in, 16)
            sp.dma_start(xb[0][:, W:W + PX], x_d[0]).then_inc(x_in[0], 16)
            sp.dma_start(xb[1][:, W:W + PX], x_d[1]).then_inc(x_in[1], 16)
            for half in range(2):
                sp.dma_start(w_off_raw[half * C:(half + 1) * C, :].rearrange("c (o t) -> c o t", t=TAPS),
                             w_off_d.rearrange("o c a b -> c o (a b)")).then_inc(w_in, 16)
                sp.dma_start(conv_raw[half * C:(half + 1) * C, :],
                             w_conv_d.rearrange("o c a b -> o (c a b)")).then_inc(w_in, 16)
                sp.dma_start(w1_raw[:, half, :], w1_d).then_inc(w_in, 16)
                for k, v in enumerate((b_conv_d, gamma_d, beta_d, None, b2_d)):
                    if v is not None:
                        sp.dma_start(vec[half * C:(half + 1) * C, k:k + 1],
                                     v.rearrange("(c a) -> c a", a=1)).then_inc(w_in, 16)
            sp.dma_start(vec[:, 3:4], b1_d.rearrange("(c a) -> c a", a=1)).then_inc(w_in, 16)
            sp.dma_start(w2_raw[:, :], w2_d).then_inc(w_in, 16)
            sp.dma_start(b_off_raw[:, :], b_off_d.rearrange("(a n) -> a n", a=1).broadcast_to([P, 2 * TAPS])).then_inc(w_in, 16)
            sp.wait_ge(pool_zero, 7)
            for q in range(PAIRS):
                for im in range(2):
                    a = im * IMG_ENTRIES
                    sp.dma_start(tables[q][a:a + W, 0:C], zbuf[0:W, 0:C]).then_inc(table_zero, 16)
                    sp.dma_start(tables[q][a + PX:a + PX + W, C:2 * C], zbuf[0:W, 0:C]).then_inc(table_zero, 16)
            for q in ROUNDS:
                cur, last, nxt = 0 <= q < PAIRS, q >= 1, q + 1 < PAIRS
                if last:
                    with sp.Fori(0, BANDS // 2) as i:
                        for u in range(2):
                            at = (i * 2 + u) * BPX
                            sp.wait_ge(y_ok, AHEAD + CHUNKS * (q - 1) + (i * 2 + u) * 2 + 2)
                            sp.dma_start(out_d[q - 1][:, bass.ds(at, BPX)], enh[:, bass.ds(at, BPX)]).then_inc(y_out, 16)
                            if nxt:
                                sp.dma_start(xb[(q + 1) % 2][:, bass.ds(at + W, BPX)], x_d[q + 1][:, bass.ds(at, BPX)])\
                                  .then_inc(x_in[(q + 1) % 2], 16)
                if q == PAIRS:
                    continue
                with sp.Fori(0, BANDS // 2) as i:
                    for u in range(2):
                        if nxt:
                            sp.wait_ge(tok_ok, AHEAD + BANDS * (q + 1) + i * 2 + u + 1)
                            for im in range(2):
                                for dy in range(2):
                                    first = im * IMG_ENTRIES + W - dy * W
                                    sp.dma_start(tables[q + 1][bass.ds((i * 2 + u) * BPX + first, BPX), dy * C:(dy + 1) * C].rearrange(
                                        "(t p) c -> p t c", p=P), tok[:, u, :, im, :]).then_inc(tok_out[u], 16)
                        if cur:
                            sp.wait_ge(m_sb, AHEAD + CHUNKS * q + (i * 2 + u) * 2 + 2)
                            for k in (2, 1, 0):
                                sp.dma_start(sums[k][:, bass.ds((i * 2 + u) * BPX, BPX)], m_band[32 * k:32 * k + 2, u, :])\
                                  .then_inc(m_out[u], 16)
                if nxt:
                    sp.wait_ge(z_sb, AHEAD + CHUNKS * (q + 2))
                    for t in range(TAPS):
                        dy, dx = t // 3, t % 3
                        src = zbuf[t:2 * OFFC:TAPS, :].rearrange("p (h w) -> p h w", w=WP)[:, dy:dy + H, dx:dx + W]
                        sp.dma_start(zbuf[64 + t:64 + 2 * OFFC:TAPS, 0:PX].rearrange("p (h w) -> p h w", w=W), src)\
                          .then_inc(z_shift, 16)
                if cur:
                    for u in range(2):
                        sp.wait_ge(m_out[u], AHEAD + 16 * 3 * (BANDS // 2) * (q + 1))
                    for k, (kind, shift) in enumerate(((0, 0), (1, 0), (2, 0), (1, 1))):
                        sp.dma_start(maps[0:H - shift, k], sums[kind][:, shift * W:PX].rearrange("i (h w) -> h i w", w=W))\
                          .then_inc(maps_in, 16)
            sp.wait_ge(y_out, 16 * BANDS * PAIRS)

        @block.gpsimd
        def _(pool):
            for counter in (z_ps, t_ps, wtok_ok, z_sb, tok_ok, w_sb, w_ps, x1_ok, m_ps, m_sb, feat_ok, h_sb, f_ps, y_ok, r_done, conv_ps, *tok_out, *m_out):
                pool.sem_inc(counter, AHEAD)
            nc.gpsimd.memset(zbuf[:, :], 0.0).then_inc(pool_zero, 1)
            nc.gpsimd.memset(wpad[:, :], 0.0).then_inc(pool_zero, 1)
            nc.gpsimd.memset(grow[:, :, :], 0.0).then_inc(pool_zero, 1)
            for k in range(2):
                nc.gpsimd.memset(xb[k][:, 0:W], 0.0).then_inc(pool_zero, 1)
                nc.gpsimd.memset(xb[k][:, W + PX:], 0.0).then_inc(pool_zero, 1)
            for q in range(PAIRS):
                pool.wait_ge(idx_ok, q + 1)
                for k in range(2):
                    pool.wait_ge(tok_out[k], AHEAD + 16 * 4 * (BANDS // 2) * (q + 1))
                before = (BANDS // 2) * q
                with pool.Fori(before + 1, before + 1 + BANDS // 2) as copies:
                    i = copies - (before + 1)
                    for u in range(2):
                        pool.wait_ge(wtok_ok, AHEAD + BANDS * q + i * 2 + u - 1)
                        nc.gpsimd.tensor_copy(idx_s[:, u, :], idx_i[:, bass.ds((i * 2 + u) * TILES, TILES), :].rearrange(
                            "p t m -> p (t m)")).then_inc(staged[u], 1)
                        pool.wait_ge(table_zero, 16 * 4 * PAIRS)
                        pool.wait_ge(staged[u], copies)
                        for t in range(TILES):
                            for im in range(2):
                                pool.indirect_dma_start(gat[:, u, t, im, :], None, tables[q][:, :],
                                                        bass.IndirectOffsetOnAxis(ap=idx_s[:, u, 2 * t + im:2 * t + im + 1], axis=0))\
                                    .then_inc(gat_in[u], 16)

        @block.scalar
        def _(act):
            own = Chain(act, act_own)
            act.preload_act_table_set("natural_log_exp_and_others")

            turn = itertools.count(1)

            def rsqrt_seed(src, mid, dst):
                act.wait_ge(ln_in, next(turn))
                own.link(nc.scalar.activation(mid, src, ACT.Ln))
                nc.scalar.activation(dst, mid, ACT.Exp, scale=-0.5).then_inc(ln_out, 1)

            act.wait_ge(c_in, 16)
            for q in ROUNDS:
                cur, last, nxt = 0 <= q < PAIRS, q >= 1, q + 1 < PAIRS
                x = xb[q % 2]

                def step(b, n, u, first):
                    if last:
                        for k in range(2):
                            chunk = CHUNKS * (q - 1) + b * 2 + k
                            act.wait_ge(h_ps, chunk + 1)
                            act.wait_ge(f_ps, AHEAD + chunk)
                            act.wait_ge(c_in, 16)
                            for im in range(2):
                                ins = nc.scalar.activation(hid[:, im, :], ps[:, 4 + im, 0:CPX], ACT.Relu, bias=b1)
                            ins.then_inc(h_sb, 1)
                    if cur:
                        act.wait_ge(w_ps, AHEAD + BANDS * q + b + 1)
                        act.wait_ge(c_in, 16)
                        nc.scalar.activation(rows(wpad, b * BAND + 1, BAND, W, 1, WP),
                                             flat[:, 0:BPX].rearrange("p (h w) -> p h w", w=W), ACT.Copy).then_inc(w_sb, 1)

                if q >= 0:
                    if q and cur:
                        act.wait_ge(conv_ps, AHEAD + CHUNKS * q)
                    sweep(act, step)
                if q == PAIRS:
                    continue
                if cur:
                    rsqrt_seed(sv[:, 4:5], sv[:, 5:6], sv[:, 6:7])
                if nxt:
                    rsqrt_seed(sa[:, 4:5], sa[:, 5:6], sa[:, 6:7])
                if cur:
                    rsqrt_seed(sv[:, 11:12], sv[:, 5:6], sv[:, 12:13])
                if nxt:
                    act.wait_ge(norm_a, q + 2)
                if cur:
                    act.wait_ge(norm_b, q + 1)
                else:
                    act.wait_ge(pool_zero, 7)
                if q > 0:
                    act.wait_ge(y_out, 16 * BANDS * q)
                with act.Fori(0, BANDS // 2) as i:
                    for u in range(2):
                        at = (i * 2 + u) * BPX
                        band = BANDS * q + i * 2 + u
                        band_a = BANDS * (q + 1) + i * 2 + u
                        if nxt:
                            act.wait_ge(z_ps, AHEAD + 2 * (band_a - 1))
                            act.wait_ge(t_ps, AHEAD + band_a - 1)
                            act.wait_ge(c_in, 16)
                            nc.scalar.activation(g_band[:, u, :], xb[(q + 1) % 2][:, bass.ds(at + W, BPX)], ACT.Identity,
                                                 bias=sa[:, 8:9], scale=sa[:, 7:8]).then_inc(g_ok, 1)
                        if cur:
                            src = x[:, bass.ds(at + W, BPX)]
                            act.wait_ge(m_ps, AHEAD + 2 * (band - 1))
                            act.wait_ge(d_ok, band + 1)
                            act.wait_ge(c_in, 16)
                            nc.scalar.activation(d_band[:, u, :], d_band[:, u, :], ACT.Abs)
                            nc.scalar.activation(s_band[:, u, :], src, ACT.Sign, bias=sv[:, 8:9], scale=sv[:, 7:8])
                            nc.scalar.activation(q_band[:, u, :], src, ACT.Square, bias=sv[:, 8:9], scale=sv[:, 7:8]).then_inc(feat_ok, 1)
                        if nxt:
                            for k in range(2):
                                act.wait_ge(z_ps, AHEAD + 2 * band_a + k + 1)
                                act.wait_ge(c_in, 16)
                                nc.scalar.activation(rows(zbuf[0:2 * OFFC], (i * 2 + u) * BAND + k * ROWS + 1, ROWS, W, 1, WP),
                                                     ps[0:2 * OFFC, 4 + k, 0:CPX].rearrange("p (r w) -> p r w", w=W),
                                                     ACT.Copy).then_inc(z_sb, 1)
                        if cur:
                            nc.scalar.activation(enh[:, bass.ds(at, BPX)], src, ACT.Identity,
                                                 bias=sv[:, 16:17], scale=sv[:, 15:16]).then_inc(enh_ok, 1)
                            act.wait_ge(m_out[u], AHEAD + 16 * 3 * ((BANDS // 2) * q + i))
                            for k in range(2):
                                act.wait_ge(m_ps, AHEAD + 2 * band + k + 1)
                                act.wait_ge(c_in, 16)
                                nc.scalar.activation(m_band[:, u, k * CPX:(k + 1) * CPX], ps[0:96, 2 + k, 0:CPX],
                                                     ACT.Copy).then_inc(m_sb, 1)
                if not cur:
                    continue
                act.wait_ge(lst_ok, q + 1)
                count = act.value_load(lst[0:1, H:H + 1], min_val=1, max_val=H)
                before = act.value_load(lst[0:1, H + 1:H + 2], min_val=0, max_val=H * PAIRS)
                with act.Fori(0, count) as i:
                    h = act.value_load(lst[0:1, bass.ds(i, 1)], min_val=0, max_val=H - 1)
                    act.wait_ge(r_done, AHEAD + before + i)
                    act.wait_ge(lst_ok, q + 1)
                    nc.scalar.activation(grow[:, :, 1:1 + W], rows(x, h, 3), ACT.Identity,
                                         bias=sv[:, 8:9], scale=sv[:, 7:8]).then_inc(r_act, 1)
                    act.wait_ge(r_dve, (before + i) * 5 + 1)
                    nc.scalar.activation(gsq[:, :, :], grow[:, :, :], ACT.Square).then_inc(r_act, 1)
                    act.wait_ge(r_dve, (before + i) * 5 + 3)
                    nc.scalar.activation(rn[:, 1], rn[:, 0], ACT.Ln, scale=LN_SHIFT).then_inc(ln_r, 1)
                    act.wait_ge(ln_r, before + i + 1)
                    nc.scalar.activation(rn[:, 2], rn[:, 1], ACT.Exp, scale=-0.5).then_inc(r_act, 1)
                    act.wait_ge(r_dve, (before + i) * 5 + 4)
                    nc.scalar.activation(sel[:, 0], sim[:, :, :], ACT.Exp).then_inc(r_act, 1)

        @block.vector
        def _(v):
            own = Chain(v, dve)

            def link(ins):
                own.link(ins)

            for t in (off_lhs, conv_blk, w1_lhs, w2_lhs):
                nc.vector.memset(t[:], 0.0).then_inc(setup_dve, 1)
            nc.vector.memset(ones4[:], 1.0).then_inc(setup_dve, 1)
            nc.vector.memset(cum[:], 0.0).then_inc(setup_dve, 1)
            nc.vector.memset(maps[:], -1.0e9).then_inc(setup_dve, 1)
            v.wait_ge(setup_dve, 7)
            v.wait_ge(c_in, 16)
            v.wait_ge(w_in, 16 * 17)
            raw = w_off_raw[:, :].rearrange("p (o k t) -> p o t k", o=2, t=TAPS)
            for im in range(2):
                a = slice(im * C, (im + 1) * C)
                nc.vector.tensor_reduce(off_lhs[a, im * OFFC:(im + 1) * OFFC].rearrange("p (o t) -> p o t", o=2),
                                        raw[a], AX.X, ALU.add)
            link(nc.vector.tensor_reduce(sv[:, 20:22], b_off_raw[:, :].rearrange("p (o k) -> p o k", o=2), AX.X, ALU.add))
            for o in range(2):
                link(nc.vector.tensor_scalar(sv[:, 22 + o:23 + o], sv[:, 20 + o:21 + o], 1.0 / TAPS, None, ALU.mult))
                link(nc.vector.tensor_scalar(grid_b[:, :, o], const("grid").rearrange("p (t o) -> p t o", o=2)[:, :, o],
                                             sv[:, 22 + o:23 + o], None, ALU.add))
            link(nc.vector.tensor_copy(hash_lhs[:, 0, :], const("hash_hi")))
            link(nc.vector.tensor_copy(hash_lhs[:, 1, :], const("hash_lo")))
            link(nc.vector.tensor_copy(blk_bf[:, :], const("blk")))
            for t in range(TAPS):
                for im in range(2):
                    a = slice(im * C, (im + 1) * C)
                    ins = nc.vector.tensor_copy(conv_blk[a, im * C:(im + 1) * C],
                                                conv_raw[a, :].rearrange("p (c t) -> p c t", t=TAPS)[:, :, t])
                ins.then_inc(ready, 1)
                v.wait_ge(setup_pe, t + 1)
                link(nc.vector.tensor_copy(conv_lhs[:, t, :], ps[:, 0, 0:P]))
            v.wait_ge(setup_pe, TAPS + 2)
            for im in range(2):
                a = slice(im * C, (im + 1) * C)
                link(nc.vector.tensor_copy(w1_lhs[a, im, :], ps[a, 1, 0:P]))
                link(nc.vector.tensor_copy(w2_lhs[:, im, a], ps[:, 2, 0:C]))
            nc.vector.tensor_copy(sv[:, 23:24], sv[:, 22:23]).then_inc(ready, 1)

            turn = itertools.count(1)

            def variance(t, bank, n):
                v.wait_ge(grp_out, n + 1)
                link(nc.vector.tensor_copy(t[:, 2:4], ps[:, bank, 0:2]))
                link(nc.vector.tensor_tensor(t[:, 9:10], t[:, 0:1], t[:, 2:3], ALU.subtract))
                link(nc.vector.tensor_tensor(t[:, 9:10], t[:, 9:10], t[:, 9:10], ALU.mult))
                link(nc.vector.tensor_tensor(t[:, 10:11], t[:, 9:10], t[:, 3:4], ALU.add))
                nc.vector.tensor_scalar(t[:, 4:5], t[:, 10:11], EPS, None, ALU.add).then_inc(ln_in, 1)

            def refine(t, val, seed, dst):
                v.wait_ge(ln_out, next(turn))
                link(nc.vector.tensor_tensor(t[:, 9:10], seed, seed, ALU.mult))
                link(nc.vector.tensor_tensor(t[:, 9:10], t[:, 9:10], val, ALU.mult))
                link(nc.vector.tensor_scalar(t[:, 9:10], t[:, 9:10], -0.5, 1.5, ALU.mult, ALU.add))
                link(nc.vector.tensor_tensor(dst, t[:, 9:10], seed, ALU.mult))

            def minus_mean(t):
                return nc.vector.scalar_tensor_tensor(out=t[:, 8:9], in0=t[:, 2:3], scalar=-1.0, in1=t[:, 7:8],
                                                      op0=ALU.mult, op1=ALU.mult)

            for q in ROUNDS:
                cur, last, nxt = 0 <= q < PAIRS, q >= 1, q + 1 < PAIRS
                x, other = xb[q % 2], xb[(q + 1) % 2]

                def residual(b, k):
                    chunk = b * 2 + k
                    v.wait_ge(conv_ps, AHEAD + CHUNKS * q + chunk + 1)
                    xs = x[:, bass.ds(chunk * CPX + W, CPX)]
                    nc.vector.scalar_tensor_tensor(out=xs, in0=ps[:, 2 + k, 0:CPX], scalar=b_conv, in1=xs,
                                                   op0=ALU.add, op1=ALU.add).then_inc(x1_ok, 1)

                def measure(b):
                    v.wait_ge(x1_ok, AHEAD + CHUNKS * q + b * 2 + 2)
                    for k in range(2):
                        nc.vector.bn_stats(stats[:, bass.ds((b * 2 + k) * 6, 6)], x[:, bass.ds((b * 2 + k) * CPX + W, CPX)])
                    img = x[:, bass.ds(b * BPX + W, BPX)].rearrange("p (n b) -> p n b", b=2)
                    link(nc.vector.tensor_tensor(hsum[:, 0, :], img[:, :, 0], img[:, :, 1], ALU.add))
                    hs = hsum[:, 0, :].rearrange("p (h a w) -> p h a w", a=2, w=W // 2)
                    link(nc.vector.tensor_tensor(xd[:, bass.ds(b * (BAND // 2) + 1, BAND // 2), 1:41],
                                                 hs[:, :, 0, :], hs[:, :, 1, :], ALU.add))

                def step(b, n, u, first):
                    if cur:
                        v.wait_ge(gat_in[u], 16 * 2 * TILES * ((BANDS // 2) * q + n + 1))
                        g = gat[:, u].rearrange("p t i (k c) -> p (t i k) c", c=C)
                        wb = wgt[:, bass.ds(b * 2 * TILES, 2 * TILES), :].rearrange("p t k -> p (t k)")\
                            .unsqueeze(2).broadcast_to([P, 8 * TILES, C])
                        link(nc.vector.tensor_tensor(g, g, wb, ALU.mult))
                        g2 = gat[:, u].rearrange("p t i (k c) -> p (t i) k c", k=2)
                        link(nc.vector.tensor_tensor(g2[:, :, 0, :], g2[:, :, 0, :], g2[:, :, 1, :], ALU.add))
                        v.wait_ge(w_ps, AHEAD + BANDS * q + b - 1)
                        nc.vector.tensor_tensor(wtok[:, u].rearrange("p t i c -> p (t i) c"), g2[:, :, 0, 0:C],
                                                g2[:, :, 0, C:2 * C], ALU.add).then_inc(wtok_ok, 1)
                    if cur and not first:
                        residual(b - 1, 0)
                    if last:
                        for k in range(2):
                            chunk = b * 2 + k
                            v.wait_ge(f_ps, AHEAD + CHUNKS * (q - 1) + chunk + 1)
                            y = enh[:, bass.ds(chunk * CPX, CPX)]
                            link(nc.vector.scalar_tensor_tensor(out=y, in0=ps[:, 6 + k, 0:CPX], scalar=b2, in1=y,
                                                                op0=ALU.add, op1=ALU.add))
                            nc.vector.tensor_tensor(y, y, other[:, bass.ds(chunk * CPX + W, CPX)], ALU.add).then_inc(y_ok, 1)
                    if cur and not first:
                        residual(b - 1, 1)
                        measure(b - 1)

                if q >= 0:
                    sweep(v, step, own, 4 * cur + 2 * last)
                if q == PAIRS:
                    continue
                if cur:
                    for k in range(2):
                        residual(BANDS - 1, k)
                    measure(BANDS - 1)
                    link(nc.vector.bn_aggr(sv[:, 0:2], stats[:, :]))
                    nc.vector.tensor_copy(sv[:, 18:20], sv[:, 0:2]).then_inc(grp_in, 1)
                    link(nc.vector.tensor_copy(xd[:, 1:41, 0:42:41], xd[:, 1:41, 1:41:39]))
                    link(nc.vector.tensor_copy(xd[:, 0:42:41, :], xd[:, 1:41:39, :]))
                if nxt:
                    v.wait_ge(x_in[(q + 1) % 2], 16 * (1 + BANDS * ((q + 1) // 2)))
                    with v.Fori(0, 4) as i:
                        for k in range(4):
                            ins = nc.vector.bn_stats(stats_a[:, bass.ds((i * 4 + k) * 6, 6)], other[:, bass.ds((i * 4 + k) * 400 + W, 400)])
                        own.loop(i, 1)
                        link(ins)
                        own.end(4)
                    link(nc.vector.bn_aggr(sa[:, 0:2], stats_a[:, :]))
                    nc.vector.tensor_copy(sa[:, 18:20], sa[:, 0:2]).then_inc(grp_in, 1)
                if cur:
                    variance(sv, 7, 2 * q + 1)
                if nxt:
                    variance(sa, 0, 2 * q + 2)
                if cur:
                    refine(sv, sv[:, 4:5], sv[:, 6:7], sv[:, 7:8])
                    link(minus_mean(sv))
                    link(nc.vector.tensor_tensor(sv[:, 11:12], sv[:, 7:8], sv[:, 7:8], ALU.mult))
                    link(nc.vector.tensor_tensor(sv[:, 11:12], sv[:, 11:12], sv[:, 10:11], ALU.mult))
                    nc.vector.tensor_scalar(sv[:, 11:12], sv[:, 11:12], EPS, None, ALU.add).then_inc(ln_in, 1)
                if nxt:
                    refine(sa, sa[:, 4:5], sa[:, 6:7], sa[:, 7:8])
                    minus_mean(sa).then_inc(norm_a, 1)
                if cur:
                    refine(sv, sv[:, 11:12], sv[:, 12:13], sv[:, 13:14])
                    link(nc.vector.tensor_tensor(sv[:, 14:15], sv[:, 13:14], gamma, ALU.mult))
                    link(nc.vector.scalar_tensor_tensor(out=sv[:, 15:16], in0=sv[:, 14:15], scalar=1.0, in1=sv[:, 7:8],
                                                        op0=ALU.add, op1=ALU.mult))
                    link(nc.vector.tensor_tensor(sv[:, 16:17], sv[:, 2:3], sv[:, 15:16], ALU.mult))
                    link(nc.vector.tensor_tensor(sv[:, 16:17], beta, sv[:, 16:17], ALU.subtract))
                    nc.vector.tensor_scalar(blk_r[:, :], const("blk"), sv[:, 7:8], None, ALU.mult).then_inc(norm_b, 1)
                    v.wait_ge(wtok_ok, AHEAD + BANDS * (q + 1))
                with v.Fori(0, BANDS // 2) as i:
                    if cur:
                        own.loop(i, 8)
                    for u in range(2):
                        band = BANDS * q + i * 2 + u
                        if cur:
                            upr = up[:, u].rearrange("p (h a) w -> p h a w", a=2)
                            half = (i * 2 + u) * (BAND // 2)
                            for a in range(2):
                                link(nc.vector.scalar_tensor_tensor(
                                    out=upr[:, :, a, :], in0=xd[:, bass.ds(half + 1, BAND // 2), :], scalar=3.0,
                                    in1=xd[:, bass.ds(half + 2 * a, BAND // 2), :], op0=ALU.mult, op1=ALU.add))
                            v.wait_ge(m_ps, AHEAD + 2 * (band - 1))
                            db = d_band[:, u, :].rearrange("p (h w a) -> p h w a", w=W // 2, a=2)
                            for a in range(2):
                                link(nc.vector.scalar_tensor_tensor(out=db[:, :, :, a], in0=up[:, u, :, 1:41], scalar=3.0,
                                                                    in1=up[:, u, :, 2 * a:2 * a + 40], op0=ALU.mult, op1=ALU.add))
                            nc.vector.scalar_tensor_tensor(out=d_band[:, u, :], in0=d_band[:, u, :], scalar=-1.0 / 64,
                                                           in1=x[:, bass.ds((i * 2 + u) * BPX + W, BPX)], op0=ALU.mult,
                                                           op1=ALU.add).then_inc(d_ok, 1)
                        if nxt:
                            v.wait_ge(t_ps, AHEAD + BANDS * (q + 1) + i * 2 + u + 1)
                            v.wait_ge(tok_out[u], AHEAD + 16 * 4 * ((BANDS // 2) * (q + 1) + i))
                            nc.vector.tensor_copy(tok[:, u].rearrange("p t i c -> p (t i c)"),
                                                  flat[:, 6 * u * 512:6 * u * 512 + BPX]).then_inc(tok_ok, 1)
                    if cur:
                        own.end(BANDS // 2)
                if nxt:
                    v.wait_ge(off_ps, q + 2)
                    link(nc.vector.tensor_tensor(pos[:, :, :].rearrange("p (t i) o -> p t i o", i=2),
                                                 ps[:, 6, 0:4 * NT].rearrange("p (t i o) -> p t i o", i=2, o=2),
                                                 grid_b[:, :, :].unsqueeze(2).broadcast_to([P, NT, 2, 2]), ALU.add))
                    link(nc.vector.tensor_scalar(pos[:], pos[:], 1.0, 0.5 * (W - 1), ALU.add, ALU.mult))
                    link(nc.vector.tensor_scalar(cell[:], pos[:], -0.5, 0.0, ALU.add, ALU.max))
                    link(nc.vector.tensor_scalar(cell[:], cell[:], float(W - 2), MAGIC, ALU.min, ALU.add))
                    link(nc.vector.tensor_scalar(cell[:], cell[:], MAGIC, None, ALU.subtract))
                    link(nc.vector.tensor_tensor(tent[:, 0], pos[:], cell[:], ALU.subtract))
                    link(nc.vector.tensor_scalar(tent[:, 1], tent[:, 0], 1.0, None, ALU.subtract))
                    tf = tent[:].rearrange("p a t o -> p (a t o)")
                    link(nc.vector.scalar_tensor_tensor(out=tf, in0=tf, scalar=-1.0, in1=tf, op0=ALU.mult, op1=ALU.min))
                    link(nc.vector.tensor_scalar(tent[:], tent[:], 1.0, 0.0, ALU.add, ALU.max))
                    link(nc.vector.tensor_scalar(ent[:], cell[:, :, 1], float(W), None, ALU.mult))
                    link(nc.vector.tensor_tensor(ent[:], ent[:], cell[:, :, 0], ALU.add))
                    for im in range(2):
                        link(nc.vector.tensor_scalar(idx_i[:, :, im], ent[:].rearrange("p (t i) -> p t i", i=2)[:, :, im],
                                                     float(im * IMG_ENTRIES + W), None, ALU.add))
                    for dx in range(2):
                        for dy in range(2):
                            ins = nc.vector.tensor_tensor(wgt[:, :, 2 * dx + dy], tent[:, dx, :, 0], tent[:, dy, :, 1], ALU.mult)
                            if dx + dy < 2:
                                link(ins)
                    ins.then_inc(idx_ok, 1)
                    v.wait_ge(idx_ok, q + 2)
                if not cur:
                    continue
                v.wait_ge(maps_in, 16 * 4 * (q + 1))
                df = maps[:, 0]
                link(nc.vector.tensor_reduce(mm[:, 0:2], df, AX.X, ALU.max))
                link(nc.vector.tensor_reduce(mm[:, 4:6], df, AX.X, ALU.min))
                nc.vector.tensor_scalar(mm[:, 2:4], mm[:, 4:6], -1.0, None, ALU.mult).then_inc(sm_dve, 1)
                v.wait_ge(sm_pe, 5 * q + 1)
                link(nc.vector.tensor_reduce(diag[:, 4:5], ps[0:4, 7, 0:H], AX.X, ALU.max))
                nc.vector.tensor_scalar(diag[:, 0:4], const("ident", 4)[:, 0:4], diag[:, 4:5], None, ALU.mult).then_inc(sm_dve, 1)
                v.wait_ge(sm_pe, 5 * q + 2)
                link(nc.vector.tensor_copy(mm[:, 6:10], ps[0:H, 7, 0:4]))
                link(nc.vector.tensor_tensor(mm[:, 10:12], mm[:, 6:8], mm[:, 8:10], ALU.add))
                link(nc.vector.tensor_scalar(mm[:, 10:12], mm[:, 10:12], 1e-8, None, ALU.add))
                link(nc.vector.reciprocal(mm[:, 10:12], mm[:, 10:12]))
                for im in range(2):
                    link(nc.vector.tensor_scalar(fl[:, 0, im], df[:, im], mm[:, 8 + im:9 + im], mm[:, 10 + im:11 + im],
                                                 ALU.add, ALU.mult))
                link(nc.vector.tensor_tensor(fl[:, 0], fl[:, 0], fl[:, 0], ALU.mult))
                link(nc.vector.tensor_tensor(fl[:, 0], fl[:, 0], fl[:, 0], ALU.mult))
                link(nc.vector.tensor_scalar(kmap[:], fl[:, 0], -0.9, 15.0 / (1.0 - 0.9 + 1e-8), ALU.add, ALU.mult))
                link(nc.vector.tensor_scalar(kmap[:], kmap[:], MAGIC, MAGIC, ALU.add, ALU.subtract))
                link(nc.vector.tensor_scalar(kmap[:], kmap[:], 0.0, None, ALU.max))
                link(nc.vector.tensor_scalar(fl[:, 0], fl[:, 0], 0.9, None, ALU.is_gt))
                link(nc.vector.tensor_tensor(kmap[:], kmap[:], fl[:, 0], ALU.mult))
                link(nc.vector.tensor_scalar(kmap[:], kmap[:], 1.0, float(GEN), ALU.add, ALU.min))
                link(nc.vector.tensor_scalar(fl[:, 0], kmap[:], 1.0, None, ALU.is_gt))
                link(nc.vector.tensor_scalar(fl[:, 1], maps[:, 2], 1e-20, None, ALU.is_lt))
                link(nc.vector.tensor_tensor(fl[:, 0], fl[:, 0], fl[:, 1], ALU.max))
                code, below = maps[:, 1], maps[:, 3]
                link(nc.vector.tensor_tensor(fl[:, 1, :, 0:W - 1], code[:, :, 0:W - 1], code[:, :, 1:W], ALU.is_equal))
                link(nc.vector.tensor_tensor(fl[:, 0, :, 0:W - 1], fl[:, 0, :, 0:W - 1], fl[:, 1, :, 0:W - 1], ALU.max))
                link(nc.vector.tensor_reduce(mm[:, 0:1], fl[:, 0].rearrange("p i w -> p (i w)"), AX.X, ALU.max))
                link(nc.vector.tensor_tensor(fl[:, 0], code, below, ALU.is_equal))
                for a, b in ((0, 1), (1, 0)):
                    link(nc.vector.tensor_tensor(fl[:, 1, :, 0:W - 1], code[:, :, a:W - 1 + a], below[:, :, b:W - 1 + b], ALU.is_equal))
                    link(nc.vector.tensor_tensor(fl[:, 0, :, 0:W - 1], fl[:, 0, :, 0:W - 1], fl[:, 1, :, 0:W - 1], ALU.max))
                nc.vector.tensor_reduce(mm[:, 1:2], fl[:, 0].rearrange("p i w -> p (i w)"), AX.X, ALU.max).then_inc(sm_dve, 1)
                v.wait_ge(sm_pe, 5 * q + 3)
                link(nc.vector.tensor_copy(kcol[:].rearrange("p i h -> p (i h)"), ps[0:H, 7, 0:2 * H]))
                nc.vector.tensor_scalar(hot[:, H:H + 1], ps[0:H, 7, 2 * H:2 * H + 1], 1.0, None, ALU.min).then_inc(sm_dve, 1)
                v.wait_ge(sm_dve, 5 * q + 4)
                v.wait_ge(sm_pe, 5 * q + 4)
                link(nc.vector.tensor_copy(mm[:, 2:3], ps[0:H, 7, 0:1]))
                nc.vector.tensor_scalar(hot[:, 0:H], const("iota", H), mm[:, 2:3], hot[:, H:H + 1], ALU.is_equal, ALU.mult)\
                    .then_inc(sm_dve, 1)
                v.wait_ge(sm_pe, 5 * q + 5)
                link(nc.vector.tensor_copy(lst[:, 0:H], ps[0:1, 7, 0:H]))
                link(nc.vector.tensor_scalar(lst[:, H:H + 1], ps[0:1, 7, H:H + 1], 1.0, None, ALU.max))
                link(nc.vector.tensor_copy(lst[:, H + 1:H + 2], cum[:, 0:1]))
                link(nc.vector.tensor_copy(cum[:, 1:2], lst[:, H:H + 1]))
                nc.vector.tensor_tensor(cum[:, 0:1], cum[:, 0:1], cum[:, 1:2], ALU.add).then_inc(lst_ok, 1)
                v.wait_ge(lst_ok, q + 1)
                count = v.value_load(lst[0:1, H:H + 1], min_val=1, max_val=H)
                before = v.value_load(lst[0:1, H + 1:H + 2], min_val=0, max_val=H * PAIRS)
                v.wait_ge(enh_ok, BANDS * (q + 1))
                with v.Fori(0, count) as i:
                    h = v.value_load(lst[0:1, bass.ds(i, 1)], min_val=0, max_val=H - 1)
                    row = before + i
                    LINKS = 25
                    k_own = [0]

                    def rlink(ins):
                        k_own[0] += 1
                        ins.then_inc(r_own, 1)
                        v.wait_ge(r_own, row * LINKS + k_own[0])

                    v.wait_ge(r_act, row * 4 + 1)
                    v.wait_ge(lst_ok, q + 1)
                    nc.vector.tensor_tensor(grow[:, :, 1:1 + W], grow[:, :, 1:1 + W],
                                            const("rowmask")[:, bass.ds(h, 3)].unsqueeze(2).broadcast_to([P, 3, W]),
                                            ALU.mult).then_inc(r_dve, 1)
                    v.wait_ge(r_dve, row * 5 + 1)
                    center = grow[:, 1, 1:1 + W]
                    for dy in range(3):
                        win = windows(dy)
                        ins = nc.vector.tensor_tensor(prod[:, 3 * dy:3 * dy + 3, :], win,
                                                      center.unsqueeze(1).broadcast_to([P, 3, W]), ALU.mult)
                    ins.then_inc(r_dve, 1)
                    v.wait_ge(r_pe, row * 2 + 1)
                    dots = ps[0:H, 6, 0:2 * GEN]
                    rlink(nc.vector.tensor_copy(rn[:, 5].rearrange("p j i -> p (j i)"), dots))
                    nc.vector.tensor_scalar(rn[:, 0].rearrange("p j i -> p (j i)"), ps[0:H, 6, 2 * GEN:4 * GEN], 1e-24, None,
                                            ALU.max).then_inc(r_dve, 1)
                    v.wait_ge(r_act, row * 4 + 3)
                    rlink(nc.vector.tensor_scalar(rn[:, 2], rn[:, 2], LN_SHIFT ** 0.5, None, ALU.mult))
                    for _ in range(2):
                        rlink(nc.vector.tensor_tensor(rn[:, 3], rn[:, 2], rn[:, 2], ALU.mult))
                        rlink(nc.vector.tensor_tensor(rn[:, 3], rn[:, 3], rn[:, 0], ALU.mult))
                        rlink(nc.vector.tensor_scalar(rn[:, 3], rn[:, 3], -0.5, 1.5, ALU.mult, ALU.add))
                        rlink(nc.vector.tensor_tensor(rn[:, 2], rn[:, 2], rn[:, 3], ALU.mult))
                    rlink(nc.vector.tensor_tensor(rn[:, 4], rn[:, 5], rn[:, 2], ALU.mult))
                    nc.vector.tensor_tensor(sim[:].rearrange("p i j -> p j i"), rn[:, 4],
                                            rn[:, 2, GEN // 2, :].unsqueeze(1).broadcast_to([H, GEN, 2]), ALU.mult).then_inc(r_dve, 1)
                    v.wait_ge(r_dve, row * 5 + 4)
                    s_i = sim[:].unsqueeze(2).broadcast_to([H, 2, GEN, GEN])
                    s_j = sim[:].unsqueeze(3).broadcast_to([H, 2, GEN, GEN])
                    rlink(nc.vector.tensor_tensor(cmp[:, 0], s_i, s_j, ALU.is_gt))
                    rlink(nc.vector.tensor_tensor(cmp[:, 1], s_i, s_j, ALU.is_equal))
                    low = const("lower", H)
                    for im in range(2):
                        rlink(nc.vector.tensor_tensor(cmp[:, 1, im].rearrange("p a b -> p (a b)"),
                                                      cmp[:, 1, im].rearrange("p a b -> p (a b)"), low, ALU.mult))
                    rlink(nc.vector.tensor_tensor(cmp[:, 0], cmp[:, 0], cmp[:, 1], ALU.add))
                    rlink(nc.vector.tensor_reduce(sel[:, 1], cmp[:, 0], AX.X, ALU.add))
                    rlink(nc.vector.tensor_tensor(sel[:, 2], sel[:, 1],
                                                  kcol[:, :, bass.ds(h, 1)].broadcast_to([H, 2, GEN]), ALU.is_lt))
                    v.wait_ge(r_act, row * 4 + 4)
                    rlink(nc.vector.tensor_tensor(sel[:, 3], sel[:, 2], sel[:, 0], ALU.mult))
                    rlink(nc.vector.tensor_reduce(dent[:, 0], sel[:, 3], AX.X, ALU.add))
                    rlink(nc.vector.tensor_scalar(dent[:, 1], dent[:, 0], 1e-8, None, ALU.add))
                    rlink(nc.vector.reciprocal(dent[:, 0], dent[:, 1]))
                    rlink(nc.vector.tensor_tensor(sel[:, 4], sel[:, 3], dent[:, 0].unsqueeze(2).broadcast_to([H, 2, GEN]), ALU.mult))
                    nc.vector.tensor_copy(wrep[:].rearrange("p j i c -> p i j c"),
                                          sel[:, 4].unsqueeze(3).broadcast_to([H, 2, GEN, C])).then_inc(r_dve, 1)
                    v.wait_ge(r_pe, row * 2 + 2)
                    for dy in range(3):
                        win = windows(dy)
                        ins = nc.vector.tensor_tensor(prod[:, 3 * dy:3 * dy + 3, :],
                                                      ps[:, dy, 0:3 * W].rearrange("p (j w) -> p j w", w=W), win, ALU.mult)
                        if dy == 2:
                            rlink(ins)
                    rlink(nc.vector.tensor_reduce(agg[:, 0], prod[:].rearrange("p j w -> p w j"), AX.X, ALU.add))
                    assert k_own[0] == LINKS, k_own
                    v.wait_ge(lst_ok, q + 1)
                    nc.vector.tensor_scalar(agg[:, 1], center, sv[:, 14:15], beta, ALU.mult, ALU.add).then_inc(r_done2, 1)
                    v.wait_ge(r_done2, row + 1)
                    v.wait_ge(lst_ok, q + 1)
                    nc.vector.tensor_tensor(enh[:, bass.ds(h * W, W)], agg[:, 0], agg[:, 1], ALU.add).then_inc(r_done, 1)

        @block.tensor
        def _(pe):
            def group_mean(n, t, bank):
                pe.wait_ge(grp_in, n + 1)
                nc.tensor.matmul(ps[:, bank, 0:2], const("group"), t[:, 18:20], start=True, stop=True).then_inc(grp_out, 1)

            pe.wait_ge(c_in, 16)
            ident = const("ident")
            for t in range(TAPS):
                pe.wait_ge(ready, t + 1)
                nc.tensor.transpose(ps[:, 0, 0:P], conv_blk[:, :], ident).then_inc(setup_pe, 1)
            pe.wait_ge(w_in, 16 * 17)
            nc.tensor.transpose(ps[:, 1, 0:P], w1_raw[:, :, :].rearrange("p a c -> p (a c)"), ident).then_inc(setup_pe, 1)
            nc.tensor.transpose(ps[:, 2, 0:C], w2_raw[:, :], const("ident", C)[:, 0:C]).then_inc(setup_pe, 1)
            pe.wait_ge(ready, TAPS + 1)
            for q in ROUNDS:
                cur, last, nxt = 0 <= q < PAIRS, q >= 1, q + 1 < PAIRS

                def hidden(b, k):
                    for im in range(2):
                        ins = nc.tensor.matmul(ps[:, 4 + im, 0:CPX], w1_lhs[:, im, :],
                                               enh[:, bass.ds((b * 2 + k) * CPX, CPX)], start=True, stop=True)
                    ins.then_inc(h_ps, 1)

                def second(b, k):
                    chunk = CHUNKS * (q - 1) + b * 2 + k
                    pe.wait_ge(h_sb, AHEAD + chunk + 1)
                    pe.wait_ge(y_ok, AHEAD + chunk - 1)
                    for im in range(2):
                        ins = nc.tensor.matmul(ps[:, 6 + k, 0:CPX], w2_lhs[:, im, :], hid[:, im, :],
                                               start=(im == 0), stop=(im == 1))
                    ins.then_inc(f_ps, 1)

                def convolve(b, k):
                    below = b + 1 if not isinstance(b, int) or b < BANDS - 1 else b
                    pe.wait_ge(w_sb, AHEAD + BANDS * q + (below if k else b) + 1)
                    pe.wait_ge(x1_ok, AHEAD + CHUNKS * q + b * 2 + k - 1)
                    for t in range(TAPS):
                        ins = nc.tensor.matmul(ps[:, 2 + k, 0:CPX], conv_lhs[:, t, :],
                                               rows(wpad, (b * 2 + k) * ROWS + t // 3, ROWS, W, t % 3, WP),
                                               start=(t == 0), stop=(t == TAPS - 1))
                    ins.then_inc(conv_ps, 1)

                def step(b, n, u, first):
                    if last:
                        hidden(b, 0)
                    if cur and not first:
                        convolve(b - 1, 0)
                    if last:
                        second(b, 0)
                        hidden(b, 1)
                    if cur:
                        pe.wait_ge(wtok_ok, AHEAD + BANDS * q + b + 1)
                        pe.wait_ge(w_sb, AHEAD + BANDS * q + b)
                        for t in range(TILES):
                            ins = nc.tensor.transpose(ps[:, t // 4, (t % 4) * P:(t % 4 + 1) * P],
                                                      g_band[:, u, t * P:(t + 1) * P], ident)
                        ins.then_inc(w_ps, 1)
                    if last:
                        second(b, 1)
                    if cur and not first:
                        convolve(b - 1, 1)

                if q >= 0:
                    sweep(pe, step)
                if q == PAIRS:
                    continue
                if cur:
                    for k in range(2):
                        convolve(BANDS - 1, k)
                    group_mean(2 * q + 1, sv, 7)
                if nxt:
                    group_mean(2 * q + 2, sa, 0)
                if cur:
                    pe.wait_ge(norm_b, q + 1)
                    pe.wait_ge(y_ok, AHEAD + CHUNKS * q)
                with pe.Fori(0, BANDS // 2) as i:
                    for u in range(2):
                        band = BANDS * q + i * 2 + u
                        band_a = BANDS * (q + 1) + i * 2 + u
                        if nxt:
                            pe.wait_ge(g_ok, band_a + 1)
                            for k in range(2):
                                pe.wait_ge(z_sb, AHEAD + 2 * band_a + k - 1)
                                nc.tensor.matmul(ps[0:2 * OFFC, 4 + k, 0:CPX], off_lhs[:, :], g_band[:, u, k * CPX:(k + 1) * CPX],
                                                 start=True, stop=True).then_inc(z_ps, 1)
                            pe.wait_ge(tok_ok, AHEAD + band_a - 1)
                            for t in range(TILES):
                                ins = nc.tensor.transpose(ps[:, 6 * u + t // 4, (t % 4) * P:(t % 4 + 1) * P],
                                                          g_band[:, u, t * P:(t + 1) * P], ident)
                            ins.then_inc(t_ps, 1)
                        if cur:
                            pe.wait_ge(feat_ok, AHEAD + band + 1)
                            for k in range(2):
                                part = slice(k * CPX, (k + 1) * CPX)
                                pe.wait_ge(m_sb, AHEAD + 2 * band + k - 1)
                                nc.tensor.matmul(ps[0:32, 2 + k, 0:CPX], blk_r[:, :], d_band[:, u, part], start=True, stop=True)
                                for n in range(2):
                                    nc.tensor.matmul(ps[32:64, 2 + k, 0:CPX], hash_lhs[:, n, :], s_band[:, u, part],
                                                     start=(n == 0), stop=(n == 1))
                                nc.tensor.matmul(ps[64:96, 2 + k, 0:CPX], blk_bf[:, :], q_band[:, u, part], start=True, stop=True)\
                                    .then_inc(m_ps, 1)
                if nxt:
                    pe.wait_ge(tok_ok, AHEAD + BANDS * (q + 2))
                    pe.wait_ge(z_shift, 16 * TAPS * (q + 2))
                    for n in range(NT):
                        ins = nc.tensor.matmul(ps[:, 6, 4 * n:4 * n + 4], zbuf[64:64 + 2 * OFFC, n * P:(n + 1) * P],
                                               cst[64:64 + 2 * OFFC, _COLS["selz"][0]:_COLS["selz"][1]], start=True, stop=True)
                    ins.then_inc(off_ps, 1)
                if not cur:
                    continue
                pe.wait_ge(sm_dve, 5 * q + 1)
                nc.tensor.transpose(ps[0:4, 7, 0:H], mm[:, 0:4], const("ident", H)[:, 0:H]).then_inc(sm_pe, 1)
                pe.wait_ge(sm_dve, 5 * q + 2)
                nc.tensor.matmul(ps[0:H, 7, 0:4], ones4[:, :], diag[:, 0:4], start=True, stop=True).then_inc(sm_pe, 1)
                pe.wait_ge(sm_dve, 5 * q + 3)
                for im in range(2):
                    nc.tensor.transpose(ps[0:H, 7, im * H:(im + 1) * H], kmap[:, im, :], const("ident", H)[:, 0:H])
                nc.tensor.matmul(ps[0:H, 7, 2 * H:2 * H + 1], const("ident", H)[:, 0:H], mm[:, 0:1], start=True, stop=False, skip_group_check=True)
                nc.tensor.matmul(ps[0:H, 7, 2 * H:2 * H + 1], const("pair", H), mm[:, 1:2], start=False, stop=True, skip_group_check=True)\
                    .then_inc(sm_pe, 1)
                pe.wait_ge(sm_dve, 5 * q + 4)
                nc.tensor.matmul(ps[0:H, 7, 0:1], const("tri", H), hot[:, H:H + 1], start=True, stop=True).then_inc(sm_pe, 1)
                pe.wait_ge(sm_dve, 5 * q + 5)
                nc.tensor.matmul(ps[0:1, 7, 0:H], const("hval", H), hot[:, 0:H], start=True, stop=True)
                nc.tensor.matmul(ps[0:1, 7, H:H + 1], const("one", H), hot[:, H:H + 1], start=True, stop=True).then_inc(sm_pe, 1)
                pe.wait_ge(lst_ok, q + 1)
                count = pe.value_load(lst[0:1, H:H + 1], min_val=1, max_val=H)
                before = pe.value_load(lst[0:1, H + 1:H + 2], min_val=0, max_val=H * PAIRS)
                with pe.Fori(0, count) as i:
                    row = before + i
                    pe.wait_ge(r_act, row * 4 + 2)
                    pe.wait_ge(r_dve, row * 5 + 2)
                    pe.wait_ge(lst_ok, q + 1)
                    for j in range(GEN):
                        nc.tensor.matmul(ps[0:H, 6, 2 * j:2 * j + 2], prod[:, j, :], const("blk")[:, 0:2], start=True, stop=True)
                    for j in range(GEN):
                        ins = nc.tensor.matmul(ps[0:H, 6, 2 * GEN + 2 * j:2 * GEN + 2 * j + 2], gsq[:, j // 3, j % 3:j % 3 + W],
                                               const("blk")[:, 0:2], start=True, stop=True)
                    ins.then_inc(r_pe, 1)
                    pe.wait_ge(r_dve, row * 5 + 5)
                    pe.wait_ge(lst_ok, q + 1)
                    for j in range(GEN):
                        ins = nc.tensor.matmul(ps[:, j // 3, (j % 3) * W:(j % 3 + 1) * W], wrep[:, j].rearrange("p i c -> p (i c)"),
                                               const("ident", H)[:, 0:H], start=True, stop=True)
                    ins.then_inc(r_pe, 1)
                    pe.wait_ge(r_done, AHEAD + row + 1)




_INS = ["x", "L0_conv_w_off", "L0_conv_b_off", "L0_conv_w_conv", "L0_conv_b_conv", "L1_conv_gamma", "L1_conv_beta",
        "L1_conv_w1", "L1_conv_b1", "L1_conv_w2", "L1_conv_b2"]


def kernel(**inputs):
    import concourse.bacc as bacc
    from concourse.bass_utils import run_bass_kernel_spmd as run

    nc = bacc.Bacc("TRN2", target_bir_lowering=False, num_devices=1)
    arrays, args = {}, []
    for name in _INS:
        a = np.ascontiguousarray(inputs[name])
        if name == "x":
            a = a.reshape(PAIRS, P, PX)
        arrays[name] = a
        args.append(nc.dram_tensor(name, a.shape, F32, kind="ExternalInput").ap())
    arrays["consts"] = constants()
    args.append(nc.dram_tensor("consts", (P, N_CONST), F32, kind="ExternalInput").ap())
    args.append([nc.dram_tensor(f"table{q}", (2 * IMG_ENTRIES, ENTRY), F32).ap() for q in range(PAIRS)])
    args.append(nc.dram_tensor("sums", (3, 2, PX), F32).ap())
    out = nc.dram_tensor("y", (PAIRS, P, PX), F32, kind="ExternalOutput").ap()
    program(nc, *args, out)
    r = run(nc, [arrays], core_ids=[0])
    return r.results[0]["y"].reshape(N_IMG, C, H, W)
```

```python
import itertools
from contextlib import ExitStack

import numpy as np

import concourse.bass as bass
from concourse import mybir

F32 = mybir.dt.float32
BF16 = mybir.dt.bfloat16
F16 = mybir.dt.float16
I32 = mybir.dt.int32
ALU = mybir.AluOpType
ACT = mybir.ActivationFunctionType
AX = mybir.AxisListType

N_IMG, C, H, W = 8, 64, 80, 80
PAIRS = N_IMG // 2
PX = H * W
P = 2 * C
TAPS = 9
GEN = 9
HID = 2 * C
HP, WP = H + 2, W + 2
BAND = 8
BANDS = H // BAND
BPX = BAND * W
TILES = BPX // 128
NT = BANDS * TILES
ROWS = 4
CPX = ROWS * W
CHUNKS = H // ROWS
EPS = 1e-5
ENTRY = 2 * C
IMG_ENTRIES = W + PX
X0 = W + 1
SEG = 16
SPR = W // SEG
SLOTS = P // SEG
SHIFT_ROWS = H - 3 * BAND
NSEG = H * SPR + SLOTS
AHEAD = 64
MAGIC = 12582912.0
EARLY = 6
STAT = 400
PART = 4
LN_SHIFT = 2.0 ** 30

_COLS = {}
_n = 0
for _name, _w in [("ident", P), ("group", P), ("selz", 12), ("grid", NT * 2), ("blk", 32), ("hash_hi", 32),
                  ("hash_lo", 32), ("tri", H), ("pair", H), ("iota", NSEG), ("place", 2 * SPR), ("one", 1),
                  ("lower", GEN * GEN)]:
    _COLS[_name] = (_n, _n + _w)
    _n += _w
N_CONST = _n


def constants():
    c = np.zeros((P, N_CONST), np.float32)

    def put(name, a):
        c[:a.shape[0], _COLS[name][0]:_COLS[name][1]] = a

    put("ident", np.eye(P))
    k = np.arange(P)
    put("group", 0.5 * (k[:, None] // 2 == k[None, :] // 2))
    sel = np.zeros((P, 3, 4))
    for j in range(4):
        for dy in range(3):
            for part in (0, C):
                sel[part + PART * (3 * j + dy):part + PART * (3 * j + dy) + 3, dy, j] = 1.0
    sel = sel.reshape(P, 12)
    put("selz", sel)
    line = np.linspace(-1.0, 1.0, H, dtype=np.float32)
    pixel = np.arange(NT)[None, :] * P + k[:, None]
    put("grid", np.stack([line[pixel // W], line[pixel % W]], -1).reshape(P, NT * 2))
    blk = np.zeros((P, 32))
    blk[k, k // C] = 1.0
    put("blk", blk)
    code = np.random.RandomState(7).randint(1, 1 << 16, C)
    for name, part in (("hash_hi", code // 256 * 256), ("hash_lo", code % 256)):
        m = np.zeros((P, 32))
        m[k, k // C] = np.tile(part, 2)
        put(name, m)
    h = np.arange(H)
    put("tri", (h[:, None] < h[None, :]) * 1.0)
    put("pair", (h[:, None] == h[None, :]) * 1.0 + (h[:, None] + 1 == h[None, :]))
    put("iota", np.tile(np.arange(NSEG), (P, 1)))
    first = h[:, None] * W + np.arange(SPR) * SEG
    put("place", np.concatenate([first, first % W], 1))
    put("one", np.ones((P, 1)))
    j = np.arange(GEN)
    put("lower", np.tile((j[None, :] < j[:, None]).reshape(1, -1) * 1.0, (P, 1)))
    return c


class Chain:

    def __init__(self, eng, sem):
        self.eng, self.sem, self.base, self.n = eng, sem, 0, 0

    def link(self, ins):
        ins.then_inc(self.sem, 1)
        self.n += 1
        self.eng.wait_ge(self.sem, self.base + self.n)

    def loop(self, i, per):
        self.saved = (self.base, self.n)
        self.base, self.n = self.base + self.n + i * per, 0
        self.per = per

    def end(self, iterations):
        assert self.n == self.per, (self.n, self.per)
        self.base, self.n = self.saved
        self.n += iterations * self.per


def program(nc, x_d, w_off_d, b_off_d, w_conv_d, b_conv_d, gamma_d, beta_d, w1_d, b1_d, w2_d, b2_d, const_d, tables, sums, kmap_d, out_d):
    with ExitStack() as ctx:
        def sb(name, shape, dt=F32):
            return ctx.enter_context(nc.sbuf_tensor(name, shape, dt))

        def sem(name):
            return ctx.enter_context(nc.semaphore(name))

        cst = sb("cst", [P, N_CONST])

        def const(name, rows=P):
            a, b = _COLS[name]
            return cst[0:rows, a:b]

        off_lhs = sb("off_lhs", [P, P])
        selz_h = sb("selz_h", [P, 12], F16)
        b_off_raw = sb("b_off_raw", [P, 2 * TAPS])
        conv_lhs = sb("conv_lhs", [P, 2, TAPS, C], F16)
        conv_scale = sb("conv_scale", [P, 4])
        ident_h = sb("ident_h", [P, P], F16)
        zeros = sb("zeros", [P, 2 * WP], F16)
        w1_lhs = sb("w1_lhs", [P, 2, P])
        w2_lhs = sb("w2_lhs", [HID, C])
        vec = sb("vec", [P, 8])
        b_conv, gamma, beta, b1, b2 = (vec[:, k:k + 1] for k in range(5))
        grid_b = sb("grid_b", [P, NT, 2])
        hash_lhs = sb("hash_lhs", [P, 2, 32], BF16)
        blk_bf = sb("blk_bf", [P, 32], BF16)
        xb = [sb(f"xb{k}", [P, X0 + PX + 2 * W]) for k in range(2)]
        g_band = sb("g_band", [P, 2, BPX])
        d_band = sb("d_band", [P, 2, BPX])
        m_band = sb("m_band", [96, 2, BPX])
        zbuf = sb("zbuf", [P, HP * WP], F16)
        zmoved = sb("zmoved", [P, HP * W], F16)
        zero_rows = sb("zero_rows", [W, C])
        gat = sb("gat", [P, 2, TILES, 2, 2 * ENTRY])
        idx_i = sb("idx_i", [P, NT, 2], I32)
        idx_s = sb("idx_s", [P, 2, TILES * 2], I32)
        wgt = sb("wgt", [P, NT * 2, 4])
        tok = gat[:, 0].rearrange("p t i n -> p (t i n)")[:, 0:2 * BPX].rearrange("p (u t i c) -> p u t i c", u=2, t=TILES, i=2)
        wsplit = sb("wsplit", [P, 2, TILES, 2, 2, C], F16)
        wring = sb("wring", [P, 2, 2, BAND + 2, WP], F16)
        hsum = sb("hsum", [P, BAND * (W // 2)])
        xd = sb("xd", [P, 42, 42])
        up = sb("up", [P, 2, BAND, 42])
        s_band = sb("s_band", [P, 2, BPX], BF16)
        q_band = sb("q_band", [P, 2, BPX], BF16)
        enh = sb("enh", [P, PX])
        at = 0
        w_off_raw = enh[:, at:at + 2 * TAPS * TAPS]
        at += 2 * TAPS * TAPS
        conv_raw = enh[:, at:at + C * TAPS]
        at += C * TAPS
        conv_dup = enh[0:C, at:at + 2 * C * TAPS]
        at += 2 * C * TAPS
        w1_raw = enh[:, at:at + 2 * C].rearrange("p (a c) -> p a c", a=2)
        at += 2 * C
        w2_raw = enh[0:C, at:at + HID]
        hid = d_band[:].rearrange("p k (i n) -> p k i n", i=2)
        stats = sb("stats", [P, CHUNKS * 6])
        stats_a = sb("stats_a", [P, 16 * 6])
        sv = sb("sv", [P, 24])
        sa = sb("sa", [P, 24])
        pos = sb("pos", [P, NT * 2, 2])
        cell = sb("cell", [P, NT * 2, 2])
        tent = sb("tent", [P, 2, NT * 2, 2])
        ent = sb("ent", [P, NT * 2])
        maps = sb("maps", [H, 4, 2, W])
        fl = sb("fl", [H, 2, 2, W])
        kmap_px = sb("kmap_px", [H, W, 2])
        kmap = kmap_px[:].rearrange("p w i -> p i w")
        counts_b = sb("counts_b", [P, 2])
        seg = sb("seg", [H, 5, SPR])
        segi = sb("segi", [H, 2, 2, SPR])
        place = sb("place", [H, 2, SPR], F16)
        inside = sb("inside", [P, 4, SLOTS])
        mm = sb("mm", [H, 12])
        diag = sb("diag", [4, 8])
        ones4 = sb("ones4", [4, H])
        hot = sb("hot", [H, SPR, NSEG], F16)
        lst = sb("lst", [1, NSEG], I32)
        lst_f = sb("lst_f", [1, NSEG])
        runs = sb("runs", [1, 2], I32)
        cum = sb("cum", [1, 2])
        blk_r = sb("blk_r", [P, 32])
        patch = sb("patch", [P, SLOTS, 3, SEG + 2])
        prod = d_band[:].rearrange("p u n -> p (u n)")[:, 0:GEN * P].rearrange("p (j w) -> p j w", w=P)
        rn = sb("rn", [P, 6, GEN, 2])
        sim = sb("sim", [P, 2, GEN])
        cmp = sb("cmp", [P, 2, 2, GEN, GEN])
        sel = sb("sel", [P, 6, 2, GEN])
        dent = sb("dent", [P, 2, 2])
        wrep = sb("wrep", [P, GEN, 2, C])
        gsq = wrep[:].rearrange("p j i c -> p j (i c)")
        agg = sb("agg", [P, 2, P])

        def windows(dy):
            return bass.AP(patch[:].tensor, patch[:, 0, dy, 0:1].offset,
                           [list(patch[:].ap[0]), [1, 3], [3 * (SEG + 2), SLOTS], [1, SEG]])

        def split_pixels(t):
            return t.rearrange("p j (s w) -> p j s w", s=SLOTS)

        ps = ctx.enter_context(nc.psum_tensor("ps", [P, 8, 512], F32))
        flat = ps[:, :, :].rearrange("p b n -> p (b n)")

        c_in = sem("c_in"); w_in = sem("w_in")
        setup_dve = sem("setup_dve"); setup_pe = sem("setup_pe"); ready = sem("ready")
        pool_zero = sem("pool_zero"); table_zero = sem("table_zero")
        x_in = [sem(f"x_in{k}") for k in range(2)]
        x_early = [sem(f"x_early{k}") for k in range(2)]
        x_first = [sem(f"x_first{k}") for k in range(4)]
        dve = sem("dve"); act_own = sem("act_own")
        grp_in = sem("grp_in"); grp_out = sem("grp_out")
        ln_in = sem("ln_in"); ln_out = sem("ln_out")
        norm_a = sem("norm_a"); norm_b = sem("norm_b")
        g_ok = sem("g_ok")
        z_ps = sem("z_ps"); z_high = sem("z_high"); z_sb = sem("z_sb")
        t_ps = sem("t_ps"); tok_ok = sem("tok_ok")
        tok_out = [sem(f"tok_out{k}") for k in range(2)]
        z_shift = [sem(f"z_shift{k}") for k in range(2)]
        off_ps = sem("off_ps"); idx_ok = sem("idx_ok")
        staged = [sem(f"staged{k}") for k in range(2)]
        gat_in = [sem(f"gat_in{k}") for k in range(2)]
        corners_ok = sem("corners_ok"); high_ok = sem("high_ok"); wtok_ok = sem("wtok_ok")
        w_ps = sem("w_ps"); w_sb = sem("w_sb"); w_end = sem("w_end")
        biased = sem("biased"); conv_ps = sem("conv_ps"); x1_ok = sem("x1_ok")
        d_ok = sem("d_ok"); feat_ok = sem("feat_ok"); enh_ok = sem("enh_ok")
        m_ps = sem("m_ps"); m_sb = sem("m_sb"); m_out = sem("m_out")
        m_last = [sem(f"m_last{k}") for k in range(2)]
        maps_in = sem("maps_in")
        sm_pe = sem("sm_pe"); sm_dve = sem("sm_dve")
        lst_ok = sem("lst_ok"); kmap_ok = sem("kmap_ok"); kmap_out = sem("kmap_out"); counts_in = sem("counts_in")
        r_act = sem("r_act"); r_dve = sem("r_dve"); r_pe = sem("r_pe"); r_own = sem("r_own"); ln_r = sem("ln_r")
        own_term_ok = sem("own_term_ok"); r_placed = sem("r_placed"); r_done = sem("r_done")
        h_ps = sem("h_ps"); h_sb = sem("h_sb"); f_ps = sem("f_ps")
        y_ok = sem("y_ok"); y_out = sem("y_out")

        block = ctx.enter_context(nc.Block())

        ROUNDS = range(-1, PAIRS + 1)

        def shift_taps(eng, first, end):
            for dx in range(3):
                src = zbuf[dx:P - 16:PART, :].rearrange("p (h w) -> p h w", w=WP)[:, first:end, dx:dx + W]
                eng.dma_start(zmoved[dx:P - 16:PART, first * W:end * W].rearrange("p (h w) -> p h w", w=W), src)\
                   .then_inc(z_shift[0 if first == 0 else 1], 16)

        def sweep(eng, step, own=None, links=0):
            step(0, 0, 1)
            step(1, 1, 1)
            with eng.Fori(1, BANDS // 2 - 1) as i:
                if own:
                    own.loop(i - 1, 2 * links)
                step(i * 2, 0, i + 1)
                step(i * 2 + 1, 1, i + 1)
                if own:
                    own.end(BANDS // 2 - 2)
            step(BANDS - 2, 0, None)
            step(BANDS - 1, 1, None)

        def there(b):
            return not isinstance(b, int) or 0 <= b < BANDS

        def rows(buf, first, n=BAND, width=W, col=0, wide=W):
            return buf[:, bass.ds(first * wide, n * wide)].rearrange("p (r w) -> p r w", w=wide)[:, :, col:col + width]

        @block.sync
        def _(sp):
            sp.dma_start(cst[:, :], const_d).then_inc(c_in, 16)
            for k in range(4):
                sp.dma_start(xb[0][:, X0 + k * PX // 4:X0 + (k + 1) * PX // 4], x_d[0][:, k * PX // 4:(k + 1) * PX // 4])\
                  .then_inc(x_first[k], 16)
            for half in range(2):
                sp.dma_start(w_off_raw[half * C:(half + 1) * C, :].rearrange("c (o t) -> c o t", t=TAPS),
                             w_off_d.rearrange("o c a b -> c o (a b)")).then_inc(w_in, 16)
                sp.dma_start(conv_raw[half * C:(half + 1) * C, :],
                             w_conv_d.rearrange("o c a b -> o (c a b)")).then_inc(w_in, 16)
                sp.dma_start(w1_raw[:, half, :], w1_d).then_inc(w_in, 16)
                for k, v in enumerate((b_conv_d, gamma_d, beta_d, None, b2_d)):
                    if v is not None:
                        sp.dma_start(vec[half * C:(half + 1) * C, k:k + 1],
                                     v.rearrange("(c a) -> c a", a=1)).then_inc(w_in, 16)
            sp.dma_start(vec[:, 3:4], b1_d.rearrange("(c a) -> c a", a=1)).then_inc(w_in, 16)
            sp.dma_start(w2_raw[:, :], w2_d).then_inc(w_in, 16)
            sp.dma_start(b_off_raw[:, :], b_off_d.rearrange("(a n) -> a n", a=1).broadcast_to([P, 2 * TAPS])).then_inc(w_in, 16)
            sp.wait_ge(pool_zero, 10)
            for q in range(PAIRS):
                for im in range(2):
                    a = im * IMG_ENTRIES
                    sp.dma_start(tables[q][a:a + W, 0:C], zero_rows[:, :]).then_inc(table_zero, 16)
                    sp.dma_start(tables[q][a + PX:a + PX + W, C:2 * C], zero_rows[:, :]).then_inc(table_zero, 16)
            for q in ROUNDS:
                cur, last, nxt = 0 <= q < PAIRS, q >= 1, q + 1 < PAIRS
                if q == 0:
                    with sp.Fori(0, BANDS // 2) as i:
                        for u in range(2):
                            sp.wait_ge(w_sb, AHEAD + i * 2 + u)
                            sp.dma_start(xb[1][:, bass.ds((i * 2 + u) * BPX + X0, BPX)], x_d[1][:, bass.ds((i * 2 + u) * BPX, BPX)])\
                              .then_inc(x_in[1], 16)
                if last:
                    for a, b, arrived in ((0, EARLY // 2, x_early[(q + 1) % 2]), (EARLY // 2, BANDS // 2, x_in[(q + 1) % 2])):
                        with sp.Fori(a, b) as i:
                            for u in range(2):
                                at = (i * 2 + u) * BPX
                                sp.wait_ge(y_ok, AHEAD + CHUNKS * (q - 1) + (i * 2 + u) * 2 + 2)
                                sp.dma_start(out_d[q - 1][:, bass.ds(at, BPX)], enh[:, bass.ds(at, BPX)]).then_inc(y_out, 16)
                                if nxt:
                                    sp.dma_start(xb[(q + 1) % 2][:, bass.ds(at + X0, BPX)], x_d[q + 1][:, bass.ds(at, BPX)])\
                                      .then_inc(arrived, 16)
                if q == PAIRS:
                    continue
                with sp.Fori(0, BANDS // 2) as i:
                    for u in range(2):
                        if nxt:
                            sp.wait_ge(tok_ok, AHEAD + BANDS * (q + 1) + i * 2 + u + 1)
                            for im in range(2):
                                for dy in range(2):
                                    first = im * IMG_ENTRIES + W - dy * W
                                    sp.dma_start(tables[q + 1][bass.ds((i * 2 + u) * BPX + first, BPX), dy * C:(dy + 1) * C].rearrange(
                                        "(t p) c -> p t c", p=P), tok[:, u, :, im, :]).then_inc(tok_out[u], 16)
                    if cur and nxt:
                        sp.wait_ge(m_sb, AHEAD + CHUNKS * q + i * 4 + 4)
                        for k in (2, 1, 0):
                            sp.dma_start(sums[k][:, bass.ds(i * 2 * BPX, 2 * BPX)],
                                         m_band[32 * k:32 * k + 2].rearrange("p u n -> p (u n)")).then_inc(m_out, 16)
                    elif cur:
                        for u in range(2):
                            sp.wait_ge(m_sb, AHEAD + CHUNKS * q + (i * 2 + u) * 2 + 2)
                            for k in (2, 1, 0):
                                sp.dma_start(sums[k][:, bass.ds((i * 2 + u) * BPX, BPX)], m_band[32 * k:32 * k + 2, u])\
                                  .then_inc(m_last[u], 16)
                if nxt:
                    sp.wait_ge(z_sb, AHEAD + CHUNKS * (q + 2))
                    shift_taps(sp, SHIFT_ROWS + 2, HP)
                if cur:
                    if nxt:
                        sp.wait_ge(m_out, AHEAD + 16 * 3 * (BANDS // 2) * (q + 1))
                    else:
                        for u in range(2):
                            sp.wait_ge(m_last[u], AHEAD + 16 * 3 * (BANDS // 2))
                    for k, (kind, shift) in enumerate(((0, 0), (1, 0), (2, 0), (1, 1))):
                        sp.dma_start(maps[0:H - shift, k], sums[kind][:, shift * W:PX].rearrange("i (h w) -> h i w", w=W))\
                          .then_inc(maps_in, 16)
                    sp.wait_ge(kmap_ok, q + 1)
                    sp.dma_start(kmap_d.rearrange("(h w) i -> h (w i)", w=W), kmap_px[:].rearrange("p w i -> p (w i)")).then_inc(kmap_out, 16)
                    sp.wait_ge(lst_ok, q + 1)
                    runs_here = sp.value_load(runs[0:1, 0:1], min_val=1, max_val=NSEG // SLOTS)
                    before = sp.value_load(runs[0:1, 1:2], min_val=0, max_val=NSEG // SLOTS * PAIRS)
                    sp.wait_ge(kmap_out, 16 * (q + 1))
                    with sp.Fori(0, runs_here) as i:
                        for slot in range(SLOTS):
                            px = sp.value_load(lst[0:1, bass.ds(i * SLOTS + slot, 1)], min_val=0, max_val=PX - SEG)
                            if slot == 0:
                                sp.wait_ge(r_done, AHEAD + before + i)
                            sp.dma_start(counts_b[slot * SEG:(slot + 1) * SEG, :], kmap_d[bass.ds(px, SEG), :]).then_inc(counts_in, 16)
            sp.wait_ge(y_out, 16 * BANDS * PAIRS)

        @block.gpsimd
        def _(pool):
            for counter in (biased, d_ok, z_ps, t_ps, wtok_ok, z_sb, tok_ok, w_sb, w_ps, x1_ok, m_ps, m_sb, feat_ok, h_sb, f_ps, y_ok, r_done, conv_ps, *tok_out, m_out, *m_last):
                pool.sem_inc(counter, AHEAD)
            nc.gpsimd.memset(zero_rows[:, :], 0.0).then_inc(pool_zero, 1)
            nc.gpsimd.memset(zbuf[:, :], 0.0).then_inc(pool_zero, 1)
            nc.gpsimd.memset(zmoved[:, :], 0.0).then_inc(pool_zero, 1)
            nc.gpsimd.memset(wring[:], 0.0).then_inc(pool_zero, 1)
            nc.gpsimd.memset(zeros[:, :], 0.0).then_inc(pool_zero, 1)
            nc.gpsimd.memset(patch[:], 0.0).then_inc(pool_zero, 1)
            for k in range(2):
                nc.gpsimd.memset(xb[k][:, 0:X0], 0.0).then_inc(pool_zero, 1)
                nc.gpsimd.memset(xb[k][:, X0 + PX:], 0.0).then_inc(pool_zero, 1)
            for q in range(PAIRS):
                pool.wait_ge(z_sb, AHEAD + CHUNKS * q + SHIFT_ROWS // ROWS + 1)
                shift_taps(pool, 0, SHIFT_ROWS + 2)
                pool.wait_ge(idx_ok, q + 1)
                for k in range(2):
                    pool.wait_ge(tok_out[k], AHEAD + 16 * 4 * (BANDS // 2) * (q + 1))
                before = (BANDS // 2) * q
                with pool.Fori(before + 1, before + 1 + BANDS // 2) as copies:
                    i = copies - (before + 1)
                    for u in range(2):
                        pool.wait_ge(wtok_ok, AHEAD + BANDS * q + i * 2 + u - 1)
                        nc.gpsimd.tensor_copy(idx_s[:, u, :], idx_i[:, bass.ds((i * 2 + u) * TILES, TILES), :].rearrange(
                            "p t m -> p (t m)")).then_inc(staged[u], 1)
                        pool.wait_ge(table_zero, 16 * 4 * PAIRS)
                        pool.wait_ge(staged[u], copies)
                        for t in range(TILES):
                            for im in range(2):
                                pool.indirect_dma_start(gat[:, u, t, im, :], None, tables[q][:, :],
                                                        bass.IndirectOffsetOnAxis(ap=idx_s[:, u, 2 * t + im:2 * t + im + 1], axis=0))\
                                    .then_inc(gat_in[u], 16)

        @block.scalar
        def _(act):
            own = Chain(act, act_own)
            act.preload_act_table_set("natural_log_exp_and_others")

            turn = itertools.count(1)

            def rsqrt_seed(src, mid, dst):
                act.wait_ge(ln_in, next(turn))
                own.link(nc.scalar.activation(mid, src, ACT.Ln))
                nc.scalar.activation(dst, mid, ACT.Exp, scale=-0.5).then_inc(ln_out, 1)

            act.wait_ge(c_in, 16)
            def relu(p, b, k, bank):
                chunk = CHUNKS * p + b * 2 + k
                act.wait_ge(h_ps, chunk + 1)
                act.wait_ge(f_ps, AHEAD + chunk - 1)
                act.wait_ge(c_in, 16)
                for im in range(2):
                    ins = nc.scalar.activation(hid[:, k, im, :], ps[:, bank + im, 0:CPX], ACT.Relu, bias=b1)
                ins.then_inc(h_sb, 1)

            def high_part(p, b, u):
                act.wait_ge(corners_ok, BANDS * p + b + 1)
                act.wait_ge(w_ps, AHEAD + BANDS * p + b - 1)
                act.wait_ge(c_in, 16)
                nc.scalar.activation(wsplit[:, u, :, :, 0, :].rearrange("p t i c -> p (t i) c"),
                                     gat[:, u].rearrange("p t i (k c) -> p (t i) k c", k=2)[:, :, 0, 0:C],
                                     ACT.Copy).then_inc(high_ok, 1)
                xs = xb[p % 2][:, bass.ds(b * BPX + X0, BPX)]
                nc.scalar.activation(xs, xs, ACT.Identity, bias=b_conv).then_inc(biased, 1)

            def to_ring(p, b, u):
                act.wait_ge(w_ps, AHEAD + BANDS * p + b + 1)
                act.wait_ge(conv_ps, AHEAD + CHUNKS * p + 2 * b - 2)
                act.wait_ge(c_in, 16)
                image = flat[:, 0:BPX].bitcast(F16).rearrange("p (i h w) -> p i h w", i=2, w=W)
                top = isinstance(b, int) and b == 0
                nc.scalar.activation(wring[:, u, :, 0, 1:1 + W], zeros[:, 0:2 * W].rearrange("p (i w) -> p i w", i=2) if top
                                     else wring[:, 1 - u, :, BAND, 1:1 + W], ACT.Copy)
                if not top:
                    nc.scalar.activation(wring[:, 1 - u, :, BAND + 1, 1:1 + W], image[:, :, 0, :], ACT.Copy)
                for im in range(2):
                    ins = nc.scalar.activation(wring[:, u, im, 1:1 + BAND, 1:1 + W], image[:, im], ACT.Copy)
                ins.then_inc(w_sb, 1)

            def first_bands(p):
                for u in range(2):
                    high_part(p, u, u)
                    to_ring(p, u, u)

            for q in ROUNDS:
                cur, last, nxt = 0 <= q < PAIRS, q >= 1, q + 1 < PAIRS
                x = xb[q % 2]

                def step(f, u, n):
                    if cur and isinstance(f, int) and f == BANDS - 2:
                        act.wait_ge(conv_ps, AHEAD + CHUNKS * (q + 1) - 3)
                        act.wait_ge(c_in, 16)
                        nc.scalar.activation(wring[:, 1, :, BAND + 1, 1:1 + W], zeros[:, 0:2 * W].rearrange("p (i w) -> p i w", i=2),
                                             ACT.Copy).then_inc(w_end, 1)
                    if last:
                        relu(q - 1, f, 0, 4)
                    if cur and there(f + 2):
                        high_part(q, f + 2, u)
                    if last:
                        relu(q - 1, f, 1, 4 if cur else 0)
                    if cur and there(f + 2):
                        to_ring(q, f + 2, u)

                if q >= 0:
                    sweep(act, step)
                if q == PAIRS:
                    continue
                if cur:
                    rsqrt_seed(sv[:, 4:5], sv[:, 5:6], sv[:, 6:7])
                if nxt:
                    rsqrt_seed(sa[:, 4:5], sa[:, 5:6], sa[:, 6:7])
                if cur:
                    rsqrt_seed(sv[:, 11:12], sv[:, 5:6], sv[:, 12:13])
                if nxt:
                    act.wait_ge(norm_a, q + 2)
                if cur:
                    act.wait_ge(norm_b, q + 1)
                else:
                    act.wait_ge(pool_zero, 10)
                if q > 0:
                    act.wait_ge(y_out, 16 * BANDS * q)
                def next_normalised(i, u):
                    band = BANDS * (q + 1) + i * 2 + u
                    act.wait_ge(z_ps, AHEAD + 2 * (band - 1))
                    act.wait_ge(t_ps, AHEAD + band - 1)
                    act.wait_ge(c_in, 16)
                    nc.scalar.activation(g_band[:, u, :], xb[(q + 1) % 2][:, bass.ds((i * 2 + u) * BPX + X0, BPX)], ACT.Identity,
                                         bias=sa[:, 8:9], scale=sa[:, 7:8]).then_inc(g_ok, 1)

                def partial_sums(i, u):
                    for k in range(2):
                        act.wait_ge(z_ps, AHEAD + 2 * (BANDS * (q + 1) + i * 2 + u) + k + 1)
                        act.wait_ge(c_in, 16)
                        nc.scalar.activation(rows(zbuf, (i * 2 + u) * BAND + k * ROWS + 1, ROWS, W, 1, WP),
                                             ps[:, 4 + k, 0:CPX].rearrange("p (r w) -> p r w", w=W), ACT.Copy).then_inc(z_high, 1)

                def features(i, u):
                    src = x[:, bass.ds((i * 2 + u) * BPX + X0, BPX)]
                    act.wait_ge(m_ps, AHEAD + 2 * (BANDS * q + i * 2 + u - 1))
                    act.wait_ge(c_in, 16)
                    nc.scalar.activation(s_band[:, u, :], src, ACT.Sign, bias=sv[:, 8:9], scale=sv[:, 7:8])
                    nc.scalar.activation(q_band[:, u, :], src, ACT.Square, bias=sv[:, 8:9], scale=sv[:, 7:8]).then_inc(feat_ok, 1)

                def enhance(i, u):
                    at = (i * 2 + u) * BPX
                    nc.scalar.activation(enh[:, bass.ds(at, BPX)], x[:, bass.ds(at + X0, BPX)], ACT.Identity,
                                         bias=sv[:, 16:17], scale=sv[:, 15:16]).then_inc(enh_ok, 1)

                def pixel_sums(i, u):
                    if nxt:
                        act.wait_ge(m_out, AHEAD + 16 * 3 * ((BANDS // 2) * q + i))
                    else:
                        act.wait_ge(m_last[u], AHEAD + 16 * 3 * i)
                    for k in range(2):
                        act.wait_ge(m_ps, AHEAD + 2 * (BANDS * q + i * 2 + u) + k + 1)
                        act.wait_ge(c_in, 16)
                        nc.scalar.activation(m_band[:, u, k * CPX:(k + 1) * CPX], ps[0:96, 2 + k, 0:CPX],
                                             ACT.Copy).then_inc(m_sb, 1)

                with act.Fori(0, BANDS // 2) as i:
                    if nxt:
                        for u in range(2):
                            next_normalised(i, u)
                            if cur:
                                features(i, u)
                            partial_sums(i, u)
                            if cur:
                                enhance(i, u)
                                pixel_sums(i, u)
                    else:
                        features(i, 0)
                        enhance(i, 0)
                        features(i, 1)
                        pixel_sums(i, 0)
                        enhance(i, 1)
                        pixel_sums(i, 1)
                if nxt:
                    first_bands(q + 1)
                if not cur:
                    continue
                act.wait_ge(lst_ok, q + 1)
                runs_here = act.value_load(runs[0:1, 0:1], min_val=1, max_val=NSEG // SLOTS)
                before = act.value_load(runs[0:1, 1:2], min_val=0, max_val=NSEG // SLOTS * PAIRS)
                with act.Fori(0, runs_here) as i:
                    for slot in range(SLOTS):
                        px = act.value_load(lst[0:1, bass.ds(i * SLOTS + slot, 1)], min_val=0, max_val=PX - SEG)
                        if slot == 0:
                            act.wait_ge(r_done, AHEAD + before + i)
                        act.wait_ge(lst_ok, q + 1)
                        ins = nc.scalar.activation(patch[:, slot], x[:, bass.ds(px + X0 - W - 1, 3 * W)].rearrange(
                            "p (r w) -> p r w", w=W)[:, :, 0:SEG + 2], ACT.Identity, bias=sv[:, 8:9], scale=sv[:, 7:8])
                    ins.then_inc(r_act, 1)
                    act.wait_ge(r_dve, (before + i) * 5 + 1)
                    for dy in range(3):
                        ins = nc.scalar.activation(split_pixels(gsq[:, 3 * dy:3 * dy + 3]), windows(dy), ACT.Square)
                    ins.then_inc(r_act, 1)
                    act.wait_ge(r_dve, (before + i) * 5 + 3)
                    nc.scalar.activation(rn[:, 1], rn[:, 0], ACT.Ln, scale=LN_SHIFT).then_inc(ln_r, 1)
                    act.wait_ge(ln_r, before + i + 1)
                    nc.scalar.activation(rn[:, 2], rn[:, 1], ACT.Exp, scale=-0.5).then_inc(r_act, 1)
                    act.wait_ge(r_dve, (before + i) * 5 + 4)
                    nc.scalar.activation(sel[:, 0], sim[:, :, :], ACT.Exp).then_inc(r_act, 1)

        @block.vector
        def _(v):
            own = Chain(v, dve)

            def link(ins):
                own.link(ins)

            for t in (off_lhs, w1_lhs):
                nc.vector.memset(t[:], 0.0).then_inc(setup_dve, 1)
            nc.vector.memset(ones4[:], 1.0).then_inc(setup_dve, 1)
            nc.vector.memset(cum[:], 0.0).then_inc(setup_dve, 1)
            nc.vector.memset(maps[:], -1.0e9).then_inc(setup_dve, 1)
            v.wait_ge(setup_dve, 5)
            for n in range(16):
                if n % 4 == 0:
                    v.wait_ge(x_first[n // 4], 16)
                nc.vector.bn_stats(stats_a[:, n * 6:(n + 1) * 6], xb[0][:, X0 + n * STAT:X0 + (n + 1) * STAT])
            v.wait_ge(c_in, 16)
            v.wait_ge(w_in, 16 * 17)
            raw = w_off_raw[:, :].rearrange("p (o k t) -> p o t k", o=2, t=TAPS)
            for im in range(2):
                a = slice(im * C, (im + 1) * C)
                for part in range(2):
                    columns = off_lhs[a, part * C:part * C + 12 * PART].rearrange("p (j a b) -> p j a b", j=4, b=PART)
                    for o in range(2):
                        nc.vector.tensor_reduce(columns[:, 2 * im + o, :, 0:3], raw[a, o].rearrange("p (a b) k -> p a b k", b=3),
                                                AX.X, ALU.add)
            link(nc.vector.tensor_reduce(sv[:, 20:22], b_off_raw[:, :].rearrange("p (o k) -> p o k", o=2), AX.X, ALU.add))
            for o in range(2):
                link(nc.vector.tensor_scalar(sv[:, 22 + o:23 + o], sv[:, 20 + o:21 + o], 1.0 / TAPS, None, ALU.mult))
                link(nc.vector.tensor_scalar(grid_b[:, :, o], const("grid").rearrange("p (t o) -> p t o", o=2)[:, :, o],
                                             sv[:, 22 + o:23 + o], None, ALU.add))
            link(nc.vector.tensor_copy(hash_lhs[:, 0, :], const("hash_hi")))
            link(nc.vector.tensor_copy(hash_lhs[:, 1, :], const("hash_lo")))
            link(nc.vector.tensor_copy(blk_bf[:, :], const("blk")))
            link(nc.vector.tensor_copy(selz_h[:, :], const("selz")))
            link(nc.vector.tensor_copy(place[:].rearrange("p a n -> p (a n)"), const("place", H)))
            nc.vector.tensor_copy(sv[:, 21:22], sv[:, 20:21]).then_inc(ready, 1)

            def late_setup():
                link(nc.vector.tensor_copy(ident_h[:, :], const("ident")))
                link(nc.vector.tensor_reduce(conv_scale[:, 0:1], conv_raw[:, :], AX.X, ALU.max))
                link(nc.vector.tensor_reduce(conv_scale[:, 1:2], conv_raw[:, :], AX.X, ALU.min))
                link(nc.vector.scalar_tensor_tensor(out=conv_scale[:, 0:1], in0=conv_scale[:, 1:2], scalar=-1.0, in1=conv_scale[:, 0:1],
                                                    op0=ALU.mult, op1=ALU.max))
                link(nc.vector.tensor_scalar(conv_scale[:, 2:3], conv_scale[:, 0:1], 1e-30, 1.0 / 256, ALU.max, ALU.mult))
                link(nc.vector.reciprocal(conv_scale[:, 3:4], conv_scale[:, 2:3]))
                dup = conv_dup[:, :].rearrange("p (t a c) -> p t a c", t=TAPS, a=2)
                for a in range(2):
                    ins = nc.vector.tensor_scalar(dup[:, :, a, :], conv_raw[0:C, :].rearrange("p (c t) -> p t c", t=TAPS),
                                                  conv_scale[0:C, 3:4], None, ALU.mult)
                ins.then_inc(ready, 1)
                v.wait_ge(setup_pe, 3)
                turned = flat[:, 0:TAPS * C]
                link(nc.vector.tensor_copy(conv_lhs[:, 0].rearrange("p t c -> p (t c)"), turned))
                link(nc.vector.tensor_tensor(conv_lhs[:, 1].rearrange("p t c -> p (t c)"), turned,
                                             conv_lhs[:, 0].rearrange("p t c -> p (t c)"), ALU.subtract))
                for im in range(2):
                    a = slice(im * C, (im + 1) * C)
                    link(nc.vector.tensor_copy(w1_lhs[a, im, :], ps[a, 3, 0:P]))
                nc.vector.tensor_copy(w2_lhs[:, :], ps[:, 2, 0:C]).then_inc(ready, 1)

            turn = itertools.count(1)

            def variance(t, bank, n):
                v.wait_ge(grp_out, n + 1)
                link(nc.vector.tensor_copy(t[:, 2:4], ps[:, bank, 0:2]))
                link(nc.vector.tensor_tensor(t[:, 9:10], t[:, 0:1], t[:, 2:3], ALU.subtract))
                link(nc.vector.tensor_tensor(t[:, 9:10], t[:, 9:10], t[:, 9:10], ALU.mult))
                link(nc.vector.tensor_tensor(t[:, 10:11], t[:, 9:10], t[:, 3:4], ALU.add))
                nc.vector.tensor_scalar(t[:, 4:5], t[:, 10:11], EPS, None, ALU.add).then_inc(ln_in, 1)

            def refine(t, val, seed, dst):
                v.wait_ge(ln_out, next(turn))
                link(nc.vector.tensor_tensor(t[:, 9:10], seed, seed, ALU.mult))
                link(nc.vector.tensor_tensor(t[:, 9:10], t[:, 9:10], val, ALU.mult))
                link(nc.vector.tensor_scalar(t[:, 9:10], t[:, 9:10], -0.5, 1.5, ALU.mult, ALU.add))
                link(nc.vector.tensor_tensor(dst, t[:, 9:10], seed, ALU.mult))

            def minus_mean(t):
                return nc.vector.scalar_tensor_tensor(out=t[:, 8:9], in0=t[:, 2:3], scalar=-1.0, in1=t[:, 7:8],
                                                      op0=ALU.mult, op1=ALU.mult)

            def corners(p, b, u, n):
                v.wait_ge(gat_in[u], 16 * 2 * TILES * ((BANDS // 2) * p + n + 1))
                g = gat[:, u].rearrange("p t i (k c) -> p (t i k) c", c=C)
                wb = wgt[:, bass.ds(b * 2 * TILES, 2 * TILES), :].rearrange("p t k -> p (t k)")\
                    .unsqueeze(2).broadcast_to([P, 8 * TILES, C])
                link(nc.vector.tensor_tensor(g, g, wb, ALU.mult))
                g2 = gat[:, u].rearrange("p t i (k c) -> p (t i) k c", k=2)
                link(nc.vector.tensor_tensor(g2[:, :, 0, :], g2[:, :, 0, :], g2[:, :, 1, :], ALU.add))
                warped = g2[:, :, 0, 0:C]
                nc.vector.tensor_tensor(warped, warped, g2[:, :, 0, C:2 * C], ALU.add).then_inc(corners_ok, 1)

            def low_part(p, b, u):
                v.wait_ge(high_ok, BANDS * p + b + 1)
                split = wsplit[:, u].rearrange("p t i a c -> p (t i) a c")
                warped = gat[:, u].rearrange("p t i (k c) -> p (t i) k c", k=2)[:, :, 0, 0:C]
                nc.vector.tensor_tensor(split[:, :, 1, :], warped, split[:, :, 0, :], ALU.subtract).then_inc(wtok_ok, 1)

            def residual(p, b, k):
                chunk = b * 2 + k
                v.wait_ge(conv_ps, AHEAD + CHUNKS * p + chunk + 1)
                xs = xb[p % 2][:, bass.ds(chunk * CPX + X0, CPX)]
                v.wait_ge(biased, AHEAD + BANDS * p + b + 1)
                nc.vector.scalar_tensor_tensor(out=xs, in0=ps[:, 2 + k, 0:CPX], scalar=conv_scale[:, 2:3], in1=xs,
                                               op0=ALU.mult, op1=ALU.add).then_inc(x1_ok, 1)

            def measure(p, b):
                x = xb[p % 2]
                v.wait_ge(x1_ok, AHEAD + CHUNKS * p + b * 2 + 2)
                for k in range(2):
                    nc.vector.bn_stats(stats[:, bass.ds((b * 2 + k) * 6, 6)], x[:, bass.ds((b * 2 + k) * CPX + X0, CPX)])
                img = x[:, bass.ds(b * BPX + X0, BPX)].rearrange("p (n b) -> p n b", b=2)
                link(nc.vector.tensor_tensor(hsum[:, :], img[:, :, 0], img[:, :, 1], ALU.add))
                hs = hsum[:, :].rearrange("p (h a w) -> p h a w", a=2, w=W // 2)
                link(nc.vector.tensor_tensor(xd[:, bass.ds(b * (BAND // 2) + 1, BAND // 2), 1:41],
                                             hs[:, :, 0, :], hs[:, :, 1, :], ALU.add))

            def output(p, b, k):
                chunk = b * 2 + k
                v.wait_ge(f_ps, AHEAD + CHUNKS * p + chunk + 1)
                y = enh[:, bass.ds(chunk * CPX, CPX)]
                link(nc.vector.scalar_tensor_tensor(out=y, in0=ps[:, 6 + k, 0:CPX], scalar=b2, in1=y,
                                                    op0=ALU.add, op1=ALU.add))
                nc.vector.tensor_tensor(y, y, xb[p % 2][:, bass.ds(chunk * CPX + X0, CPX)], ALU.add).then_inc(y_ok, 1)

            for q in ROUNDS:
                cur, last, nxt = 0 <= q < PAIRS, q >= 1, q + 1 < PAIRS
                x, other = xb[q % 2], xb[(q + 1) % 2]

                def next_stats(a, b):
                    for n in range(a, b):
                        nc.vector.bn_stats(stats_a[:, n * 6:(n + 1) * 6], other[:, X0 + n * STAT:X0 + (n + 1) * STAT])

                def step(f, u, n):
                    if cur and there(f + 2):
                        corners(q, f + 2, u, n)
                    elif nxt:
                        if f == BANDS - 2:
                            v.wait_ge(*((x_in[1], 16 * BANDS) if q == 0 else (x_early[(q + 1) % 2], 16 * EARLY)))
                        pieces = 16 if q == 0 else EARLY * BPX // STAT
                        next_stats(*((0, pieces // 2) if f == BANDS - 2 else (pieces // 2, pieces)))
                    if last and not (isinstance(f, int) and f == 0):
                        output(q - 1, f - 1, 1)
                    if cur:
                        residual(q, f, 1)
                        measure(q, f)
                    if cur and there(f + 2):
                        low_part(q, f + 2, u)
                    if last:
                        output(q - 1, f, 0)
                    if cur and there(f + 1):
                        residual(q, f + 1, 0)

                if q >= 0:
                    sweep(v, step, own, 4 * cur + 2 * last)
                if last:
                    output(q - 1, BANDS - 1, 1)
                if q == PAIRS:
                    continue
                if cur:
                    link(nc.vector.bn_aggr(sv[:, 0:2], stats[:, :]))
                    nc.vector.tensor_copy(sv[:, 18:20], sv[:, 0:2]).then_inc(grp_in, 1)
                    link(nc.vector.tensor_copy(xd[:, 1:41, 0:42:41], xd[:, 1:41, 1:41:39]))
                    link(nc.vector.tensor_copy(xd[:, 0:42:41, :], xd[:, 1:41:39, :]))
                if nxt:
                    if q >= 1:
                        v.wait_ge(x_in[(q + 1) % 2], 16 * (BANDS - EARLY) + 16 * BANDS * (q == 2))
                        next_stats(EARLY * BPX // STAT, 16)
                    link(nc.vector.memset(sa[:, 17:18], 0.0))
                    link(nc.vector.bn_aggr(sa[:, 0:2], stats_a[:, :]))
                    nc.vector.tensor_copy(sa[:, 18:20], sa[:, 0:2]).then_inc(grp_in, 1)
                if cur:
                    variance(sv, 7, 2 * q + 1)
                if nxt:
                    variance(sa, 0, 2 * q + 2)
                if cur:
                    refine(sv, sv[:, 4:5], sv[:, 6:7], sv[:, 7:8])
                    link(minus_mean(sv))
                    link(nc.vector.tensor_tensor(sv[:, 11:12], sv[:, 7:8], sv[:, 7:8], ALU.mult))
                    link(nc.vector.tensor_tensor(sv[:, 11:12], sv[:, 11:12], sv[:, 10:11], ALU.mult))
                    nc.vector.tensor_scalar(sv[:, 11:12], sv[:, 11:12], EPS, None, ALU.add).then_inc(ln_in, 1)
                if nxt:
                    refine(sa, sa[:, 4:5], sa[:, 6:7], sa[:, 7:8])
                    minus_mean(sa).then_inc(norm_a, 1)
                if cur:
                    refine(sv, sv[:, 11:12], sv[:, 12:13], sv[:, 13:14])
                    link(nc.vector.tensor_tensor(sv[:, 14:15], sv[:, 13:14], gamma, ALU.mult))
                    link(nc.vector.scalar_tensor_tensor(out=sv[:, 15:16], in0=sv[:, 14:15], scalar=1.0, in1=sv[:, 7:8],
                                                        op0=ALU.add, op1=ALU.mult))
                    link(nc.vector.tensor_tensor(sv[:, 16:17], sv[:, 2:3], sv[:, 15:16], ALU.mult))
                    link(nc.vector.tensor_tensor(sv[:, 16:17], beta, sv[:, 16:17], ALU.subtract))
                    nc.vector.tensor_scalar(blk_r[:, :], const("blk"), sv[:, 7:8], None, ALU.mult).then_inc(norm_b, 1)
                    v.wait_ge(wtok_ok, AHEAD + BANDS * (q + 1))
                with v.Fori(0, BANDS // 2) as i:
                    if cur:
                        own.loop(i, 10)
                    for u in range(2):
                        band = BANDS * q + i * 2 + u
                        if cur:
                            upr = up[:, u].rearrange("p (h a) w -> p h a w", a=2)
                            half = (i * 2 + u) * (BAND // 2)
                            for a in range(2):
                                link(nc.vector.scalar_tensor_tensor(
                                    out=upr[:, :, a, :], in0=xd[:, bass.ds(half + 1, BAND // 2), :], scalar=3.0,
                                    in1=xd[:, bass.ds(half + 2 * a, BAND // 2), :], op0=ALU.mult, op1=ALU.add))
                            v.wait_ge(m_ps, AHEAD + 2 * (band - 1))
                            db = d_band[:, u, :].rearrange("p (h w a) -> p h w a", w=W // 2, a=2)
                            for a in range(2):
                                link(nc.vector.scalar_tensor_tensor(out=db[:, :, :, a], in0=up[:, u, :, 1:41], scalar=3.0,
                                                                    in1=up[:, u, :, 2 * a:2 * a + 40], op0=ALU.mult, op1=ALU.add))
                            link(nc.vector.scalar_tensor_tensor(out=d_band[:, u, :], in0=d_band[:, u, :], scalar=-1.0 / 64,
                                                                in1=x[:, bass.ds((i * 2 + u) * BPX + X0, BPX)], op0=ALU.mult,
                                                                op1=ALU.add))
                            nc.vector.scalar_tensor_tensor(out=d_band[:, u, :], in0=d_band[:, u, :], scalar=-1.0, in1=d_band[:, u, :],
                                                           op0=ALU.mult, op1=ALU.max).then_inc(d_ok, 1)
                        if nxt:
                            v.wait_ge(t_ps, AHEAD + BANDS * (q + 1) + i * 2 + u + 1)
                            v.wait_ge(tok_out[u], AHEAD + 16 * 4 * ((BANDS // 2) * (q + 1) + i))
                            nc.vector.tensor_copy(tok[:, u].rearrange("p t i c -> p (t i c)"),
                                                  flat[:, 6 * u * 512:6 * u * 512 + BPX]).then_inc(tok_ok, 1)
                            for k in range(2):
                                v.wait_ge(z_high, 2 * (BANDS * (q + 1) + i * 2 + u) + k + 1)
                                low = rows(zbuf[C:P], (i * 2 + u) * BAND + k * ROWS + 1, ROWS, W, 1, WP)
                                nc.vector.tensor_tensor(low, ps[C:P, 4 + k, 0:CPX].rearrange("p (r w) -> p r w", w=W), low,
                                                        ALU.subtract).then_inc(z_sb, 1)
                    if cur:
                        own.end(BANDS // 2)
                if not cur:
                    late_setup()
                if nxt:
                    v.wait_ge(off_ps, q + 2)
                    for im in range(2):
                        link(nc.vector.scalar_tensor_tensor(
                            out=pos[:, :, :].rearrange("p (t i) o -> p t i o", i=2)[:, :, im],
                            in0=ps[:, 6, 0:4 * NT].rearrange("p (t i o) -> p t i o", i=2, o=2)[:, :, im], scalar=1.0 / TAPS,
                            in1=grid_b[:, :, :], op0=ALU.mult, op1=ALU.add))
                    link(nc.vector.tensor_scalar(pos[:], pos[:], 1.0, 0.5 * (W - 1), ALU.add, ALU.mult))
                    link(nc.vector.tensor_scalar(cell[:], pos[:], -0.5, 0.0, ALU.add, ALU.max))
                    link(nc.vector.tensor_scalar(cell[:], cell[:], float(W - 2), MAGIC, ALU.min, ALU.add))
                    link(nc.vector.tensor_scalar(cell[:], cell[:], MAGIC, None, ALU.subtract))
                    link(nc.vector.tensor_tensor(tent[:, 0], pos[:], cell[:], ALU.subtract))
                    link(nc.vector.tensor_scalar(tent[:, 1], tent[:, 0], 1.0, None, ALU.subtract))
                    tf = tent[:].rearrange("p a t o -> p (a t o)")
                    link(nc.vector.scalar_tensor_tensor(out=tf, in0=tf, scalar=-1.0, in1=tf, op0=ALU.mult, op1=ALU.min))
                    link(nc.vector.tensor_scalar(tent[:], tent[:], 1.0, 0.0, ALU.add, ALU.max))
                    link(nc.vector.tensor_scalar(ent[:], cell[:, :, 1], float(W), None, ALU.mult))
                    link(nc.vector.tensor_tensor(ent[:], ent[:], cell[:, :, 0], ALU.add))
                    for im in range(2):
                        link(nc.vector.tensor_scalar(idx_i[:, :, im], ent[:].rearrange("p (t i) -> p t i", i=2)[:, :, im],
                                                     float(im * IMG_ENTRIES + W), None, ALU.add))
                    for dx in range(2):
                        for dy in range(2):
                            ins = nc.vector.tensor_tensor(wgt[:, :, 2 * dx + dy], tent[:, dx, :, 0], tent[:, dy, :, 1], ALU.mult)
                            if dx + dy < 2:
                                link(ins)
                    ins.then_inc(idx_ok, 1)
                    v.wait_ge(idx_ok, q + 2)
                if not cur:
                    for u in range(2):
                        corners(q + 1, u, u, 0)
                        low_part(q + 1, u, u)
                    residual(q + 1, 0, 0)
                    continue
                v.wait_ge(maps_in, 16 * 4 * (q + 1))
                df = maps[:, 0]
                link(nc.vector.tensor_reduce(mm[:, 0:2], df, AX.X, ALU.max))
                link(nc.vector.tensor_reduce(mm[:, 4:6], df, AX.X, ALU.min))
                nc.vector.tensor_scalar(mm[:, 2:4], mm[:, 4:6], -1.0, None, ALU.mult).then_inc(sm_dve, 1)
                v.wait_ge(sm_pe, 5 * q + 1)
                link(nc.vector.tensor_reduce(diag[:, 4:5], ps[0:4, 7, 0:H], AX.X, ALU.max))
                nc.vector.tensor_scalar(diag[:, 0:4], const("ident", 4)[:, 0:4], diag[:, 4:5], None, ALU.mult).then_inc(sm_dve, 1)
                v.wait_ge(sm_pe, 5 * q + 2)
                link(nc.vector.tensor_copy(mm[:, 6:10], ps[0:H, 7, 0:4]))
                link(nc.vector.tensor_tensor(mm[:, 10:12], mm[:, 6:8], mm[:, 8:10], ALU.add))
                link(nc.vector.tensor_scalar(mm[:, 10:12], mm[:, 10:12], 1e-8, None, ALU.add))
                link(nc.vector.reciprocal(mm[:, 10:12], mm[:, 10:12]))
                for im in range(2):
                    link(nc.vector.tensor_scalar(fl[:, 0, im], df[:, im], mm[:, 8 + im:9 + im], mm[:, 10 + im:11 + im],
                                                 ALU.add, ALU.mult))
                link(nc.vector.tensor_tensor(fl[:, 0], fl[:, 0], fl[:, 0], ALU.mult))
                link(nc.vector.tensor_tensor(fl[:, 0], fl[:, 0], fl[:, 0], ALU.mult))
                link(nc.vector.tensor_scalar(kmap[:], fl[:, 0], -0.9, 15.0 / (1.0 - 0.9 + 1e-8), ALU.add, ALU.mult))
                link(nc.vector.tensor_scalar(kmap[:], kmap[:], MAGIC, MAGIC, ALU.add, ALU.subtract))
                link(nc.vector.tensor_scalar(kmap[:], kmap[:], 0.0, None, ALU.max))
                link(nc.vector.tensor_scalar(fl[:, 0], fl[:, 0], 0.9, None, ALU.is_gt))
                link(nc.vector.tensor_tensor(kmap[:], kmap[:], fl[:, 0], ALU.mult))
                nc.vector.tensor_scalar(kmap[:], kmap[:], 1.0, float(GEN), ALU.add, ALU.min).then_inc(kmap_ok, 1)
                v.wait_ge(kmap_ok, q + 1)
                link(nc.vector.tensor_scalar(fl[:, 0], kmap[:], 1.0, None, ALU.is_gt))
                link(nc.vector.tensor_scalar(fl[:, 1], maps[:, 2], 1e-20, None, ALU.is_lt))
                link(nc.vector.tensor_tensor(fl[:, 0], fl[:, 0], fl[:, 1], ALU.max))
                code, below = maps[:, 1], maps[:, 3]

                def mark_both():
                    for a in range(2):
                        link(nc.vector.tensor_tensor(fl[:, 0, :, a:W - 1 + a], fl[:, 0, :, a:W - 1 + a], fl[:, 1, :, 0:W - 1], ALU.max))

                def mark_segments(n):
                    link(nc.vector.tensor_reduce(segi[:, n], fl[:, 0].rearrange("p i (s w) -> p i s w", w=SEG), AX.X, ALU.max))
                    return nc.vector.tensor_tensor(seg[:, n], segi[:, n, 0], segi[:, n, 1], ALU.max)

                link(nc.vector.tensor_tensor(fl[:, 1, :, 0:W - 1], code[:, :, 0:W - 1], code[:, :, 1:W], ALU.is_equal))
                mark_both()
                link(mark_segments(0))
                link(nc.vector.tensor_tensor(fl[:, 0], code, below, ALU.is_equal))
                for a, b in ((0, 1), (1, 0)):
                    link(nc.vector.tensor_tensor(fl[:, 1, :, 0:W - 1], code[:, :, a:W - 1 + a], below[:, :, b:W - 1 + b], ALU.is_equal))
                    mark_both()
                mark_segments(1).then_inc(sm_dve, 1)
                if nxt:
                    corners(q + 1, 0, 0, 0)
                v.wait_ge(sm_pe, 5 * q + 3)
                nc.vector.tensor_scalar(seg[:, 2], ps[0:H, 7, 0:SPR], 1.0, None, ALU.min).then_inc(sm_dve, 1)
                if nxt:
                    low_part(q + 1, 0, 0)
                v.wait_ge(sm_dve, 5 * q + 4)
                v.wait_ge(sm_pe, 5 * q + 4)
                link(nc.vector.tensor_reduce(seg[:, 3, 0:1], ps[0:H, 7, 0:SPR], AX.X, ALU.add))
                for n in range(1, SPR):
                    link(nc.vector.tensor_tensor(seg[:, 3, n:n + 1], seg[:, 3, n - 1:n], seg[:, 2, n - 1:n], ALU.add))
                for n in range(SPR):
                    ins = nc.vector.tensor_scalar(hot[:, n, :], const("iota", H), seg[:, 3, n:n + 1], seg[:, 2, n:n + 1],
                                                  ALU.is_equal, ALU.mult)
                ins.then_inc(sm_dve, 1)
                if nxt:
                    corners(q + 1, 1, 1, 0)
                v.wait_ge(sm_pe, 5 * q + 5)
                link(nc.vector.tensor_copy(lst_f[:, :], ps[0:1, 7, 0:NSEG]))
                link(nc.vector.tensor_copy(lst[:, :], lst_f[:, :]))
                link(nc.vector.tensor_reduce(cum[:, 1:2], ps[0:1, 4, 0:SPR], AX.X, ALU.add))
                link(nc.vector.tensor_scalar(cum[:, 1:2], cum[:, 1:2], (SLOTS - 1) / 2, 1.0 / SLOTS, ALU.add, ALU.mult))
                link(nc.vector.tensor_scalar(cum[:, 1:2], cum[:, 1:2], MAGIC, MAGIC, ALU.add, ALU.subtract))
                link(nc.vector.tensor_scalar(cum[:, 1:2], cum[:, 1:2], 1.0, None, ALU.max))
                link(nc.vector.tensor_copy(runs[:, 0:1], cum[:, 1:2]))
                link(nc.vector.tensor_copy(runs[:, 1:2], cum[:, 0:1]))
                nc.vector.tensor_tensor(cum[:, 0:1], cum[:, 0:1], cum[:, 1:2], ALU.add).then_inc(lst_ok, 1)
                v.wait_ge(lst_ok, q + 1)
                runs_here = v.value_load(runs[0:1, 0:1], min_val=1, max_val=NSEG // SLOTS)
                before = v.value_load(runs[0:1, 1:2], min_val=0, max_val=NSEG // SLOTS * PAIRS)
                if nxt:
                    low_part(q + 1, 1, 1)
                    residual(q + 1, 0, 0)
                v.wait_ge(enh_ok, BANDS * (q + 1))
                with v.Fori(0, runs_here) as i:
                    batch = before + i
                    LINKS = 27
                    k_own = [0]

                    def rlink(ins):
                        k_own[0] += 1
                        ins.then_inc(r_own, 1)
                        v.wait_ge(r_own, batch * LINKS + k_own[0])

                    starts = [v.value_load(lst[0:1, bass.ds(i * SLOTS + slot, 1)], min_val=0, max_val=PX - SEG) for slot in range(SLOTS)]
                    v.wait_ge(r_act, batch * 4 + 1)
                    v.wait_ge(lst_ok, q + 1)
                    px0, col0 = ps[:, 7, bass.ds(i * SLOTS, SLOTS)], ps[:, 5, bass.ds(i * SLOTS, SLOTS)]
                    nc.vector.tensor_scalar(inside[:, 0], px0, float(W), None, ALU.is_ge)
                    nc.vector.tensor_scalar(inside[:, 1], px0, float(PX - W), None, ALU.is_lt)
                    nc.vector.tensor_scalar(inside[:, 2], col0, 0.0, None, ALU.is_gt)
                    rlink(nc.vector.tensor_scalar(inside[:, 3], col0, float(W - SEG), None, ALU.is_lt))
                    for n, dy in enumerate((0, 2)):
                        edge = patch[:, :, dy, :]
                        ins = nc.vector.tensor_tensor(edge, edge, inside[:, n].unsqueeze(2).broadcast_to([P, SLOTS, SEG + 2]), ALU.mult)
                    rlink(ins)
                    for n, dx in ((2, 0), (3, SEG + 1)):
                        edge = patch[:, :, :, dx]
                        ins = nc.vector.tensor_tensor(edge, edge, inside[:, n].unsqueeze(2).broadcast_to([P, SLOTS, 3]), ALU.mult)
                    ins.then_inc(r_dve, 1)
                    v.wait_ge(r_dve, batch * 5 + 1)
                    center = patch[:, :, 1, 1:1 + SEG]
                    for dy in range(3):
                        ins = nc.vector.tensor_tensor(split_pixels(prod[:, 3 * dy:3 * dy + 3, :]), windows(dy),
                                                      center.unsqueeze(1).broadcast_to([P, 3, SLOTS, SEG]), ALU.mult)
                    ins.then_inc(r_dve, 1)
                    v.wait_ge(r_pe, batch * 2 + 1)
                    dots = ps[:, 6, 0:2 * GEN]
                    rlink(nc.vector.tensor_copy(rn[:, 5].rearrange("p j i -> p (j i)"), dots))
                    nc.vector.tensor_scalar(rn[:, 0].rearrange("p j i -> p (j i)"), ps[:, 6, 2 * GEN:4 * GEN], 1e-24, None,
                                            ALU.max).then_inc(r_dve, 1)
                    v.wait_ge(r_act, batch * 4 + 3)
                    rlink(nc.vector.tensor_scalar(rn[:, 2], rn[:, 2], LN_SHIFT ** 0.5, None, ALU.mult))
                    for _ in range(2):
                        rlink(nc.vector.tensor_tensor(rn[:, 3], rn[:, 2], rn[:, 2], ALU.mult))
                        rlink(nc.vector.tensor_tensor(rn[:, 3], rn[:, 3], rn[:, 0], ALU.mult))
                        rlink(nc.vector.tensor_scalar(rn[:, 3], rn[:, 3], -0.5, 1.5, ALU.mult, ALU.add))
                        rlink(nc.vector.tensor_tensor(rn[:, 2], rn[:, 2], rn[:, 3], ALU.mult))
                    rlink(nc.vector.tensor_tensor(rn[:, 4], rn[:, 5], rn[:, 2], ALU.mult))
                    nc.vector.tensor_tensor(sim[:].rearrange("p i j -> p j i"), rn[:, 4],
                                            rn[:, 2, GEN // 2, :].unsqueeze(1).broadcast_to([P, GEN, 2]), ALU.mult).then_inc(r_dve, 1)
                    v.wait_ge(r_dve, batch * 5 + 4)
                    s_i = sim[:].unsqueeze(2).broadcast_to([P, 2, GEN, GEN])
                    s_j = sim[:].unsqueeze(3).broadcast_to([P, 2, GEN, GEN])
                    rlink(nc.vector.tensor_tensor(cmp[:, 0], s_i, s_j, ALU.is_gt))
                    rlink(nc.vector.tensor_tensor(cmp[:, 1], s_i, s_j, ALU.is_equal))
                    low = const("lower")
                    for im in range(2):
                        rlink(nc.vector.tensor_tensor(cmp[:, 1, im].rearrange("p a b -> p (a b)"),
                                                      cmp[:, 1, im].rearrange("p a b -> p (a b)"), low, ALU.mult))
                    rlink(nc.vector.tensor_tensor(cmp[:, 0], cmp[:, 0], cmp[:, 1], ALU.add))
                    rlink(nc.vector.tensor_reduce(sel[:, 1], cmp[:, 0], AX.X, ALU.add))
                    v.wait_ge(counts_in, 16 * SLOTS * (batch + 1))
                    rlink(nc.vector.tensor_tensor(sel[:, 2], sel[:, 1],
                                                  counts_b[:, :].unsqueeze(2).broadcast_to([P, 2, GEN]), ALU.is_lt))
                    v.wait_ge(r_act, batch * 4 + 4)
                    rlink(nc.vector.tensor_tensor(sel[:, 3], sel[:, 2], sel[:, 0], ALU.mult))
                    rlink(nc.vector.tensor_reduce(dent[:, 0], sel[:, 3], AX.X, ALU.add))
                    rlink(nc.vector.tensor_scalar(dent[:, 1], dent[:, 0], 1e-8, None, ALU.add))
                    rlink(nc.vector.reciprocal(dent[:, 0], dent[:, 1]))
                    rlink(nc.vector.tensor_tensor(sel[:, 4], sel[:, 3], dent[:, 0].unsqueeze(2).broadcast_to([P, 2, GEN]), ALU.mult))
                    nc.vector.tensor_copy(wrep[:].rearrange("p j i c -> p i j c"),
                                          sel[:, 4].unsqueeze(3).broadcast_to([P, 2, GEN, C])).then_inc(r_dve, 1)
                    v.wait_ge(r_pe, batch * 2 + 2)
                    for dy in range(3):
                        ins = nc.vector.tensor_tensor(split_pixels(prod[:, 3 * dy:3 * dy + 3, :]),
                                                      split_pixels(ps[:, dy, 0:3 * P].rearrange("p (j w) -> p j w", w=P)), windows(dy), ALU.mult)
                        if dy == 2:
                            rlink(ins)
                    rlink(nc.vector.tensor_reduce(agg[:, 0], prod[:].rearrange("p j w -> p w j"), AX.X, ALU.add))
                    assert k_own[0] == LINKS, k_own
                    v.wait_ge(lst_ok, q + 1)
                    nc.vector.tensor_scalar(agg[:, 1].rearrange("p (s w) -> p s w", s=SLOTS), center, sv[:, 14:15], beta,
                                            ALU.mult, ALU.add).then_inc(own_term_ok, 1)
                    for slot in range(SLOTS):
                        if slot == 0:
                            v.wait_ge(own_term_ok, batch + 1)
                        else:
                            v.wait_ge(r_placed, batch * (SLOTS - 1) + slot)
                        part = slice(slot * SEG, (slot + 1) * SEG)
                        ins = nc.vector.tensor_tensor(enh[:, bass.ds(starts[slot], SEG)], agg[:, 0, part], agg[:, 1, part], ALU.add)
                        ins.then_inc(r_placed if slot < SLOTS - 1 else r_done, 1)

        @block.tensor
        def _(pe):
            def group_mean(n, t, bank):
                pe.wait_ge(grp_in, n + 1)
                nc.tensor.matmul(ps[:, bank, 0:2], const("group"), t[:, 18:20], start=True, stop=True).then_inc(grp_out, 1)

            pe.wait_ge(c_in, 16)
            ident = const("ident")
            pe.wait_ge(ready, 1)

            def late_setup():
                pe.wait_ge(ready, 2)
                for t in range(TAPS):
                    ins = nc.tensor.transpose(ps[:, t // 8, (t % 8) * C:(t % 8 + 1) * C], conv_dup[:, t * P:(t + 1) * P],
                                              const("ident", C)[:, 0:C])
                ins.then_inc(setup_pe, 1)
                pe.wait_ge(w_in, 16 * 17)
                nc.tensor.transpose(ps[:, 3, 0:P], w1_raw[:, :, :].rearrange("p a c -> p (a c)"), ident).then_inc(setup_pe, 1)
                nc.tensor.transpose(ps[:, 2, 0:C], w2_raw[:, :], const("ident", C)[:, 0:C]).then_inc(setup_pe, 1)
                pe.wait_ge(ready, 3)

            def hidden(b, k, bank):
                for im in range(2):
                    ins = nc.tensor.matmul(ps[:, bank + im, 0:CPX], w1_lhs[:, im, :],
                                           enh[:, bass.ds((b * 2 + k) * CPX, CPX)], start=True, stop=True)
                ins.then_inc(h_ps, 1)

            def second(p, b, k):
                chunk = CHUNKS * p + b * 2 + k
                pe.wait_ge(h_sb, AHEAD + chunk + 1)
                pe.wait_ge(y_ok, AHEAD + chunk - 1)
                for im in range(2):
                    ins = nc.tensor.matmul(ps[im * C:(im + 1) * C, 6 + k, 0:CPX], w2_lhs[:, :], hid[:, k, im, :],
                                           start=True, stop=True)
                ins.then_inc(f_ps, 1)

            def turn_back(p, b, u):
                pe.wait_ge(wtok_ok, AHEAD + BANDS * p + b + 1)
                pe.wait_ge(w_sb, AHEAD + BANDS * p + b)
                for im in range(2):
                    for t in range(TILES):
                        n = im * TILES + t
                        ins = nc.tensor.transpose(flat[:, n * C:(n + 1) * C].bitcast(F16),
                                                  wsplit[:, u, t, im].rearrange("p a c -> p (a c)"), ident_h[:, :])
                ins.then_inc(w_ps, 1)

            def convolve(p, b, k, u):
                if isinstance(b, int) and b == BANDS - 1:
                    pe.wait_ge(w_end, p + 1)
                else:
                    pe.wait_ge(w_sb, AHEAD + BANDS * p + b + 1 + k)
                pe.wait_ge(x1_ok, AHEAD + CHUNKS * p + b * 2 + k - 1)
                for a in range(2):
                    for t in range(TAPS):
                        for im in range(2):
                            ins = nc.tensor.matmul(ps[im * C:(im + 1) * C, 2 + k, 0:CPX], conv_lhs[:, a, t, :],
                                                   wring[:, u, im, k * ROWS + t // 3:(k + 1) * ROWS + t // 3, t % 3:t % 3 + W],
                                                   start=(a + t == 0), stop=(a == 1 and t == TAPS - 1))
                ins.then_inc(conv_ps, 1)

            for q in ROUNDS:
                cur, last, nxt = 0 <= q < PAIRS, q >= 1, q + 1 < PAIRS

                def step(f, u, n):
                    if last:
                        hidden(f, 0, 4)
                    if cur and there(f + 1):
                        convolve(q, f + 1, 0, 1 - u)
                    if last:
                        second(q - 1, f, 0)
                        hidden(f, 1, 4)
                    if cur and there(f + 2):
                        turn_back(q, f + 2, u)
                    if last:
                        second(q - 1, f, 1)
                    if cur and there(f + 1):
                        convolve(q, f + 1, 1, 1 - u)

                def last_step(f, u, n):
                    hidden(f, 1, 0)
                    second(q - 1, f, 0)
                    if there(f + 1):
                        hidden(f + 1, 0, 4)
                    second(q - 1, f, 1)

                if q == PAIRS:
                    hidden(0, 0, 4)
                    sweep(pe, last_step)
                elif q >= 0:
                    sweep(pe, step)
                if q == PAIRS:
                    continue
                if cur:
                    group_mean(2 * q + 1, sv, 7)
                if nxt:
                    group_mean(2 * q + 2, sa, 0)
                if cur:
                    pe.wait_ge(norm_b, q + 1)
                    pe.wait_ge(y_ok, AHEAD + CHUNKS * q)
                with pe.Fori(0, BANDS // 2) as i:
                    for u in range(2):
                        band = BANDS * q + i * 2 + u
                        band_a = BANDS * (q + 1) + i * 2 + u
                        if nxt:
                            pe.wait_ge(g_ok, band_a + 1)
                            for k in range(2):
                                pe.wait_ge(z_sb, AHEAD + 2 * band_a + k - 1)
                                nc.tensor.matmul(ps[:, 4 + k, 0:CPX], off_lhs[:, :], g_band[:, u, k * CPX:(k + 1) * CPX],
                                                 start=True, stop=True).then_inc(z_ps, 1)
                            pe.wait_ge(tok_ok, AHEAD + band_a - 1)
                            for t in range(TILES):
                                ins = nc.tensor.transpose(ps[:, 6 * u + t // 4, (t % 4) * P:(t % 4 + 1) * P],
                                                          g_band[:, u, t * P:(t + 1) * P], ident)
                            ins.then_inc(t_ps, 1)
                        if cur:
                            pe.wait_ge(feat_ok, AHEAD + band + 1)
                            pe.wait_ge(d_ok, AHEAD + band + 1)
                            for k in range(2):
                                part = slice(k * CPX, (k + 1) * CPX)
                                pe.wait_ge(m_sb, AHEAD + 2 * band + k - 1)
                                nc.tensor.matmul(ps[0:32, 2 + k, 0:CPX], blk_r[:, :], d_band[:, u, part], start=True, stop=True)
                                for n in range(2):
                                    nc.tensor.matmul(ps[32:64, 2 + k, 0:CPX], hash_lhs[:, n, :], s_band[:, u, part],
                                                     start=(n == 0), stop=(n == 1))
                                nc.tensor.matmul(ps[64:96, 2 + k, 0:CPX], blk_bf[:, :], q_band[:, u, part], start=True, stop=True)\
                                    .then_inc(m_ps, 1)
                if not cur:
                    late_setup()
                if nxt:
                    pe.wait_ge(tok_ok, AHEAD + BANDS * (q + 2))
                    pe.wait_ge(z_shift[0], 16 * 3 * (q + 2))
                    for n in range(NT):
                        if n == SHIFT_ROWS * W // P:
                            pe.wait_ge(z_shift[1], 16 * 3 * (q + 2))
                        for dy in range(3):
                            at = n * P + dy * W
                            ins = nc.tensor.matmul(ps[:, 6, 4 * n:4 * n + 4], zmoved[:, at:at + P], selz_h[:, 4 * dy:4 * dy + 4],
                                                   start=(dy == 0), stop=(dy == 2))
                    ins.then_inc(off_ps, 1)
                if not cur:
                    turn_back(q + 1, 0, 0)
                    turn_back(q + 1, 1, 1)
                    for k in range(2):
                        convolve(q + 1, 0, k, 0)
                    continue
                pe.wait_ge(sm_dve, 5 * q + 1)
                nc.tensor.transpose(ps[0:4, 7, 0:H], mm[:, 0:4], const("ident", H)[:, 0:H]).then_inc(sm_pe, 1)
                pe.wait_ge(sm_dve, 5 * q + 2)
                nc.tensor.matmul(ps[0:H, 7, 0:4], ones4[:, :], diag[:, 0:4], start=True, stop=True).then_inc(sm_pe, 1)
                pe.wait_ge(sm_dve, 5 * q + 3)
                nc.tensor.matmul(ps[0:H, 7, 0:SPR], const("ident", H)[:, 0:H], seg[:, 0], start=True, stop=False)
                nc.tensor.matmul(ps[0:H, 7, 0:SPR], const("pair", H), seg[:, 1], start=False, stop=True).then_inc(sm_pe, 1)
                pe.wait_ge(sm_dve, 5 * q + 4)
                nc.tensor.matmul(ps[0:H, 7, 0:SPR], const("tri", H), seg[:, 2], start=True, stop=True).then_inc(sm_pe, 1)
                if nxt:
                    turn_back(q + 1, 0, 0)
                pe.wait_ge(sm_dve, 5 * q + 5)
                for part, bank in ((0, 7), (1, 5)):
                    for n in range(SPR):
                        nc.tensor.matmul(ps[:, bank, 0:NSEG], place[:, part, n:n + 1].broadcast_to([H, P]), hot[:, n, :],
                                         start=(n == 0), stop=(n == SPR - 1))
                nc.tensor.matmul(ps[0:1, 4, 0:SPR], const("one", H), seg[:, 2], start=True, stop=True).then_inc(sm_pe, 1)
                if nxt:
                    turn_back(q + 1, 1, 1)
                    for k in range(2):
                        convolve(q + 1, 0, k, 0)
                pe.wait_ge(lst_ok, q + 1)
                runs_here = pe.value_load(runs[0:1, 0:1], min_val=1, max_val=NSEG // SLOTS)
                before = pe.value_load(runs[0:1, 1:2], min_val=0, max_val=NSEG // SLOTS * PAIRS)
                with pe.Fori(0, runs_here) as i:
                    batch = before + i
                    pe.wait_ge(r_act, batch * 4 + 2)
                    pe.wait_ge(r_dve, batch * 5 + 2)
                    pe.wait_ge(lst_ok, q + 1)
                    for j in range(GEN):
                        nc.tensor.matmul(ps[:, 6, 2 * j:2 * j + 2], prod[:, j, :], const("blk")[:, 0:2], start=True, stop=True)
                    for j in range(GEN):
                        ins = nc.tensor.matmul(ps[:, 6, 2 * GEN + 2 * j:2 * GEN + 2 * j + 2], gsq[:, j, :],
                                               const("blk")[:, 0:2], start=True, stop=True)
                    ins.then_inc(r_pe, 1)
                    pe.wait_ge(r_dve, batch * 5 + 5)
                    pe.wait_ge(lst_ok, q + 1)
                    for j in range(GEN):
                        ins = nc.tensor.matmul(ps[:, j // 3, (j % 3) * P:(j % 3 + 1) * P], wrep[:, j].rearrange("p i c -> p (i c)"),
                                               ident, start=True, stop=True)
                    ins.then_inc(r_pe, 1)
                    pe.wait_ge(r_done, AHEAD + batch + 1)


_INS = ["x", "L0_conv_w_off", "L0_conv_b_off", "L0_conv_w_conv", "L0_conv_b_conv", "L1_conv_gamma", "L1_conv_beta",
        "L1_conv_w1", "L1_conv_b1", "L1_conv_w2", "L1_conv_b2"]


def kernel(**inputs):
    import concourse.bacc as bacc
    from concourse.bass_utils import run_bass_kernel_spmd as run

    nc = bacc.Bacc("TRN2", target_bir_lowering=False, num_devices=1)
    arrays, args = {}, []
    for name in _INS:
        a = np.ascontiguousarray(inputs[name])
        if name == "x":
            a = a.reshape(PAIRS, P, PX)
        arrays[name] = a
        args.append(nc.dram_tensor(name, a.shape, F32, kind="ExternalInput").ap())
    arrays["consts"] = constants()
    args.append(nc.dram_tensor("consts", (P, N_CONST), F32, kind="ExternalInput").ap())
    args.append([nc.dram_tensor(f"table{q}", (2 * IMG_ENTRIES, ENTRY), F32).ap() for q in range(PAIRS)])
    args.append(nc.dram_tensor("sums", (3, 2, PX), F32).ap())
    args.append(nc.dram_tensor("kmap_d", (PX, 2), F32).ap())
    out = nc.dram_tensor("y", (PAIRS, P, PX), F32, kind="ExternalOutput").ap()
    program(nc, *args, out)
    r = run(nc, [arrays], core_ids=[0])
    return r.results[0]["y"].reshape(N_IMG, C, H, W)
```
